# Optimizing a Trainium2 kernel written in Bass

```python
import numpy as np
import jax
import jax.numpy as jnp

def _softmax(x, axis=-1):
    return jax.nn.softmax(x, axis=axis)

def _gelu(x):
    return jax.nn.gelu(x, approximate=True)

def _silu(x):
    return jax.nn.silu(x)

def _sigmoid(x):
    return jax.nn.sigmoid(x)

def _layernorm(x, axis=-1, eps=1e-05):
    m = jnp.mean(x, axis=axis, keepdims=True)
    v = jnp.var(x, axis=axis, keepdims=True)
    return (x - m) / jnp.sqrt(v + eps)

def _scatter_add(tgt, idx, src, axis=0):
    return tgt.at[idx].add(src)

def _segment_sum(src, seg, n):
    return jax.ops.segment_sum(src, seg, n)
kernel_name = 'mk_sandwich_d1_jaxref_r8_a5e3a6'

def setup_inputs(seed: int=0):
    np.random.seed(seed)
    _w = jnp.asarray

    def _L0_attn_setup():
        import jax, jax.numpy as jnp
        import numpy as np
        ROPE_THETA = 10000.0

        def rope(t, rot_dim):
            S = t.shape[-2]
            half = rot_dim // 2
            inv_freq = 1.0 / ROPE_THETA ** (jnp.arange(0, rot_dim, 2, dtype=jnp.float32) / rot_dim)
            freqs = jnp.arange(S, dtype=jnp.float32)[:, None] * inv_freq[None, :]
            freqs = jnp.repeat(freqs, 2, axis=-1)
            cos, sin = (jnp.cos(freqs), jnp.sin(freqs))
            t_rot, t_pass = (t[..., :rot_dim], t[..., rot_dim:])
            x = t_rot.reshape(*t_rot.shape[:-1], half, 2)
            rh = jnp.stack([-x[..., 1], x[..., 0]], axis=-1).reshape(t_rot.shape)
            t_rot = t_rot * cos + rh * sin
            return jnp.concatenate([t_rot, t_pass], axis=-1)

        def feature_map(x):
            norm = jnp.sqrt(jnp.sum(x * x, axis=-1, keepdims=True))
            return x / jnp.maximum(norm, 1e-12)
        key = jax.random.key(seed)
        kx, kwi, kwo = jax.random.split(key, 3)
        B, S, D = (8, 512, 256)
        scale = 0.02
        return {'X': jax.random.normal(kx, (B, S, D), dtype=jnp.float32), 'W_in': jax.random.normal(kwi, (3 * D, D), dtype=jnp.float32) * scale, 'b_in': jnp.zeros((3 * D,), dtype=jnp.float32), 'W_out': jax.random.normal(kwo, (D, D), dtype=jnp.float32) * scale, 'b_out': jnp.zeros((D,), dtype=jnp.float32)}
    _L0_attn_in = _L0_attn_setup()

    def _L0_ffn_setup():
        import jax, jax.numpy as jnp
        import numpy as np
        B, S, H = (1, 128, 256)
        NH, NKV, D = (32, 8, 64)
        GROUPS = NH // NKV
        E, F, TOPK = (8, 1024, 2)
        EPS = 1e-05

        def rmsnorm(x, w):
            return x * jax.lax.rsqrt(jnp.mean(x * x, axis=-1, keepdims=True) + EPS) * w

        def attention(h, wq, wk, wv, wo):
            b, s, _ = h.shape
            q = (h @ wq).reshape(b, s, NH, D).transpose(0, 2, 1, 3)
            k = (h @ wk).reshape(b, s, NKV, D).transpose(0, 2, 1, 3)
            v = (h @ wv).reshape(b, s, NKV, D).transpose(0, 2, 1, 3)
            k = jnp.repeat(k, GROUPS, axis=1)
            v = jnp.repeat(v, GROUPS, axis=1)
            scores = jnp.einsum('bhqd,bhkd->bhqk', q, k) / jnp.sqrt(jnp.float32(D))
            causal = jnp.tril(jnp.ones((s, s), bool))
            scores = jnp.where(causal, scores, jnp.finfo(scores.dtype).min)
            attn = jax.nn.softmax(scores, axis=-1)
            out = jnp.einsum('bhqk,bhkd->bhqd', attn, v)
            out = out.transpose(0, 2, 1, 3).reshape(b, s, NH * D)
            return out @ wo

        def moe(h, gate_w, w1, w2, w3):
            b, s, hd = h.shape
            t = h.reshape(-1, hd)
            T = t.shape[0]
            probs = jax.nn.softmax(t @ gate_w, axis=-1)
            topw, topi = jax.lax.top_k(probs, TOPK)
            topw = topw / jnp.sum(topw, axis=-1, keepdims=True)
            combine = jnp.zeros((T, E), t.dtype).at[jnp.arange(T)[:, None], topi].add(topw)
            up = jnp.einsum('th,ehf->etf', t, w1)
            gated = jax.nn.relu(up) * jnp.einsum('th,ehf->etf', t, w3)
            down = jnp.einsum('etf,efh->eth', gated, w2)
            out = jnp.einsum('eth,te->th', down, combine)
            return out.reshape(b, s, hd)
        key = jax.random.key(seed)
        ks = jax.random.split(key, 12)
        sc = 0.02
        return {'x': jax.random.normal(ks[0], (B, S, H), dtype=jnp.float32), 'ln1_w': jnp.ones((H,), jnp.float32), 'wq': jax.random.normal(ks[1], (H, NH * D), jnp.float32) * sc, 'wk': jax.random.normal(ks[2], (H, NKV * D), jnp.float32) * sc, 'wv': jax.random.normal(ks[3], (H, NKV * D), jnp.float32) * sc, 'wo': jax.random.normal(ks[4], (NH * D, H), jnp.float32) * sc, 'ln2_w': jnp.ones((H,), jnp.float32), 'gate_w': jax.random.normal(ks[5], (H, E), jnp.float32) * sc, 'w1': jax.random.normal(ks[6], (E, H, F), jnp.float32) * sc, 'w2': jax.random.normal(ks[7], (E, F, H), jnp.float32) * sc, 'w3': jax.random.normal(ks[8], (E, H, F), jnp.float32) * sc}
    _L0_ffn_in = _L0_ffn_setup()
    _d = {'L0_attn_X': _L0_attn_in['X'], 'L0_attn_W_in': _L0_attn_in['W_in'], 'L0_attn_b_in': _L0_attn_in['b_in'], 'L0_attn_W_out': _L0_attn_in['W_out'], 'L0_attn_b_out': _L0_attn_in['b_out'], 'L0_ffn_ln1_w': _L0_ffn_in['ln1_w'], 'L0_ffn_wq': _L0_ffn_in['wq'], 'L0_ffn_wk': _L0_ffn_in['wk'], 'L0_ffn_wv': _L0_ffn_in['wv'], 'L0_ffn_wo': _L0_ffn_in['wo'], 'L0_ffn_ln2_w': _L0_ffn_in['ln2_w'], 'L0_ffn_gate_w': _L0_ffn_in['gate_w'], 'L0_ffn_w1': _L0_ffn_in['w1'], 'L0_ffn_w2': _L0_ffn_in['w2'], 'L0_ffn_w3': _L0_ffn_in['w3']}
    _x0 = _d['L0_attn_X']
    _d['L0_attn_X'] = jax.random.normal(jax.random.fold_in(jax.random.key(seed), 1), (4, 512, 256), dtype=_x0.dtype)
    del _x0
    return _d

def reference(L0_attn_X, L0_attn_W_in, L0_attn_b_in, L0_attn_W_out, L0_attn_b_out, L0_ffn_ln1_w, L0_ffn_wq, L0_ffn_wk, L0_ffn_wv, L0_ffn_wo, L0_ffn_ln2_w, L0_ffn_gate_w, L0_ffn_w1, L0_ffn_w2, L0_ffn_w3):

    def _L0_attn_ref(X, W_in, b_in, W_out, b_out):
        import jax, jax.numpy as jnp
        import numpy as np
        ROPE_THETA = 10000.0

        def rope(t, rot_dim):
            S = t.shape[-2]
            half = rot_dim // 2
            inv_freq = 1.0 / ROPE_THETA ** (jnp.arange(0, rot_dim, 2, dtype=jnp.float32) / rot_dim)
            freqs = jnp.arange(S, dtype=jnp.float32)[:, None] * inv_freq[None, :]
            freqs = jnp.repeat(freqs, 2, axis=-1)
            cos, sin = (jnp.cos(freqs), jnp.sin(freqs))
            t_rot, t_pass = (t[..., :rot_dim], t[..., rot_dim:])
            x = t_rot.reshape(*t_rot.shape[:-1], half, 2)
            rh = jnp.stack([-x[..., 1], x[..., 0]], axis=-1).reshape(t_rot.shape)
            t_rot = t_rot * cos + rh * sin
            return jnp.concatenate([t_rot, t_pass], axis=-1)

        def feature_map(x):
            norm = jnp.sqrt(jnp.sum(x * x, axis=-1, keepdims=True))
            return x / jnp.maximum(norm, 1e-12)
        D = X.shape[-1]
        QKV = jnp.einsum('bsd,ed->bse', X, W_in) + b_in
        Q, K, V = jnp.split(QKV, 3, axis=-1)
        rot_dim = D // 2
        Q = rope(Q, rot_dim)
        K = rope(K, rot_dim)
        A = jnp.sum(feature_map(K) * V, axis=-2)
        Y = A[:, None, :] * Q
        Y = jnp.einsum('bsd,ed->bse', Y, W_out) + b_out
        return Y + X

    def _L0_ffn_ref(x, ln1_w, wq, wk, wv, wo, ln2_w, gate_w, w1, w2, w3):
        import jax, jax.numpy as jnp
        import numpy as np
        B, S, H = (1, 128, 256)
        NH, NKV, D = (32, 8, 64)
        GROUPS = NH // NKV
        E, F, TOPK = (8, 1024, 2)
        EPS = 1e-05

        def rmsnorm(x, w):
            return x * jax.lax.rsqrt(jnp.mean(x * x, axis=-1, keepdims=True) + EPS) * w

        def attention(h, wq, wk, wv, wo):
            b, s, _ = h.shape
            q = (h @ wq).reshape(b, s, NH, D).transpose(0, 2, 1, 3)
            k = (h @ wk).reshape(b, s, NKV, D).transpose(0, 2, 1, 3)
            v = (h @ wv).reshape(b, s, NKV, D).transpose(0, 2, 1, 3)
            k = jnp.repeat(k, GROUPS, axis=1)
            v = jnp.repeat(v, GROUPS, axis=1)
            scores = jnp.einsum('bhqd,bhkd->bhqk', q, k) / jnp.sqrt(jnp.float32(D))
            causal = jnp.tril(jnp.ones((s, s), bool))
            scores = jnp.where(causal, scores, jnp.finfo(scores.dtype).min)
            attn = jax.nn.softmax(scores, axis=-1)
            out = jnp.einsum('bhqk,bhkd->bhqd', attn, v)
            out = out.transpose(0, 2, 1, 3).reshape(b, s, NH * D)
            return out @ wo

        def moe(h, gate_w, w1, w2, w3):
            b, s, hd = h.shape
            t = h.reshape(-1, hd)
            T = t.shape[0]
            probs = jax.nn.softmax(t @ gate_w, axis=-1)
            topw, topi = jax.lax.top_k(probs, TOPK)
            topw = topw / jnp.sum(topw, axis=-1, keepdims=True)
            combine = jnp.zeros((T, E), t.dtype).at[jnp.arange(T)[:, None], topi].add(topw)
            up = jnp.einsum('th,ehf->etf', t, w1)
            gated = jax.nn.relu(up) * jnp.einsum('th,ehf->etf', t, w3)
            down = jnp.einsum('etf,efh->eth', gated, w2)
            out = jnp.einsum('eth,te->th', down, combine)
            return out.reshape(b, s, hd)
        h = x + attention(rmsnorm(x, ln1_w), wq, wk, wv, wo)
        return h + moe(rmsnorm(h, ln2_w), gate_w, w1, w2, w3)
    x = L0_attn_X
    x = x + _layernorm(_L0_attn_ref(_layernorm(x, axis=-1), L0_attn_W_in, L0_attn_b_in, L0_attn_W_out, L0_attn_b_out), axis=-1)
    x = x + _layernorm(_L0_ffn_ref(_layernorm(x, axis=-1), L0_ffn_ln1_w, L0_ffn_wq, L0_ffn_wk, L0_ffn_wv, L0_ffn_wo, L0_ffn_ln2_w, L0_ffn_gate_w, L0_ffn_w1, L0_ffn_w2, L0_ffn_w3), axis=-1)
    return x

_drawn_inputs = setup_inputs


def setup_inputs(seed=0):
    import zlib

    import numpy as np

    out = dict(_drawn_inputs(seed))
    spreads = {'L0_attn_b_in': (0.0, 0.1),
     'L0_attn_b_out': (0.0, 0.1),
     'L0_ffn_ln1_w': (1.0, 0.6),
     'L0_ffn_ln2_w': (1.0, 0.6)}
    factors = {'L0_ffn_wq': 8.0,
     'L0_ffn_wk': 8.0,
     'L0_ffn_wv': 4.397,
     'L0_ffn_wo': 4.402,
     'L0_ffn_gate_w': 5.222,
     'L0_ffn_w1': 5.574,
     'L0_ffn_w2': 4.618,
     'L0_ffn_w3': 4.617}
    for name, (base, spread) in spreads.items():
        noise = np.random.default_rng([zlib.crc32(name.encode()), seed]).standard_normal(out[name].shape)
        drawn = base * np.exp(spread * noise) if base else spread * noise
        out[name] = jnp.asarray(drawn.astype(out[name].dtype))
    for name, factor in factors.items():
        out[name] = (out[name] * factor).astype(out[name].dtype)
    return out
```

```python
from contextlib import ExitStack

import numpy as np

import concourse.bass as bass
from concourse import mybir

ALU = mybir.AluOpType
ACT = mybir.ActivationFunctionType
AX = mybir.AxisListType
F32 = mybir.dt.float32
I32 = mybir.dt.int32
U32 = mybir.dt.uint32

P = 128
B, S, D = 4, 512, 256
T = B * S
TT = T // P
TS = S // P
DC = D // P
ROT = D // 2
NH, NKV, HD = 32, 8, 64
GR = NH // NKV
QG = GR * HD
E, F, TOPK = 8, 1024, 2
FC = F // P
EPS = 1e-5
BLK = 256
BH = BLK // P
NBLK = (TOPK * T + E * (BLK - 1)) // BLK
SLOTS = NBLK * BLK
NEG = -1e30
NORMS = 3


def layer_one(nc, dram, keep):
    with ExitStack() as ctx:
        def sb(name, shape, dt=F32):
            return ctx.enter_context(nc.sbuf_tensor(name, shape, dt))

        def sem(name):
            return ctx.enter_context(nc.semaphore(name))

        winT = sb("winT", [P, DC, 3 * D])
        wswT = sb("wswT", [P, DC, ROT])
        woutT = sb("woutT", [P, DC, D])
        kvbias = sb("kvbias", [P, 2 * D])
        outbias = sb("outbias", [P, D])
        qbias = sb("qbias", [P, 3])
        ln1 = sb("ln1", [P, DC])
        cos_tok = sb("cos_tok", [P, TS, ROT])
        sin_tok = sb("sin_tok", [P, TS, ROT])
        cos_ch = sb("cos_ch", [ROT, S])
        sin_ch = sb("sin_ch", [ROT, S])
        ident = keep["ident"]
        x = sb("x", [P, TS, D])
        zc = sb("zc", [P, TS, D])
        stats = sb("stats", [P, TS, 6])
        mean = sb("mean", [P, TS])
        apart = sb("apart", [P, TS])
        spread = sb("spread", [P, TS])
        rstd = sb("rstd", [P, TS])
        xn = sb("xn", [P, TS, D])
        xnb = sb("xnb", [P, TS, D])
        xnT = sb("xnT", [P, DC, S])
        kv = sb("kv", [P, TS, 2 * D])
        kswap = sb("kswap", [P, TS, ROT])
        square = sb("square", [P, TS, D])
        ksum = sb("ksum", [P, TS])
        rnorm = sb("rnorm", [P, TS])
        kvprod = sb("kvprod", [P, TS, D])
        q0 = sb("q0", [P, S])
        qsw = sb("qsw", [P, S])
        qT = sb("qT", [P, DC, S])
        state = sb("state", [P, DC])
        wstate = sb("wstate", [P, DC, D])
        y = sb("y", [P, TS, D])
        root = sb("root", [P, TS])
        knorm = sb("knorm", [P, TS])
        zroot = sb("zroot", [P, TS])
        zscale = sb("zscale", [P, TS])
        zsum = sb("zsum", [P, TS])
        zn = sb("zn", [P, TS, D])
        zeros = sb("zeros", [P, 8 * D])
        ps = ctx.enter_context(nc.psum_tensor("ps1", [P, 8, 512], F32))

        x_loaded = sem("x_loaded")
        x_taken = sem("x_taken")
        kept = sem("kept")
        weights_loaded = sem("weights_loaded")
        zeroed = sem("zeroed")
        eps_set = sem("eps_set")
        slots_zero = sem("slots_zero")
        dve_step = sem("dve_step")
        gp_step = sem("gp_step")
        xn_ready = sem("xn_ready")
        xnT_in_psum = sem("xnT_in_psum")
        xnT_ready = sem("xnT_ready")
        kv_in_psum = sem("kv_in_psum")
        kv_taken = sem("kv_taken")
        q_in_psum = sem("q_in_psum")
        q_biased = sem("q_biased")
        qT_ready = sem("qT_ready")
        k_rotated = sem("k_rotated")
        var_ready = sem("var_ready")
        root_ready = sem("root_ready")
        act_step = sem("act_step")
        ksum_ready = sem("ksum_ready")
        kvprod_ready = sem("kvprod_ready")
        rnorm_ready = sem("rnorm_ready")
        state_in_psum = sem("state_in_psum")
        wstate_ready = sem("wstate_ready")
        y_in_psum = sem("y_in_psum")
        xnb_ready = sem("xnb_ready")
        z_ready = sem("z_ready")
        zsum_ready = sem("zsum_ready")
        zn_ready = sem("zn_ready")
        znT_in_psum = sem("znT_in_psum")
        hT_done = sem("hT_done")

        block = ctx.enter_context(nc.Block())

        @block.sync
        def _(sp):
            xd = dram["x"].rearrange("b (t p) d -> b p t d", p=P)
            sp.dma_start(x[:], xd[0]).then_inc(x_loaded, 16)
            loads = [
                (winT[:], dram["winT"].rearrange("(c p) n -> p c n", p=P)),
                (wswT[:], dram["wswT"].rearrange("(c p) n -> p c n", p=P)),
                (woutT[:], dram["woutT"].rearrange("(c p) n -> p c n", p=P)),
                (kvbias[:], dram["b_in"][:, D:3 * D].to_broadcast([P, 2 * D])),
                (outbias[:], dram["b_out"].to_broadcast([P, D])),
                (qbias[:], dram["qbias"]),
                (ln1[:], dram["ln1"]),
                (cos_tok[:], dram["cos_tok"].rearrange("(t p) n -> p t n", p=P)),
                (sin_tok[:], dram["sin_tok"].rearrange("(t p) n -> p t n", p=P)),
                (cos_ch[:], dram["cos_ch"]),
                (sin_ch[:], dram["sin_ch"]),
                (ident[:], dram["ident"]),
            ]
            for dst, src in loads:
                sp.dma_start(dst, src).then_inc(weights_loaded, 16)
            sp.wait_ge(zeroed, 1)
            fill = dram["slot_rows"].rearrange("(n p) d -> p n d", p=P)
            rows = SLOTS // P
            fills = 0
            for n in range(0, rows, 8):
                k = min(8, rows - n)
                sp.dma_start(fill[:, n:n + k, :], zeros[:, 0:k * D].rearrange("p (n d) -> p n d", d=D)).then_inc(slots_zero, 16)
                fills += 1
            with sp.Fori(1, B) as b:
                sp.wait_ge(x_taken, b)
                sp.dma_start(x[:], xd[bass.ds(b, 1)].rearrange("o p t d -> (o p) t d")).then_inc(x_loaded, 16)
            sp.wait_ge(slots_zero, 16 * fills)
        n_loads = 12

        @block.tensor
        def _(pe):
            pe.wait_ge(weights_loaded, 16 * n_loads)
            with pe.Fori(0, B) as b:
                pe.wait_ge(xn_ready, b + 1)
                for c in range(DC):
                    for t in range(TS):
                        last = pe.transpose(ps[:, c, t * P:(t + 1) * P], xn[:, t, c * P:(c + 1) * P], ident[:])
                last.then_inc(xnT_in_psum, 1)
                pe.wait_ge(xnT_ready, b + 1)
                for t in range(TS):
                    if t >= 2:
                        pe.wait_ge(kv_taken, b * TS + t - 1)
                    for c in range(DC):
                        last = pe.matmul(ps[:, 2 + t % 2, :], xnT[:, c, t * P:(t + 1) * P], winT[:, c, D:3 * D],
                                         start=(c == 0), stop=(c == DC - 1))
                    last.then_inc(kv_in_psum, 1)
                for m in range(DC + 1):
                    for c in range(DC):
                        w = winT[:, c, m * P:(m + 1) * P] if m < DC else wswT[:, c, :]
                        last = pe.matmul(ps[:, 4 + m, :], w, xnT[:, c, :], start=(c == 0), stop=(c == DC - 1))
                last.then_inc(q_in_psum, 1)
                pe.wait_ge(kvprod_ready, b + 1)
                pe.wait_ge(rnorm_ready, b + 1)
                for m in range(DC):
                    for t in range(TS):
                        last = pe.matmul(ps[:, 7, m:m + 1], kvprod[:, t, m * P:(m + 1) * P], rnorm[:, t:t + 1],
                                         start=(t == 0), stop=(t == TS - 1))
                last.then_inc(state_in_psum, 1)
                pe.wait_ge(wstate_ready, b + 1)
                pe.wait_ge(qT_ready, 2 * b + 2)
                pe.wait_ge(kv_taken, b * TS + TS)
                for t in range(TS):
                    for m in range(DC):
                        last = pe.matmul(ps[:, 2 + t // 2, (t % 2) * D:(t % 2 + 1) * D], qT[:, m, t * P:(t + 1) * P],
                                         wstate[:, m, :], start=(m == 0), stop=(m == DC - 1))
                last.then_inc(y_in_psum, 1)
                pe.wait_ge(zn_ready, b + 1)
                for c in range(DC):
                    for t in range(TS):
                        last = pe.transpose(ps[:, c, t * P:(t + 1) * P], zn[:, t, c * P:(c + 1) * P], ident[:])
                last.then_inc(znT_in_psum, 1)

        @block.scalar
        def _(act):
            act.wait_ge(weights_loaded, 16 * n_loads)
            act.wait_ge(eps_set, 1)
            with act.Fori(0, B) as b:
                norms = [0]

                def deviation():
                    norms[0] += 1
                    act.wait_ge(var_ready, b * NORMS + norms[0])
                    act.activation(root[:], spread[:], ACT.Sqrt, bias=keep["eps"][:, 0:1], scale=1.0 / D).then_inc(root_ready, 1)

                deviation()
                act.wait_ge(xnT_in_psum, b + 1)
                for c in range(DC):
                    last = act.copy(xnT[:, c, :], ps[:, c, :])
                last.then_inc(xnT_ready, 1)
                act.wait_ge(q_in_psum, b + 1)
                act.activation(q0[:], ps[:, 4, :], ACT.Identity, bias=qbias[:, 0:1])
                act.activation(qsw[:], ps[:, 6, :], ACT.Identity, bias=qbias[:, 2:3]).then_inc(q_biased, 1)
                act.activation(qT[:, 1, :], ps[:, 5, :], ACT.Identity, bias=qbias[:, 1:2]).then_inc(qT_ready, 1)
                act.wait_ge(k_rotated, b + 1)
                for t in range(TS):
                    last = act.activation(square[:, t, :], kv[:, t, 0:D], ACT.Square, accum_out=ksum[:, t:t + 1])
                last.then_inc(act_step, 1)
                act.wait_ge(act_step, 2 * b + 1)
                act.activation(knorm[:], ksum[:], ACT.Sqrt).then_inc(ksum_ready, 1)
                deviation()
                deviation()
                act.wait_ge(z_ready, b + 1)
                for t in range(TS):
                    last = act.activation(square[:, t, :], zc[:, t, :], ACT.Square, accum_out=zsum[:, t:t + 1])
                last.then_inc(act_step, 1)
                act.wait_ge(act_step, 2 * b + 2)
                act.activation(zroot[:], zsum[:], ACT.Sqrt, bias=keep["eps"][:, 0:1], scale=1.0 / D).then_inc(zsum_ready, 1)
                act.wait_ge(znT_in_psum, b + 1)
                for c in range(DC):
                    last = act.activation(keep["hT"][:, c, bass.ds(b * S, S)], ps[:, c, :], ACT.Copy, scale=ln1[:, c:c + 1])
                last.then_inc(hT_done, 1)

        @block.gpsimd
        def _(pool):
            pool.memset(zeros[:], 0.0).then_inc(zeroed, 1)
            pool.memset(keep["eps"][:], EPS).then_inc(eps_set, 1)
            pool.wait_ge(weights_loaded, 16 * n_loads)
            with pool.Fori(0, B) as b:
                pool.wait_ge(xn_ready, b + 1)
                for t in range(TS):
                    last = pool.tensor_tensor(xnb[:, t, :], xn[:, t, :], outbias[:], ALU.add)
                last.then_inc(xnb_ready, 1)
                pool.wait_ge(q_biased, b + 1)
                pool.tensor_tensor(q0[:], q0[:], cos_ch[:], ALU.mult)
                pool.tensor_tensor(qsw[:], qsw[:], sin_ch[:], ALU.mult).then_inc(gp_step, 1)
                pool.wait_ge(gp_step, b + 1)
                pool.tensor_tensor(qT[:, 0, :], q0[:], qsw[:], ALU.add).then_inc(qT_ready, 1)
                pool.wait_ge(k_rotated, b + 1)
                pool.tensor_tensor(kvprod[:], kv[:, :, 0:D], kv[:, :, D:2 * D], ALU.mult).then_inc(kvprod_ready, 1)
                tiles = bass.ds(b * TS, TS)
                pool.wait_ge(x_taken, b + 1)
                pool.tensor_copy(keep["x1"][:, tiles, :], y[:])
                pool.wait_ge(z_ready, b + 1)
                pool.tensor_copy(keep["z"][:, tiles, :], zc[:]).then_inc(kept, 1)

        @block.vector
        def _(dve):
            STEPS = 19
            dve.wait_ge(weights_loaded, 16 * n_loads)
            with dve.Fori(0, B) as b:
                done, norms = [0], [0]

                def link(ins):
                    done[0] += 1
                    ins.then_inc(dve_step, 1)
                    dve.wait_ge(dve_step, b * STEPS + done[0])

                def moments(rows):
                    for t in range(TS):
                        last = dve.bn_stats(stats[:, t, :], rows[t])
                    link(last)
                    dve.tensor_tensor(mean[:], stats[:, :, 1], stats[:, :, 4], ALU.add)
                    dve.tensor_tensor(apart[:], stats[:, :, 1], stats[:, :, 4], ALU.subtract)
                    link(dve.tensor_tensor(spread[:], stats[:, :, 2], stats[:, :, 5], ALU.add))
                    dve.tensor_scalar(mean[:], mean[:], 0.5, None, ALU.mult)
                    link(dve.tensor_tensor(apart[:], apart[:], apart[:], ALU.mult))
                    dve.scalar_tensor_tensor(spread[:], apart[:], D / 4.0, spread[:], ALU.mult, ALU.add).then_inc(var_ready, 1)
                    norms[0] += 1
                    dve.wait_ge(root_ready, b * NORMS + norms[0])
                    link(dve.reciprocal(rstd[:], root[:]))

                dve.wait_ge(x_loaded, 16 * b + 16)
                moments([x[:, t, :] for t in range(TS)])
                for t in range(TS):
                    last = dve.tensor_scalar(xn[:, t, :], x[:, t, :], mean[:, t:t + 1], rstd[:, t:t + 1], ALU.subtract, ALU.mult)
                last.then_inc(xn_ready, 1)
                for t in range(TS):
                    dve.wait_ge(kv_in_psum, b * TS + t + 1)
                    last = dve.tensor_tensor(kv[:, t, :], ps[:, 2 + t % 2, :], kvbias[:], ALU.add)
                    last.then_inc(kv_taken, 1)
                dve.wait_ge(kv_taken, b * TS + TS)
                k = kv[:, :, 0:ROT]
                for a in range(2):
                    last = dve.tensor_tensor(kswap[:, :, a:ROT:2], k[:, :, 1 - a:ROT:2], sin_tok[:, :, a:ROT:2], ALU.mult)
                link(last)
                link(dve.tensor_tensor(k, k, cos_tok[:], ALU.mult))
                dve.tensor_tensor(k, k, kswap[:], ALU.add).then_inc(k_rotated, 1)
                dve.wait_ge(ksum_ready, b + 1)
                link(dve.tensor_scalar(rnorm[:], knorm[:], 1e-12, None, ALU.max))
                dve.reciprocal(rnorm[:], rnorm[:]).then_inc(rnorm_ready, 1)
                dve.wait_ge(state_in_psum, b + 1)
                link(dve.tensor_copy(state[:], ps[:, 7, 0:DC]))
                for m in range(DC):
                    last = dve.tensor_scalar(wstate[:, m, :], woutT[:, m, :], state[:, m:m + 1], None, ALU.mult)
                last.then_inc(wstate_ready, 1)
                dve.wait_ge(y_in_psum, b + 1)
                dve.wait_ge(xnb_ready, b + 1)
                for c in range(TS // 2):
                    last = dve.tensor_tensor(y[:, 2 * c:2 * c + 2, :], ps[:, 2 + c, :].rearrange("p (t d) -> p t d", d=D),
                                             xnb[:, 2 * c:2 * c + 2, :], ALU.add)
                link(last)
                moments([y[:, t, :] for t in range(TS)])
                for t in range(TS):
                    last = dve.tensor_scalar(y[:, t, :], y[:, t, :], mean[:, t:t + 1], rstd[:, t:t + 1], ALU.subtract, ALU.mult)
                link(last)
                dve.tensor_tensor(y[:], y[:], x[:], ALU.add).then_inc(x_taken, 1)
                dve.wait_ge(x_taken, b + 1)
                moments([y[:, t, :] for t in range(TS)])
                for t in range(TS):
                    last = dve.tensor_scalar(zc[:, t, :], y[:, t, :], mean[:, t:t + 1], rstd[:, t:t + 1], ALU.subtract, ALU.mult)
                last.then_inc(z_ready, 1)
                dve.wait_ge(zsum_ready, b + 1)
                link(dve.reciprocal(zscale[:], zroot[:]))
                dve.wait_ge(z_ready, b + 1)
                for t in range(TS):
                    last = dve.tensor_scalar(zn[:, t, :], zc[:, t, :], zscale[:, t:t + 1], None, ALU.mult)
                last.then_inc(zn_ready, 1)
                dve.wait_ge(hT_done, b + 1)
                dve.wait_ge(kept, b + 1)
                assert done[0] == STEPS


def attention(nc, dram, keep):
    UNITS = TS
    TURNS = UNITS * (UNITS + 1) // 2
    KT = NH * HD // P
    PAIRS = NKV // 2
    with ExitStack() as ctx:
        def sb(name, shape, dt=F32):
            return ctx.enter_context(nc.sbuf_tensor(name, shape, dt))

        def sem(name):
            return ctx.enter_context(nc.semaphore(name))

        wq = sb("wq", [P, 2, DC, QG])
        wkv = sb("wkv", [P, 2, DC, 2 * HD])
        wo = sb("wo", [P, KT, D])
        causal = sb("causal", [P, S])
        qT = sb("qTg", [P, 2, 2, S])
        kT = sb("kTg", [P, 2, S])
        vT = sb("vTg", [P, S])
        v = sb("vg", [P, 2, TS, HD])
        probs = sb("probs", [P, 2, GR, S])
        shift = sb("shift", [P, 2, GR])
        total = sb("total", [P, 2, GR])
        inverse = sb("inverse", [P, 2, GR])
        probsT = sb("probsT", [P, 4, GR * P])
        outT = sb("outT", [P, KT, S])
        ident = keep["ident"]
        ps = ctx.enter_context(nc.psum_tensor("ps2", [P, 8, 512], F32))
        SCORES, TURN, MIX, PROJ = 0, 4, 6, 7

        consts_loaded = sem("consts_loaded")
        w_loaded = [sem("w_loaded0"), sem("w_loaded1")]
        proj_in_psum = sem("proj_in_psum")
        proj_taken = sem("proj_taken")
        scores_in_psum = sem("scores_in_psum")
        shift_ready = sem("shift_ready")
        exp_done = sem("exp_done")
        probs_ready = sem("probs_ready")
        turned_in_psum = sem("turned_in_psum")
        turned_taken = [sem("turned_by_dve"), sem("turned_by_act")]
        mixed_in_psum = sem("mixed_in_psum")
        mixed_taken = sem("mixed_taken")
        rows_in_psum = sem("rows_in_psum")
        rows_added = sem("rows_added")
        dve_step = sem("dve_step2")
        dve_passed = sem("dve_passed")
        pe_passed = sem("pe_passed")

        block = ctx.enter_context(nc.Block())

        WIDTH = [4, 3, 2, 1]
        FIRST = [0, 4, 7, 9]
        AGENDA = [
            ["turn 0", "turn 1", "score 0", "mix 0", "project 1", "turn 2", "score 1", "turn 3", "score 2", "mix 1", "score 3",
             "project 2", "mix 2", "mix 3"],
            ["turn 0", "turn 1", "score 0", "score 1", "turn 2", "mix 0", "score 2", "score 3", "project 3", "mix 1", "mix 2"],
            ["turn 0", "turn 1", "score 0", "score 1", "score 2", "score 3", "mix 0", "mix 1"],
            ["turn 0", "score 0", "score 1", "score 2", "score 3", "project 0", "mix 0"],
        ]

        def steps(u, nxt, following, behind=0):
            todo = [(what, int(n)) for what, n in (step.split() for step in AGENDA[u])]
            late = [(at + (behind if step[0] == "score" else 0), at, step) for at, step in enumerate(todo)]
            for _, _, (what, n) in sorted(late):
                if not (what == "score" and not nxt or what == "project" and not following):
                    yield what, n

        def over_sequences(eng, first, unit, end):
            def group(turn, pair, par, more, ahead=True):
                it, g = turn * 2 + par, pair * 2 + par
                following = (turn, 1) if par == 0 else (turn + 1, 0)
                for u in range(UNITS):
                    if u + 1 < UNITS:
                        unit(it, g, par, u, (turn, par, u + 1), following if more else None)
                    else:
                        unit(it, g, par, u, (*following, 0) if more else None, (turn + 1, par) if ahead else None)

            first((0, 0), (0, 1))
            with eng.Fori(0, B - 1) as b:
                with eng.Fori(0, PAIRS) as pair:
                    turn = eng.snap(b * PAIRS + pair)
                    group(turn, pair, 0, True)
                    group(turn, pair, 1, True)
                end(b)
            b = B - 1
            with eng.Fori(0, PAIRS - 1) as pair:
                turn = eng.snap(pair + b * PAIRS)
                group(turn, pair, 0, True)
                group(turn, pair, 1, True)
            pair = PAIRS - 1
            group(b * PAIRS + pair, pair, 0, True, False)
            group(b * PAIRS + pair, pair, 1, False, False)
            end(b)

        @block.sync
        def _(sp):
            sp.dma_start(wo[:], dram["wo"].rearrange("(k p) n -> p k n", p=P)).then_inc(consts_loaded, 16)
            sp.dma_start(causal[:], dram["causal"]).then_inc(consts_loaded, 16)
            wqd = dram["wq"].rearrange("g (c p) n -> g p c n", p=P)
            wkvd = dram["wkv"].rearrange("g (c p) n -> g p c n", p=P)
            with sp.Fori(0, B) as b:
                with sp.Fori(0, NKV // 2) as pair:
                    for par in range(2):
                        sp.wait_ge(proj_in_psum, (b * NKV + pair * 2 + par) * 4 + 4)
                        g = bass.ds(pair * 2 + par, 1)
                        sp.dma_start(wq[:, par], wqd[g].rearrange("o p c n -> (o p) c n")).then_inc(w_loaded[par], 16)
                        sp.dma_start(wkv[:, par], wkvd[g].rearrange("o p c n -> (o p) c n")).then_inc(w_loaded[par], 16)

        @block.tensor
        def _(pe):
            pe.sem_inc(proj_in_psum, 8)
            pe.wait_ge(consts_loaded, 32)

            def project(turn, par, part):
                it, b = turn * 2 + par, turn // PAIRS
                if part == 0:
                    pe.wait_ge(w_loaded[par], turn * 32 + 32)
                pe.wait_ge(proj_taken, it * 4 + part + 1)
                if part == 1:
                    pe.sem_inc(pe_passed, 1)
                    for t in range(TS):
                        last = pe.transpose(ps[:, PROJ, t * HD:(t + 1) * HD], vT[HD:2 * HD, t * P:(t + 1) * P],
                                            ident[HD:2 * HD, HD:2 * HD])
                else:
                    for c in range(DC):
                        w = wkv[:, par, c, :] if part == 0 else wq[:, par, c, (part - 2) * P:(part - 1) * P]
                        last = pe.matmul(ps[:, PROJ, :], w, keep["hT"][:, c, bass.ds(b * S, S)], start=(c == 0), stop=(c == DC - 1))
                last.then_inc(proj_in_psum, 1)

            def score(turn, par, u, h):
                it, n, i = turn * 2 + par, WIDTH[u] * P, WIDTH[u] - 1
                if u == 0 and h == 0:
                    pe.wait_ge(proj_taken, it * 4 + 5)
                half = slice(h % 2 * HD, h % 2 * HD + HD)
                pe.wait_ge(exp_done, (it * UNITS + u) * GR + h + 1)
                pe.matmul(ps[:, SCORES + h, 0:n], qT[half, par, h // 2, i * P:(i + 1) * P], kT[half, par, 0:n],
                          start=True, stop=True).then_inc(scores_in_psum, 1)

            def first(group, second):
                for part in range(4):
                    project(*group, part)
                project(*second, 0)
                for h in range(GR):
                    score(*group, 0, h)

            def unit(it, g, par, u, nxt, following):
                if u == 0:
                    pe.wait_ge(rows_added, (it // NKV) + 1)
                for what, j in steps(u, nxt, following):
                    n = FIRST[u] + j
                    if what == "turn":
                        pe.wait_ge(turned_taken[n % 2], it * (TURNS // 2) + n // 2 + 1)
                        for h in range(GR):
                            if j == 0:
                                pe.wait_ge(probs_ready, (it * UNITS + u) * GR + h + 1)
                            last = pe.transpose(ps[:, TURN + n % 2, h * P:(h + 1) * P], probs[:, u % 2, h, j * P:(j + 1) * P], ident[:])
                        last.then_inc(turned_in_psum, 1)
                    elif what == "mix":
                        pe.wait_ge(turned_taken[n % 2], it * (TURNS // 2) + n // 2 + 2)
                        if j == 0:
                            pe.wait_ge(mixed_taken, it * UNITS + u + 1)
                        heads = probsT[:, (n + 2 * par) % 4, :].rearrange("p (m a q) -> p a m q", a=2, q=P)
                        for a in range(2):
                            last = pe.matmul(ps[a * HD:(a + 1) * HD, MIX, 0:2 * P].rearrange("p (m q) -> p m q", q=P),
                                             v[:, par, j, :], heads[:, a], start=(j == 0), stop=(j == WIDTH[u] - 1))
                        if j == WIDTH[u] - 1:
                            last.then_inc(mixed_in_psum, 1)
                    elif what == "score":
                        score(*nxt, j)
                    else:
                        project(*following, j)

            def end(b):
                pe.wait_ge(mixed_taken, (b + 1) * (NKV * UNITS) + 1)
                pe.wait_ge(turned_taken[0], (b + 1) * (NKV * TURNS // 2) + 1)
                pe.wait_ge(turned_taken[1], (b + 1) * (NKV * TURNS // 2) + 1)
                for t in range(TS):
                    for k in range(KT):
                        last = pe.matmul(ps[:, TURN + t // 2, t % 2 * D:(t % 2 + 1) * D], outT[:, k, t * P:(t + 1) * P], wo[:, k, :],
                                         start=(k == 0), stop=(k == KT - 1))
                    if t % 2:
                        last.then_inc(rows_in_psum, 1)

            over_sequences(pe, first, unit, end)

        @block.scalar
        def _(act):
            act.sem_inc(proj_taken, 1)
            act.sem_inc(exp_done, GR)
            act.sem_inc(turned_taken[1], 1)
            act.sem_inc(mixed_taken, 1)

            def take(turn, par, part):
                act.wait_ge(proj_in_psum, (turn * 2 + par) * 4 + part + 9)
                if part == 0:
                    act.copy(kT[0:HD, par, :], ps[0:HD, PROJ, :])
                    act.copy(kT[HD:2 * HD, par, :], ps[0:HD, PROJ, :])
                    last = act.copy(vT[HD:2 * HD, :], ps[HD:2 * HD, PROJ, :])
                elif part == 1:
                    last = act.copy(v[:, par, :, :], ps[:, PROJ, 0:TS * HD].rearrange("p (t d) -> p t d", d=HD))
                else:
                    last = act.copy(qT[:, par, part - 2, :], ps[:, PROJ, :])
                last.then_inc(proj_taken, 1)

            def exponential(turn, par, u, h):
                n = WIDTH[u] * P
                act.wait_ge(shift_ready, ((turn * 2 + par) * UNITS + u) * GR + h + 1)
                act.activation(probs[:, u % 2, h, 0:n], ps[:, SCORES + h, 0:n], ACT.Exp, bias=shift[:, u % 2, h:h + 1],
                               scale=-1.0, accum_out=total[:, u % 2, h:h + 1]).then_inc(exp_done, 1)

            def first(group, second):
                for part in range(4):
                    take(*group, part)
                take(*second, 0)
                for h in range(GR):
                    exponential(*group, 0, h)

            def unit(it, g, par, u, nxt, following):
                for what, j in steps(u, nxt, following, behind=1):
                    n = FIRST[u] + j
                    if what == "turn" and n % 2:
                        act.wait_ge(turned_in_psum, it * TURNS + n + 1)
                        act.copy(probsT[:, (n + 2 * par) % 4, :], ps[:, TURN + 1, :]).then_inc(turned_taken[1], 1)
                    elif what == "score":
                        exponential(*nxt, j)
                    elif what == "project":
                        take(*following, j)
                i = WIDTH[u] - 1
                act.wait_ge(mixed_in_psum, it * UNITS + u + 1)
                act.copy(outT[:, bass.ds(g * 2, 2), i * P:(i + 1) * P],
                         ps[:, MIX, 0:2 * P].rearrange("p (m q) -> p m q", q=P)).then_inc(mixed_taken, 1)

            over_sequences(act, first, unit, lambda b: None)

        @block.vector
        def _(dve):
            dve.sem_inc(turned_taken[0], 1)
            dve.sem_inc(rows_added, 1)
            dve.wait_ge(consts_loaded, 32)

            def largest(turn, par, u, h):
                n = WIDTH[u] * P
                dve.wait_ge(scores_in_psum, ((turn * 2 + par) * UNITS + u) * GR + h + 1)
                dve.sem_inc(dve_passed, 1)
                bank = ps[:, SCORES + h, 0:n]
                dve.tensor_tensor_reduce(bank, bank, causal[:, S - n:S], -float(HD) ** -0.5, -NEG, ALU.add, ALU.min,
                                         shift[:, u % 2, h:h + 1]).then_inc(shift_ready, 1)

            def first(group, second):
                for h in range(GR):
                    largest(*group, 0, h)

            def unit(it, g, par, u, nxt, following):
                n = WIDTH[u] * P
                for h in range(0, GR, 2):
                    dve.wait_ge(exp_done, (it * UNITS + u) * GR + GR + h + 2)
                    dve.reciprocal(inverse[:, u % 2, h:h + 2], total[:, u % 2, h:h + 2]).then_inc(dve_step, 1)
                    dve.wait_ge(dve_step, (it * UNITS + u) * 2 + h // 2 + 1)
                    for k in range(h, h + 2):
                        dve.tensor_scalar(probs[:, u % 2, k, 0:n], probs[:, u % 2, k, 0:n], inverse[:, u % 2, k:k + 1],
                                          None, ALU.mult).then_inc(probs_ready, 1)
                for what, j in steps(u, nxt, following):
                    n = FIRST[u] + j
                    if what == "score":
                        largest(*nxt, j)
                    elif what == "turn" and n % 2 == 0:
                        dve.wait_ge(turned_in_psum, it * TURNS + n + 1)
                        dve.tensor_copy(probsT[:, (n + 2 * par) % 4, :], ps[:, TURN, :]).then_inc(turned_taken[0], 1)

            def end(b):
                for k in range(2):
                    dve.wait_ge(rows_in_psum, b * 2 + k + 1)
                    rows = keep["z"][:, bass.ds(b * TS + 2 * k, 2), :]
                    last = dve.tensor_tensor(rows, rows, ps[:, TURN + k, :].rearrange("p (t d) -> p t d", d=D), ALU.add)
                last.then_inc(rows_added, 1)

            over_sequences(dve, first, unit, end)


def route(nc, dram, keep):
    ROUND = 4
    with ExitStack() as ctx:
        def sb(name, shape, dt=F32):
            return ctx.enter_context(nc.sbuf_tensor(name, shape, dt))

        def sem(name):
            return ctx.enter_context(nc.semaphore(name))

        ln2 = sb("ln2", [P, D])
        gate = sb("gate", [P, DC, E])
        before = sb("before", [P, P])
        ones = sb("ones", [P, P])
        expert_ids = sb("expert_ids", [P, E])
        block_ids = sb("block_ids", [P, NBLK])
        square = sb("square3", [P, TT, D])
        meansq = sb("meansq", [P, TT])
        root = sb("root3", [P, TT])
        scale = sb("scale3", [P, TT])
        t_rows = sb("t_rows", [P, TT, D])
        tT = sb("tT", [P, 2, DC, ROUND * P])
        logits = sb("logits", [P, TT, E])
        largest = sb("largest", [P, TT])
        odds = sb("odds", [P, TT, E])
        odds_sum = sb("odds_sum", [P, TT])
        prob = sb("prob", [P, TT, E])
        best = sb("best", [P, TT, 8])
        best_at = sb("best_at", [P, TT, 8], U32)
        best_id = sb("best_id", [P, TT, TOPK])
        pair_sum = sb("pair_sum", [P, TT])
        chosen = [sb(f"chosen{k}", [P, TT, E]) for k in range(TOPK)]
        member = sb("member", [P, TT, E])
        count = sb("count", [P, TT + 1, E])
        nblocks_i = sb("nblocks_i", [P, E], I32)
        nblocks = sb("nblocks", [P, E])
        blocks_end = sb("blocks_end", [P, E])
        first_slot = sb("first_slot", [P, E])
        slot = sb("slot", [P, TT, E])
        picked = [sb(f"picked{k}", [P, TT, E]) for k in range(TOPK)]
        slot_k = sb("slot_k", [P, TOPK, TT])
        past = sb("past", [P, NBLK, E])
        owner = sb("owner", [P, NBLK])
        ps = ctx.enter_context(nc.psum_tensor("ps3", [P, 8, 512], F32))
        LOGITS, BEFORE, TOTAL = 4, 5, 6

        loaded = sem("loaded3")
        ones_set = sem("ones_set")
        square_sum = sem("square_sum")
        root_ready = sem("root_ready3")
        t_ready = sem("t_ready")
        turned = sem("turned3")
        turned_taken = sem("turned_taken3")
        logits_in_psum = sem("logits_in_psum")
        shifted = sem("shifted")
        odds_ready = sem("odds_ready")
        member_ready = sem("member_ready")
        counted = sem("counted")
        slots_ready = sem("slots_ready")
        scattered = sem("scattered")
        dve_step = sem("dve_step3")

        block = ctx.enter_context(nc.Block())
        loads = [(ln2[:], dram["ln2"].to_broadcast([P, D])), (gate[:], dram["gate_w"].rearrange("(c p) e -> p c e", p=P)),
                 (before[:], dram["before"]), (expert_ids[:], dram["expert_ids"]), (block_ids[:], dram["block_ids"])]

        @block.sync
        def _(sp):
            for dst, src in loads:
                sp.dma_start(dst, src).then_inc(loaded, 16)

        @block.scalar
        def _(act):
            for t in range(TT):
                last = act.activation(square[:, t, :], keep["z"][:, t, :], ACT.Square, accum_out=meansq[:, t:t + 1])
            last.then_inc(square_sum, 1)
            act.wait_ge(square_sum, 1)
            act.activation(root[:], meansq[:], ACT.Sqrt, bias=keep["eps"][:, 0:1], scale=1.0 / D).then_inc(root_ready, 1)
            for r in range(TT // ROUND):
                act.wait_ge(turned, r + 1)
                for c in range(DC):
                    last = act.copy(tT[:, r % 2, c, :], ps[:, r % 2 * DC + c, :])
                last.then_inc(turned_taken, 1)
            act.wait_ge(shifted, 1)
            act.activation(odds[:], odds[:], ACT.Exp).then_inc(odds_ready, 1)

        @block.tensor
        def _(pe):
            pe.wait_ge(loaded, 16 * len(loads))
            for r in range(TT // ROUND):
                pe.wait_ge(t_ready, (r + 1) * ROUND)
                if r >= 2:
                    pe.wait_ge(turned_taken, r - 1)
                for c in range(DC):
                    for t in range(ROUND):
                        last = pe.transpose(ps[:, r % 2 * DC + c, t * P:(t + 1) * P], t_rows[:, r * ROUND + t, c * P:(c + 1) * P],
                                            keep["ident"][:])
                last.then_inc(turned, 1)
                pe.wait_ge(turned_taken, r + 1)
                for t in range(ROUND):
                    at = (r * ROUND + t) * E
                    for c in range(DC):
                        last = pe.matmul(ps[:, LOGITS, at:at + E], tT[:, r % 2, c, t * P:(t + 1) * P], gate[:, c, :],
                                         start=(c == 0), stop=(c == DC - 1))
            last.then_inc(logits_in_psum, 1)
            pe.wait_ge(ones_set, 1)
            pe.wait_ge(member_ready, 1)
            flat = member[:].rearrange("p t e -> p (t e)")
            pe.matmul(ps[:, BEFORE, 0:TT * E], before[:], flat, start=True, stop=True)
            pe.matmul(ps[:, TOTAL, 0:TT * E], ones[:], flat, start=True, stop=True).then_inc(counted, 1)

        @block.gpsimd
        def _(pool):
            pool.memset(ones[:], 1.0).then_inc(ones_set, 1)
            pool.wait_ge(slots_ready, 1)
            pool.wait_ge(t_ready, TT)
            for t in range(TT):
                for k in range(TOPK):
                    pool.indirect_dma_start(dram["slot_rows"], bass.IndirectOffsetOnAxis(keep["slots"][:, k, t:t + 1], 0),
                                            t_rows[:, t, :], None).then_inc(scattered, 16)
            pool.wait_ge(scattered, 16 * TT * TOPK)

        @block.vector
        def _(dve):
            done = [0]

            def link(ins):
                done[0] += 1
                ins.then_inc(dve_step, 1)
                dve.wait_ge(dve_step, done[0])

            dve.wait_ge(loaded, 16 * len(loads))
            dve.wait_ge(root_ready, 1)
            link(dve.reciprocal(scale[:], root[:]))
            for t in range(TT):
                dve.scalar_tensor_tensor(t_rows[:, t, :], keep["z"][:, t, :], scale[:, t:t + 1], ln2[:], ALU.mult, ALU.mult)\
                   .then_inc(t_ready, 1)
            dve.wait_ge(logits_in_psum, 1)
            link(dve.tensor_copy(logits[:].rearrange("p t e -> p (t e)"), ps[:, LOGITS, 0:TT * E]))
            link(dve.tensor_reduce(largest[:], logits[:], AX.X, ALU.max))
            dve.tensor_tensor(odds[:], logits[:], largest[:].unsqueeze(2).to_broadcast([P, TT, E]), ALU.subtract)\
               .then_inc(shifted, 1)
            dve.wait_ge(odds_ready, 1)
            link(dve.tensor_reduce(odds_sum[:], odds[:], AX.X, ALU.add))
            link(dve.reciprocal(odds_sum[:], odds_sum[:]))
            link(dve.tensor_tensor(prob[:], odds[:], odds_sum[:].unsqueeze(2).to_broadcast([P, TT, E]), ALU.mult))
            for t in range(TT):
                last = dve.max(best[:, t, :], prob[:, t, :])
            link(last)
            for t in range(TT):
                last = dve.max_index(best_at[:, t, :], best[:, t, :], prob[:, t, :])
            link(last)
            dve.tensor_copy(best_id[:], best_at[:, :, 0:TOPK])
            link(dve.tensor_tensor(pair_sum[:], best[:, :, 0], best[:, :, 1], ALU.add))
            link(dve.reciprocal(pair_sum[:], pair_sum[:]))
            dve.tensor_tensor(keep["shares"][:], best[:, :, 0:TOPK], pair_sum[:].unsqueeze(2).to_broadcast([P, TT, TOPK]), ALU.mult)
            ids = expert_ids[:].unsqueeze(1).to_broadcast([P, TT, E])
            for k in range(TOPK):
                last = dve.tensor_tensor(chosen[k][:], ids, best_id[:, :, k:k + 1].to_broadcast([P, TT, E]), ALU.is_equal)
            link(last)
            dve.tensor_tensor(member[:], chosen[0][:], chosen[1][:], ALU.add).then_inc(member_ready, 1)
            link(dve.memset(count[:, 0, :], 0.0))
            dve.wait_ge(counted, 1)
            for t in range(TT):
                link(dve.tensor_tensor(count[:, t + 1, :], count[:, t, :], ps[:, TOTAL, t * E:(t + 1) * E], ALU.add))
            link(dve.tensor_scalar(nblocks_i[:], count[:, TT, :], float(BLK - 1), None, ALU.add))
            link(dve.tensor_scalar(nblocks_i[:], nblocks_i[:], BLK.bit_length() - 1, None, ALU.arith_shift_right))
            link(dve.tensor_copy(nblocks[:], nblocks_i[:]))
            link(dve.tensor_copy(blocks_end[:, 0:1], nblocks[:, 0:1]))
            for e in range(1, E):
                link(dve.tensor_tensor(blocks_end[:, e:e + 1], blocks_end[:, e - 1:e], nblocks[:, e:e + 1], ALU.add))
            link(dve.tensor_tensor(first_slot[:], blocks_end[:], nblocks[:], ALU.subtract))
            link(dve.tensor_scalar(first_slot[:], first_slot[:], float(BLK), None, ALU.mult))
            link(dve.tensor_tensor(slot[:], count[:, 0:TT, :], first_slot[:].unsqueeze(1).to_broadcast([P, TT, E]), ALU.add))
            link(dve.tensor_tensor(slot[:], slot[:], ps[:, BEFORE, 0:TT * E].rearrange("p (t e) -> p t e", e=E), ALU.add))
            for k in range(TOPK):
                last = dve.tensor_tensor(picked[k][:], chosen[k][:], slot[:], ALU.mult)
            link(last)
            for k in range(TOPK):
                last = dve.tensor_reduce(slot_k[:, k, :], picked[k][:], AX.X, ALU.add)
            link(last)
            dve.tensor_copy(keep["slots"][:], slot_k[:]).then_inc(slots_ready, 1)
            link(dve.tensor_tensor(past[:], blocks_end[:].unsqueeze(1).to_broadcast([P, NBLK, E]),
                                   block_ids[:].unsqueeze(2).to_broadcast([P, NBLK, E]), ALU.is_le))
            link(dve.tensor_reduce(owner[:], past[:], AX.X, ALU.add))
            link(dve.tensor_scalar(keep["block_expert"][:], owner[:], float(E - 1), None, ALU.min))


def experts(nc, dram, keep):
    with ExitStack() as ctx:
        def sb(name, shape, dt=F32):
            return ctx.enter_context(nc.sbuf_tensor(name, shape, dt))

        def sem(name):
            return ctx.enter_context(nc.semaphore(name))

        w1 = sb("w1", [P, 2, DC, F])
        w3 = sb("w3", [P, 2, DC, F])
        w2 = sb("w2", [P, 2, FC, D])
        rows = sb("rows", [P, 2, BH, D])
        rowsT = sb("rowsT", [P, 2, DC, BLK])
        relu = sb("relu", [P, 4, BLK])
        gatedT = sb("gatedT", [P, 2, FC, BLK])
        result = sb("result", [P, 2, BH, D])
        ps = ctx.enter_context(nc.psum_tensor("ps4", [P, 8, 512], F32))
        TURN, DOWN, UP = 0, 2, 4

        w_loaded = [sem("up_loaded0"), sem("up_loaded1")]
        rows_loaded = [sem("rows_loaded0"), sem("rows_loaded1")]
        turned = sem("turned4")
        turned_taken = sem("turned_taken4")
        up_in_psum = sem("up_in_psum")
        relu_ready = sem("relu_ready")
        gated_ready = sem("gated_ready")
        down_in_psum = sem("down_in_psum")
        result_ready = sem("result_ready")
        stored = [sem("stored0"), sem("stored1")]

        block = ctx.enter_context(nc.Block())
        slot_rows = dram["slot_rows"].rearrange("(n h p) d -> n p h d", h=BH, p=P)
        expert_rows = dram["expert_rows"].rearrange("(n h p) d -> n p h d", h=BH, p=P)

        def one(ap):
            return ap.rearrange("o p c n -> (o p) c n")

        def over_blocks(eng, step):
            with eng.Fori(0, NBLK // 2) as pair:
                step(pair * 2, pair, 0, True)
                step(pair * 2 + 1, pair, 1, True)
            if NBLK % 2:
                step(NBLK - 1, NBLK // 2, 0, False)

        @block.sync
        def _(sp):
            def step(j, pair, par, more):
                e = sp.value_load(keep["block_expert"][0:1, bass.ds(j, 1)], min_val=0, max_val=E - 1)
                sp.wait_ge(down_in_psum, j + 1)
                sp.dma_start(rows[:, par], one(slot_rows[bass.ds(j, 1)])).then_inc(rows_loaded[par], 16)
                at = bass.ds(e, 1)
                sp.dma_start(w1[:, par], one(dram["w1"].rearrange("e (c p) f -> e p c f", p=P)[at])).then_inc(w_loaded[par], 16)
                sp.dma_start(w3[:, par], one(dram["w3"].rearrange("e (c p) f -> e p c f", p=P)[at])).then_inc(w_loaded[par], 16)
                sp.dma_start(w2[:, par], one(dram["w2"].rearrange("e (c p) d -> e p c d", p=P)[at])).then_inc(w_loaded[par], 16)

            over_blocks(sp, step)

        @block.tensor
        def _(pe):
            pe.sem_inc(down_in_psum, 2)

            def turn(j, pair, par):
                pe.wait_ge(rows_loaded[par], pair * 16 + 16)
                for c in range(DC):
                    for h in range(BH):
                        last = pe.transpose(ps[:, TURN + par, c * BLK + h * P:c * BLK + (h + 1) * P], rows[:, par, h, c * P:(c + 1) * P],
                                            keep["ident"][:])
                last.then_inc(turned, 1)

            def step(j, pair, par, more):
                pe.wait_ge(turned_taken, j + 1)
                pe.wait_ge(w_loaded[par], pair * 48 + 48)
                for m in range(FC):
                    pe.wait_ge(gated_ready, j * FC + m + FC - 3)
                    for w, at in ((w1, 0), (w3, BLK)):
                        for c in range(DC):
                            last = pe.matmul(ps[:, UP + m % 4, at:at + BLK], w[:, par, c, m * P:(m + 1) * P], rowsT[:, par, c, :],
                                             start=(c == 0), stop=(c == DC - 1))
                    last.then_inc(up_in_psum, 1)
                if more:
                    if par == 0:
                        turn(j + 1, pair, 1)
                    else:
                        turn(j + 1, pair + 1, 0)
                pe.wait_ge(result_ready, j + 1)
                for h in range(BH):
                    for m in range(FC):
                        if h == 0:
                            pe.wait_ge(gated_ready, j * FC + m + 1 + FC)
                        last = pe.matmul(ps[:, DOWN, h * D:(h + 1) * D], gatedT[:, par, m, h * P:(h + 1) * P], w2[:, par, m, :],
                                         start=(m == 0), stop=(m == FC - 1))
                last.then_inc(down_in_psum, 1)

            turn(0, 0, 0)
            over_blocks(pe, step)

        @block.scalar
        def _(act):
            act.sem_inc(result_ready, 1)
            act.sem_inc(stored[0], 16)
            act.sem_inc(stored[1], 16)

            def take_turned(j, par):
                act.wait_ge(turned, j + 1)
                act.copy(rowsT[:, par].rearrange("p c n -> p (c n)"), ps[:, TURN + par, 0:DC * BLK]).then_inc(turned_taken, 1)

            def step(j, pair, par, more):
                for m in range(FC):
                    act.wait_ge(up_in_psum, j * FC + m + 1)
                    act.activation(relu[:, m % 4, :], ps[:, UP + m % 4, 0:BLK], ACT.Relu).then_inc(relu_ready, 1)
                if more:
                    take_turned(j + 1, 1 - par)
                act.wait_ge(down_in_psum, j + 3)
                act.wait_ge(stored[par], pair * 16 + 16)
                act.copy(result[:, par].rearrange("p h d -> p (h d)"), ps[:, DOWN, 0:BH * D]).then_inc(result_ready, 1)
                act.wait_ge(result_ready, j + 2)
                act.dma_start(one(expert_rows[bass.ds(j, 1)]), result[:, par]).then_inc(stored[par], 16)

            take_turned(0, 0)
            over_blocks(act, step)
            act.wait_ge(stored[0], 16 * ((NBLK + 1) // 2) + 16)
            act.wait_ge(stored[1], 16 * (NBLK // 2) + 16)

        @block.vector
        def _(dve):
            dve.sem_inc(gated_ready, FC)

            def step(j, pair, par, more):
                for m in range(FC):
                    dve.wait_ge(relu_ready, j * FC + m + 1)
                    dve.tensor_tensor(gatedT[:, par, m, :], relu[:, m % 4, :], ps[:, UP + m % 4, BLK:2 * BLK], ALU.mult)\
                       .then_inc(gated_ready, 1)

            over_blocks(dve, step)


def combine(nc, dram, keep):
    with ExitStack() as ctx:
        def sb(name, shape, dt=F32):
            return ctx.enter_context(nc.sbuf_tensor(name, shape, dt))

        def sem(name):
            return ctx.enter_context(nc.semaphore(name))

        y = sb("y5", [P, TT, TOPK, D])
        stats = sb("stats5", [P, TT, 6])
        mean = sb("mean5", [P, TT])
        apart = sb("apart5", [P, TT])
        spread = sb("spread5", [P, TT])
        root = sb("root5", [P, TT])
        rstd = sb("rstd5", [P, TT])
        final = sb("final5", [P, TT, D])

        gathered = [sem(f"gathered{b}") for b in range(B)]
        mixed = sem("mixed5")
        var_ready = sem("var_ready5")
        root_ready = sem("root_ready5")
        out_ready = sem("out_ready5")
        stored = sem("stored5")
        dve_step = sem("dve_step5")

        block = ctx.enter_context(nc.Block())

        @block.gpsimd
        def _(pool):
            for t in range(TT):
                for k in range(TOPK):
                    pool.indirect_dma_start(y[:, t, k, :], None, dram["expert_rows"],
                                            bass.IndirectOffsetOnAxis(keep["slots"][:, k, t:t + 1], 0)).then_inc(gathered[t // TS], 16)

        @block.scalar
        def _(act):
            for b in range(B):
                at = slice(b * TS, (b + 1) * TS)
                act.wait_ge(var_ready, b + 1)
                act.activation(root[:, at], spread[:, at], ACT.Sqrt, bias=keep["eps"][:, 0:1], scale=1.0 / D).then_inc(root_ready, 1)

        @block.sync
        def _(sp):
            for b in range(B):
                sp.wait_ge(out_ready, b + 1)
                sp.dma_start(dram["out"][b].rearrange("(t p) d -> p t d", p=P), final[:, b * TS:(b + 1) * TS, :]).then_inc(stored, 16)
            sp.wait_ge(stored, 16 * B)

        @block.vector
        def _(dve):
            done = [0]

            def link(ins):
                done[0] += 1
                ins.then_inc(dve_step, 1)
                dve.wait_ge(dve_step, done[0])

            for b in range(B):
                tiles = range(b * TS, (b + 1) * TS)
                at = slice(b * TS, (b + 1) * TS)
                dve.wait_ge(gathered[b], 16 * TOPK * TS)
                for k in range(TOPK):
                    for t in tiles:
                        last = dve.scalar_tensor_tensor(keep["z"][:, t, :], y[:, t, k, :], keep["shares"][:, t, k:k + 1], keep["z"][:, t, :],
                                                        ALU.mult, ALU.add)
                    link(last)
                for t in tiles:
                    last = dve.bn_stats(stats[:, t, :], keep["z"][:, t, :])
                link(last)
                dve.tensor_tensor(mean[:, at], stats[:, at, 1], stats[:, at, 4], ALU.add)
                dve.tensor_tensor(apart[:, at], stats[:, at, 1], stats[:, at, 4], ALU.subtract)
                link(dve.tensor_tensor(spread[:, at], stats[:, at, 2], stats[:, at, 5], ALU.add))
                dve.tensor_scalar(mean[:, at], mean[:, at], 0.5, None, ALU.mult)
                link(dve.tensor_tensor(apart[:, at], apart[:, at], apart[:, at], ALU.mult))
                dve.scalar_tensor_tensor(spread[:, at], apart[:, at], D / 4.0, spread[:, at], ALU.mult, ALU.add).then_inc(var_ready, 1)
                dve.wait_ge(root_ready, b + 1)
                link(dve.reciprocal(rstd[:, at], root[:, at]))
                for t in tiles:
                    last = dve.tensor_scalar(final[:, t, :], keep["z"][:, t, :], mean[:, t:t + 1], rstd[:, t:t + 1], ALU.subtract, ALU.mult)
                link(last)
                dve.tensor_tensor(final[:, at, :], final[:, at, :], keep["x1"][:, at, :], ALU.add).then_inc(out_ready, 1)


def program(nc, dram):
    with ExitStack() as ctx:
        def sb(name, shape, dt=F32):
            return ctx.enter_context(nc.sbuf_tensor(name, shape, dt))

        keep = dict(
            ident=sb("ident", [P, P]),
            eps=sb("eps", [P, 1]),
            x1=sb("x1", [P, TT, D]),
            z=sb("z", [P, TT, D]),
            hT=sb("hT", [P, DC, T]),
            slots=sb("slots", [P, TOPK, TT], U32),
            shares=sb("shares", [P, TT, TOPK]),
            block_expert=sb("block_expert", [P, NBLK], I32),
        )
        layer_one(nc, dram, keep)
        attention(nc, dram, keep)
        route(nc, dram, keep)
        experts(nc, dram, keep)
        combine(nc, dram, keep)


def kernel(**inputs):
    import concourse.bacc as bacc
    from concourse.bass_utils import run_bass_kernel_spmd

    X, W_in, W_out = (np.asarray(inputs[f"L0_attn_{n}"]) for n in ("X", "W_in", "W_out"))
    b_in, b_out = np.asarray(inputs["L0_attn_b_in"]), np.asarray(inputs["L0_attn_b_out"])
    ffn = {n: np.asarray(inputs[f"L0_ffn_{n}"]) for n in ("ln1_w", "wq", "wk", "wv", "wo", "ln2_w", "gate_w", "w1", "w2", "w3")}

    inv_freq = (1.0 / np.float32(10000.0) ** (np.arange(0, ROT, 2, dtype=np.float32) / np.float32(ROT))).astype(np.float32)
    angle = np.repeat(np.arange(S, dtype=np.float32)[:, None] * inv_freq[None, :], 2, axis=-1)
    cos = np.cos(angle).astype(np.float32)
    sin = (np.sin(angle) * np.where(np.arange(ROT) % 2 == 0, -1.0, 1.0)).astype(np.float32)
    swap = np.arange(ROT).reshape(-1, 2)[:, ::-1].ravel()
    causal = np.zeros((P, S), np.float32)
    causal[:, S - P:] = np.where(np.arange(P)[:, None] >= np.arange(P)[None, :], 0.0, NEG)

    arrays = {
        "x": X,
        "winT": W_in.T,
        "wswT": W_in[swap].T,
        "woutT": W_out.T,
        "b_in": b_in[None, :],
        "b_out": b_out[None, :],
        "qbias": np.stack([b_in[:P], b_in[P:2 * P], b_in[swap]], axis=1),
        "ln1": ffn["ln1_w"].reshape(DC, P).T,
        "ln2": ffn["ln2_w"][None, :],
        "wq": ffn["wq"].reshape(D, NKV, QG).transpose(1, 0, 2),
        "wkv": np.concatenate([ffn["wk"].reshape(D, NKV, HD), ffn["wv"].reshape(D, NKV, HD)], axis=2).transpose(1, 0, 2),
        "wo": ffn["wo"],
        "gate_w": ffn["gate_w"],
        "w1": ffn["w1"],
        "w2": ffn["w2"],
        "w3": ffn["w3"],
        "cos_tok": cos,
        "sin_tok": sin,
        "cos_ch": cos.T,
        "sin_ch": sin.T,
        "ident": np.eye(P, dtype=np.float32),
        "causal": causal,
        "before": np.triu(np.ones((P, P), np.float32), 1),
        "expert_ids": np.tile(np.arange(E, dtype=np.float32), (P, 1)),
        "block_ids": np.tile(np.arange(NBLK, dtype=np.float32), (P, 1)),
    }
    nc = bacc.Bacc("TRN2", target_bir_lowering=False, num_devices=1)
    given, dram = {}, {}
    for name, array in arrays.items():
        array = np.ascontiguousarray(array)
        given[f"in_{name}"] = array
        dram[name] = nc.dram_tensor(f"in_{name}", array.shape, mybir.dt.from_np(array.dtype), kind="ExternalInput").ap()
    dram["slot_rows"] = nc.dram_tensor("slot_rows", (SLOTS, D), F32, kind="Internal").ap()
    dram["expert_rows"] = nc.dram_tensor("expert_rows", (SLOTS, D), F32, kind="Internal").ap()
    dram["out"] = nc.dram_tensor("out_rows", (B, S, D), F32, kind="ExternalOutput").ap()
    program(nc, dram)
    result = run_bass_kernel_spmd(nc, [given], core_ids=[0])
    return result.results[0]["out_rows"]
```

```python
from contextlib import ExitStack

import numpy as np

import concourse.bass as bass
from concourse import mybir

ALU = mybir.AluOpType
ACT = mybir.ActivationFunctionType
AX = mybir.AxisListType
F32 = mybir.dt.float32
F32R = mybir.dt.float32r
I32 = mybir.dt.int32
U32 = mybir.dt.uint32

P = 128
B, S, D = 4, 512, 256
T = B * S
TT = T // P
TS = S // P
DC = D // P
ROT = D // 2
NH, NKV, HD = 32, 8, 64
GR = NH // NKV
QG = GR * HD
E, F, TOPK = 8, 1024, 2
FC = F // P
EPS = 1e-5
BLK = 256
BH = BLK // P
NBLK = (TOPK * T + E * (BLK - 1)) // BLK
SLOTS = NBLK * BLK
NEG = -1e30
NORMS = 3


def layer_one(nc, dram, keep):
    with ExitStack() as ctx:
        def sb(name, shape, dt=F32):
            return ctx.enter_context(nc.sbuf_tensor(name, shape, dt))

        def sem(name):
            return ctx.enter_context(nc.semaphore(name))

        winT = sb("winT", [P, DC, 3 * D])
        wswT = sb("wswT", [P, DC, ROT])
        woutT = sb("woutT", [P, DC, D])
        kvbias = sb("kvbias", [P, 2 * D])
        outbias = sb("outbias", [P, D])
        qbias = sb("qbias", [P, 3])
        ln1 = sb("ln1", [P, DC])
        cos_tok = sb("cos_tok", [P, TS, ROT])
        sin_tok = sb("sin_tok", [P, TS, ROT])
        cos_ch = sb("cos_ch", [ROT, S])
        sin_ch = sb("sin_ch", [ROT, S])
        ident = keep["ident"]
        x = sb("x", [P, TS, D])
        xres = sb("xres", [P, TS, D])
        zc = sb("zc", [P, TS, D])
        stats = sb("stats", [P, TS, 6])
        mean = sb("mean", [P, TS])
        apart = sb("apart", [P, TS])
        spread = sb("spread", [P, TS])
        rstd = sb("rstd", [P, TS])
        xn = sb("xn", [P, TS, D])
        xnb = sb("xnb", [P, TS, D])
        xnT = sb("xnT", [P, DC, S])
        kv = sb("kv", [P, TS, 2 * D])
        kswap = sb("kswap", [P, TS, ROT])
        square = sb("square", [P, TS, D])
        ksum = sb("ksum", [P, TS])
        rnorm = sb("rnorm", [P, TS])
        kvprod = sb("kvprod", [P, TS, D])
        q0 = sb("q0", [P, S])
        qsw = sb("qsw", [P, S])
        qT = sb("qT", [P, DC, S])
        state = sb("state", [P, DC])
        wstate = sb("wstate", [P, DC, D])
        y = sb("y", [P, TS, D])
        root = sb("root", [P, TS])
        knorm = sb("knorm", [P, TS])
        zroot = sb("zroot", [P, TS])
        zscale = sb("zscale", [P, TS])
        zsum = sb("zsum", [P, TS])
        zn = sb("zn", [P, TS, D])
        zeros = sb("zeros", [P, 8 * D])
        ps = ctx.enter_context(nc.psum_tensor("ps1", [P, 8, 512], F32))

        x_loaded = sem("x_loaded")
        xres_loaded = sem("xres_loaded")
        x_taken = sem("x_taken")
        kept = sem("kept")
        y_added = sem("y_added")
        y_normalised = sem("y_normalised")
        weights_loaded = sem("weights_loaded")
        zeroed = sem("zeroed")
        eps_set = sem("eps_set")
        slots_zero = sem("slots_zero")
        project_step = sem("project_step")
        finish_step = sem("finish_step")
        gp_step = sem("gp_step")
        xn_ready = sem("xn_ready")
        xnT_in_psum = sem("xnT_in_psum")
        xnT_ready = sem("xnT_ready")
        kv_in_psum = sem("kv_in_psum")
        kv_taken = sem("kv_taken")
        q_in_psum = sem("q_in_psum")
        q_biased = sem("q_biased")
        qT_ready = sem("qT_ready")
        k_rotated = sem("k_rotated")
        var_ready = sem("var_ready")
        root_ready = sem("root_ready")
        ksquares = sem("ksquares")
        zsquares = sem("zsquares")
        ksum_ready = sem("ksum_ready")
        kvprod_ready = sem("kvprod_ready")
        rnorm_ready = sem("rnorm_ready")
        state_in_psum = sem("state_in_psum")
        wstate_ready = sem("wstate_ready")
        y_in_psum = sem("y_in_psum")
        xnb_ready = sem("xnb_ready")
        z_ready = sem("z_ready")
        zsum_ready = sem("zsum_ready")
        zn_ready = sem("zn_ready")
        znT_in_psum = sem("znT_in_psum")
        hT_done = sem("hT_done")

        block = ctx.enter_context(nc.Block())

        T_BANK, Q_BANK, KV_BANK, Y_BANK, STATE_BANK = 0, (2, 7, 6), 3, 6, 6

        def over_sequences(eng, step):
            step(None, 0)
            with eng.Fori(0, B - 1) as b:
                step(b, b + 1)
            step(B - 1, None)

        @block.sync
        def _(sp):
            xd = dram["x"].rearrange("b (t p) d -> b p t d", p=P)
            sp.dma_start(x[:], xd[0]).then_inc(x_loaded, 16)
            loads = [
                (winT[:], dram["winT"].rearrange("(c p) n -> p c n", p=P)),
                (wswT[:], dram["wswT"].rearrange("(c p) n -> p c n", p=P)),
                (woutT[:], dram["woutT"].rearrange("(c p) n -> p c n", p=P)),
                (kvbias[:], dram["b_in"][:, D:3 * D].to_broadcast([P, 2 * D])),
                (outbias[:], dram["b_out"].to_broadcast([P, D])),
                (qbias[:], dram["qbias"]),
                (ln1[:], dram["ln1"]),
                (cos_tok[:], dram["cos_tok"].rearrange("(t p) n -> p t n", p=P)),
                (sin_tok[:], dram["sin_tok"].rearrange("(t p) n -> p t n", p=P)),
                (cos_ch[:], dram["cos_ch"]),
                (sin_ch[:], dram["sin_ch"]),
                (ident[:], dram["ident"]),
            ]
            for dst, src in loads:
                sp.dma_start(dst, src).then_inc(weights_loaded, 16)
            sp.dma_start(xres[:], xd[0]).then_inc(xres_loaded, 16)
            sp.wait_ge(zeroed, 1)
            fill = dram["slot_rows"].rearrange("(n p) d -> p n d", p=P)
            rows = SLOTS // P
            fills = 0
            for n in range(0, rows, 8):
                k = min(8, rows - n)
                sp.dma_start(fill[:, n:n + k, :], zeros[:, 0:k * D].rearrange("p (n d) -> p n d", d=D)).then_inc(slots_zero, 16)
                fills += 1
            with sp.Fori(1, B) as b:
                rows = xd[bass.ds(b, 1)].rearrange("o p t d -> (o p) t d")
                sp.wait_ge(xn_ready, b)
                sp.dma_start(x[:], rows).then_inc(x_loaded, 16)
                sp.wait_ge(x_taken, b)
                sp.dma_start(xres[:], rows).then_inc(xres_loaded, 16)
            sp.wait_ge(slots_zero, 16 * fills)
        n_loads = 12

        @block.tensor
        def _(pe):
            pe.wait_ge(weights_loaded, 16 * n_loads)

            def step(b, a):
                if b is not None:
                    pe.wait_ge(kvprod_ready, b + 1)
                    pe.wait_ge(rnorm_ready, b + 1)
                    pe.wait_ge(q_biased, b + 1)
                    for m in range(DC):
                        for t in range(TS):
                            last = pe.matmul(ps[:, STATE_BANK, m:m + 1], kvprod[:, t, m * P:(m + 1) * P], rnorm[:, t:t + 1],
                                             start=(t == 0), stop=(t == TS - 1))
                    last.then_inc(state_in_psum, 1)
                if a is not None:
                    pe.wait_ge(xn_ready, a + 1)
                    for c in range(DC):
                        for t in range(TS):
                            last = pe.transpose(ps[:, T_BANK + c, t * P:(t + 1) * P], xn[:, t, c * P:(c + 1) * P], ident[:])
                    last.then_inc(xnT_in_psum, 1)
                if b is not None:
                    pe.wait_ge(wstate_ready, b + 1)
                    pe.wait_ge(qT_ready, b * 2 + 2)
                    for t in range(TS):
                        for m in range(DC):
                            last = pe.matmul(ps[:, Y_BANK + t // 2, (t % 2) * D:(t % 2 + 1) * D], qT[:, m, t * P:(t + 1) * P],
                                             wstate[:, m, :], start=(m == 0), stop=(m == DC - 1))
                    last.then_inc(y_in_psum, 1)
                if a is not None:
                    pe.wait_ge(xnT_ready, a + 1)
                    for t in range(TS):
                        if t >= 3:
                            pe.wait_ge(kv_taken, a * TS + t - 2)
                        for c in range(DC):
                            last = pe.matmul(ps[:, KV_BANK + t % 3, :], xnT[:, c, t * P:(t + 1) * P], winT[:, c, D:3 * D],
                                             start=(c == 0), stop=(c == DC - 1))
                        last.then_inc(kv_in_psum, 1)
                if b is not None:
                    pe.wait_ge(zn_ready, b + 1)
                    for c in range(DC):
                        for t in range(TS):
                            last = pe.transpose(ps[:, T_BANK + c, t * P:(t + 1) * P], zn[:, t, c * P:(c + 1) * P], ident[:])
                    last.then_inc(znT_in_psum, 1)
                if a is not None:
                    if b is not None:
                        pe.wait_ge(y_added, b + 1)
                    for m in range(DC + 1):
                        for c in range(DC):
                            w = winT[:, c, m * P:(m + 1) * P] if m < DC else wswT[:, c, :]
                            last = pe.matmul(ps[:, Q_BANK[m], :], w, xnT[:, c, :], start=(c == 0), stop=(c == DC - 1))
                    last.then_inc(q_in_psum, 1)

            over_sequences(pe, step)

        @block.scalar
        def _(act):
            act.wait_ge(weights_loaded, 16 * n_loads)
            act.wait_ge(eps_set, 1)

            def step(b, a):
                def deviation(n):
                    act.wait_ge(var_ready, n)
                    act.activation(root[:], spread[:], ACT.Sqrt, bias=keep["eps"][:, 0:1], scale=1.0 / D).then_inc(root_ready, 1)

                if a is not None:
                    deviation(1 if b is None else b * NORMS + 2)
                    act.wait_ge(xnT_in_psum, a + 1)
                    for c in range(DC):
                        last = act.copy(xnT[:, c, :], ps[:, T_BANK + c, :])
                    last.then_inc(xnT_ready, 1)
                if b is not None:
                    first = b * NORMS + (2 if a is None else 3)
                    deviation(first)
                    deviation(first + 1)
                    act.wait_ge(z_ready, b + 1)
                    for t in range(TS):
                        last = act.activation(square[:, t, :], zc[:, t, :], ACT.Square, accum_out=zsum[:, t:t + 1])
                    last.then_inc(zsquares, 1)
                    act.wait_ge(zsquares, b + 1)
                    act.activation(zroot[:], zsum[:], ACT.Sqrt, bias=keep["eps"][:, 0:1], scale=1.0 / D).then_inc(zsum_ready, 1)
                if a is not None:
                    act.wait_ge(k_rotated, a + 1)
                    for t in range(TS):
                        last = act.activation(square[:, t, :], kv[:, t, 0:D], ACT.Square, accum_out=ksum[:, t:t + 1])
                    last.then_inc(ksquares, 1)
                    act.wait_ge(ksquares, a + 1)
                    act.activation(knorm[:], ksum[:], ACT.Sqrt).then_inc(ksum_ready, 1)
                if b is not None:
                    act.wait_ge(znT_in_psum, b + 1)
                    for c in range(DC):
                        last = act.activation(keep["hT"][:, c, bass.ds(b * S, S)], ps[:, T_BANK + c, :], ACT.Copy, scale=ln1[:, c:c + 1])
                    last.then_inc(hT_done, 1)
                if a is not None:
                    if b is not None:
                        act.wait_ge(y_in_psum, b + 1)
                    act.wait_ge(q_in_psum, a + 1)
                    act.activation(q0[:], ps[:, Q_BANK[0], :], ACT.Identity, bias=qbias[:, 0:1])
                    act.activation(qsw[:], ps[:, Q_BANK[2], :], ACT.Identity, bias=qbias[:, 2:3]).then_inc(q_biased, 1)
                    act.activation(qT[:, 1, :], ps[:, Q_BANK[1], :], ACT.Identity, bias=qbias[:, 1:2]).then_inc(qT_ready, 1)

            over_sequences(act, step)

        @block.gpsimd
        def _(pool):
            pool.memset(zeros[:], 0.0).then_inc(zeroed, 1)
            pool.memset(keep["eps"][:], EPS).then_inc(eps_set, 1)
            pool.sem_inc(kept, 1)
            pool.wait_ge(weights_loaded, 16 * n_loads)

            def step(b, a):
                if a is not None:
                    pool.wait_ge(xn_ready, a + 1)
                    if b is not None:
                        pool.wait_ge(y_added, b + 1)
                    for t in range(TS):
                        last = pool.tensor_tensor(xnb[:, t, :], xn[:, t, :], outbias[:], ALU.add)
                    last.then_inc(xnb_ready, 1)
                if b is not None:
                    tiles = bass.ds(b * TS, TS)
                    pool.wait_ge(x_taken, b + 1)
                    pool.tensor_copy(keep["x1"][:, tiles, :], y[:])
                    pool.wait_ge(z_ready, b + 1)
                    pool.tensor_copy(keep["z"][:, tiles, :], zc[:]).then_inc(kept, 1)
                if a is not None:
                    pool.wait_ge(q_biased, a + 1)
                    pool.tensor_tensor(q0[:], q0[:], cos_ch[:], ALU.mult)
                    pool.tensor_tensor(qsw[:], qsw[:], sin_ch[:], ALU.mult).then_inc(gp_step, 1)
                    pool.wait_ge(gp_step, a + 1)
                    pool.tensor_tensor(qT[:, 0, :], q0[:], qsw[:], ALU.add).then_inc(qT_ready, 1)

            over_sequences(pool, step)

        @block.vector
        def _(dve):
            PROJECT, FINISH = 7, 10
            dve.wait_ge(weights_loaded, 16 * n_loads)

            def step(b, a):
                links = {project_step: 0, finish_step: 0}
                which, norm = [None], [0]
                norms_before = 0 if b is None else b * NORMS + 1

                def link(ins):
                    sequence, count = (a, PROJECT) if which[0] is project_step else (b, FINISH)
                    links[which[0]] += 1
                    ins.then_inc(which[0], 1)
                    dve.wait_ge(which[0], sequence * count + links[which[0]])

                def moments(rows):
                    for t in range(TS):
                        last = dve.bn_stats(stats[:, t, :], rows[:, t, :])
                    link(last)
                    dve.tensor_tensor(mean[:], stats[:, :, 1], stats[:, :, 4], ALU.add)
                    dve.tensor_tensor(apart[:], stats[:, :, 1], stats[:, :, 4], ALU.subtract)
                    link(dve.tensor_tensor(spread[:], stats[:, :, 2], stats[:, :, 5], ALU.add))
                    dve.tensor_scalar(mean[:], mean[:], 0.5, None, ALU.mult)
                    link(dve.tensor_tensor(apart[:], apart[:], apart[:], ALU.mult))
                    dve.scalar_tensor_tensor(spread[:], apart[:], D / 4.0, spread[:], ALU.mult, ALU.add).then_inc(var_ready, 1)
                    norm[0] += 1
                    dve.wait_ge(root_ready, norms_before + norm[0])
                    link(dve.reciprocal(rstd[:], root[:]))

                def normalised(out, rows, done):
                    for t in range(TS):
                        last = dve.tensor_scalar(out[:, t, :], rows[:, t, :], mean[:, t:t + 1], rstd[:, t:t + 1], ALU.subtract, ALU.mult)
                    last.then_inc(done, 1)

                def take_kv(t):
                    if a is not None:
                        dve.wait_ge(kv_in_psum, a * TS + t + 1)
                        dve.tensor_tensor(kv[:, t, :], ps[:, KV_BANK + t % 3, :], kvbias[:], ALU.add).then_inc(kv_taken, 1)

                if a is not None:
                    which[0] = project_step
                    dve.wait_ge(x_loaded, a * 16 + 16)
                    moments(x)
                    if b is not None:
                        dve.wait_ge(xnb_ready, b + 1)
                    normalised(xn, x, xn_ready)
                if b is not None:
                    which[0] = finish_step
                    dve.wait_ge(state_in_psum, b + 1)
                    link(dve.tensor_copy(state[:], ps[:, STATE_BANK, 0:DC]))
                    for m in range(DC):
                        last = dve.tensor_scalar(wstate[:, m, :], woutT[:, m, :], state[:, m:m + 1], None, ALU.mult)
                    last.then_inc(wstate_ready, 1)
                    dve.wait_ge(kept, b + 1)
                    dve.wait_ge(xnb_ready, b + 1)
                    dve.wait_ge(y_in_psum, b + 1)
                    for c in range(TS // 2):
                        last = dve.tensor_tensor(y[:, 2 * c:2 * c + 2, :], ps[:, Y_BANK + c, :].rearrange("p (t d) -> p t d", d=D),
                                                 xnb[:, 2 * c:2 * c + 2, :], ALU.add)
                    last.then_inc(y_added, 1)
                    dve.wait_ge(y_added, b + 1)
                    moments(y)
                    normalised(y, y, y_normalised)
                take_kv(0)
                if b is not None:
                    dve.wait_ge(y_normalised, b + 1)
                    dve.wait_ge(xres_loaded, b * 16 + 16)
                    dve.tensor_tensor(y[:], y[:], xres[:], ALU.add).then_inc(x_taken, 1)
                    dve.wait_ge(x_taken, b + 1)
                    moments(y)
                    normalised(zc, y, z_ready)
                take_kv(1)
                take_kv(2)
                if b is not None:
                    dve.wait_ge(zsum_ready, b + 1)
                    link(dve.reciprocal(zscale[:], zroot[:]))
                    dve.wait_ge(z_ready, b + 1)
                    for t in range(TS):
                        last = dve.tensor_scalar(zn[:, t, :], zc[:, t, :], zscale[:, t:t + 1], None, ALU.mult)
                    last.then_inc(zn_ready, 1)
                    assert links[finish_step] == FINISH
                take_kv(3)
                if a is not None:
                    which[0] = project_step
                    dve.wait_ge(kv_taken, a * TS + TS)
                    k = kv[:, :, 0:ROT]
                    for s in range(2):
                        last = dve.tensor_tensor(kswap[:, :, s:ROT:2], k[:, :, 1 - s:ROT:2], sin_tok[:, :, s:ROT:2], ALU.mult)
                    link(last)
                    link(dve.tensor_tensor(k, k, cos_tok[:], ALU.mult))
                    dve.tensor_tensor(k, k, kswap[:], ALU.add).then_inc(k_rotated, 1)
                    dve.wait_ge(k_rotated, a + 1)
                    dve.tensor_tensor(kvprod[:], kv[:, :, 0:D], kv[:, :, D:2 * D], ALU.mult).then_inc(kvprod_ready, 1)
                    dve.wait_ge(ksum_ready, a + 1)
                    link(dve.tensor_scalar(rnorm[:], knorm[:], 1e-12, None, ALU.max))
                    dve.reciprocal(rnorm[:], rnorm[:]).then_inc(rnorm_ready, 1)
                    assert links[project_step] == PROJECT

            over_sequences(dve, step)
            dve.wait_ge(hT_done, B)
            dve.wait_ge(kept, B + 1)


def attention(nc, dram, keep):
    UNITS = TS
    TURNS = UNITS * (UNITS + 1) // 2
    KT = NH * HD // P
    PAIRS = NKV // 2
    with ExitStack() as ctx:
        def sb(name, shape, dt=F32):
            return ctx.enter_context(nc.sbuf_tensor(name, shape, dt))

        def sem(name):
            return ctx.enter_context(nc.semaphore(name))

        wq = sb("wq", [P, 2, DC, QG])
        wkv = sb("wkv", [P, 2, DC, 2 * HD])
        wo = sb("wo", [P, KT, D])
        causal = sb("causal", [P, S])
        qT = sb("qTg", [P, 2, 2, S])
        kT = sb("kTg", [P, 2, S])
        vT = sb("vTg", [P, S])
        v = sb("vg", [P, 2, TS, HD])
        probs = sb("probs", [P, 2, GR, S])
        shift = sb("shift", [P, 2, GR])
        total = sb("total", [P, 2, GR])
        inverse = sb("inverse", [P, 2, GR])
        probsT = sb("probsT", [P, 4, GR * P])
        outT = sb("outT", [P, KT, S])
        ident = keep["ident"]
        ps = ctx.enter_context(nc.psum_tensor("ps2", [P, 8, 512], F32))
        SCORES, TURN, MIX, PROJ = 0, 4, 6, 7

        consts_loaded = sem("consts_loaded")
        w_loaded = [sem("w_loaded0"), sem("w_loaded1")]
        proj_in_psum = sem("proj_in_psum")
        proj_taken = sem("proj_taken")
        scores_in_psum = sem("scores_in_psum")
        shift_ready = sem("shift_ready")
        exp_done = sem("exp_done")
        probs_ready = sem("probs_ready")
        turned_in_psum = sem("turned_in_psum")
        turned_taken = [sem("turned_by_dve"), sem("turned_by_act")]
        mixed_in_psum = sem("mixed_in_psum")
        mixed_taken = sem("mixed_taken")
        rows_in_psum = sem("rows_in_psum")
        rows_added = sem("rows_added")
        dve_step = sem("dve_step2")
        dve_passed = sem("dve_passed")
        pe_passed = sem("pe_passed")

        block = ctx.enter_context(nc.Block())

        WIDTH = [4, 3, 2, 1]
        FIRST = [0, 4, 7, 9]
        AGENDA = [
            ["turn 0", "turn 1", "score 0", "mix 0", "project 1", "turn 2", "score 1", "turn 3", "score 2", "mix 1", "score 3",
             "project 2", "mix 2", "mix 3"],
            ["turn 0", "turn 1", "score 0", "score 1", "turn 2", "mix 0", "score 2", "score 3", "project 3", "mix 1", "mix 2"],
            ["turn 0", "turn 1", "score 0", "score 1", "score 2", "score 3", "mix 0", "mix 1"],
            ["turn 0", "score 0", "score 1", "score 2", "score 3", "project 0", "mix 0"],
        ]

        def steps(u, nxt, following, behind=0):
            todo = [(what, int(n)) for what, n in (step.split() for step in AGENDA[u])]
            late = [(at + (behind if step[0] == "score" else 0), at, step) for at, step in enumerate(todo)]
            for _, _, (what, n) in sorted(late):
                if not (what == "score" and not nxt or what == "project" and not following):
                    yield what, n

        def over_sequences(eng, first, unit, end):
            def group(turn, pair, par, more, ahead=True):
                it, g = turn * 2 + par, pair * 2 + par
                following = (turn, 1) if par == 0 else (turn + 1, 0)
                for u in range(UNITS):
                    if u + 1 < UNITS:
                        unit(it, g, par, u, (turn, par, u + 1), following if more else None)
                    else:
                        unit(it, g, par, u, (*following, 0) if more else None, (turn + 1, par) if ahead else None)

            first((0, 0), (0, 1))
            with eng.Fori(0, B - 1) as b:
                with eng.Fori(0, PAIRS) as pair:
                    turn = eng.snap(b * PAIRS + pair)
                    group(turn, pair, 0, True)
                    group(turn, pair, 1, True)
                end(b)
            b = B - 1
            with eng.Fori(0, PAIRS - 1) as pair:
                turn = eng.snap(pair + b * PAIRS)
                group(turn, pair, 0, True)
                group(turn, pair, 1, True)
            pair = PAIRS - 1
            group(b * PAIRS + pair, pair, 0, True, False)
            group(b * PAIRS + pair, pair, 1, False, False)
            end(b)

        @block.sync
        def _(sp):
            sp.dma_start(wo[:], dram["wo"].rearrange("(k p) n -> p k n", p=P)).then_inc(consts_loaded, 16)
            sp.dma_start(causal[:], dram["causal"]).then_inc(consts_loaded, 16)
            wqd = dram["wq"].rearrange("g (c p) n -> g p c n", p=P)
            wkvd = dram["wkv"].rearrange("g (c p) n -> g p c n", p=P)
            with sp.Fori(0, B) as b:
                with sp.Fori(0, NKV // 2) as pair:
                    for par in range(2):
                        sp.wait_ge(proj_in_psum, (b * NKV + pair * 2 + par) * 4 + 4)
                        g = bass.ds(pair * 2 + par, 1)
                        sp.dma_start(wq[:, par], wqd[g].rearrange("o p c n -> (o p) c n")).then_inc(w_loaded[par], 16)
                        sp.dma_start(wkv[:, par], wkvd[g].rearrange("o p c n -> (o p) c n")).then_inc(w_loaded[par], 16)

        @block.tensor
        def _(pe):
            pe.sem_inc(proj_in_psum, 8)
            pe.wait_ge(consts_loaded, 32)

            def project(turn, par, part):
                it, b = turn * 2 + par, turn // PAIRS
                if part == 0:
                    pe.wait_ge(w_loaded[par], turn * 32 + 32)
                pe.wait_ge(proj_taken, it * 4 + part + 1)
                if part == 1:
                    pe.sem_inc(pe_passed, 1)
                    for t in range(TS):
                        last = pe.transpose(ps[:, PROJ, t * HD:(t + 1) * HD], vT[HD:2 * HD, t * P:(t + 1) * P],
                                            ident[HD:2 * HD, HD:2 * HD])
                else:
                    for c in range(DC):
                        w = wkv[:, par, c, :] if part == 0 else wq[:, par, c, (part - 2) * P:(part - 1) * P]
                        last = pe.matmul(ps[:, PROJ, :], w, keep["hT"][:, c, bass.ds(b * S, S)], start=(c == 0), stop=(c == DC - 1))
                last.then_inc(proj_in_psum, 1)

            def score(turn, par, u, h):
                it, n, i = turn * 2 + par, WIDTH[u] * P, WIDTH[u] - 1
                if u == 0 and h == 0:
                    pe.wait_ge(proj_taken, it * 4 + 5)
                half = slice(h % 2 * HD, h % 2 * HD + HD)
                pe.wait_ge(exp_done, (it * UNITS + u) * GR + h + 1)
                pe.matmul(ps[:, SCORES + h, 0:n], qT[half, par, h // 2, i * P:(i + 1) * P], kT[half, par, 0:n],
                          start=True, stop=True).then_inc(scores_in_psum, 1)

            def first(group, second):
                for part in range(4):
                    project(*group, part)
                project(*second, 0)
                for h in range(GR):
                    score(*group, 0, h)

            def unit(it, g, par, u, nxt, following):
                if u == 0:
                    pe.wait_ge(rows_added, (it // NKV) + 1)
                for what, j in steps(u, nxt, following):
                    n = FIRST[u] + j
                    if what == "turn":
                        pe.wait_ge(turned_taken[n % 2], it * (TURNS // 2) + n // 2 + 1)
                        for h in range(GR):
                            if j == 0:
                                pe.wait_ge(probs_ready, (it * UNITS + u) * GR + h + 1)
                            last = pe.transpose(ps[:, TURN + n % 2, h * P:(h + 1) * P], probs[:, u % 2, h, j * P:(j + 1) * P], ident[:])
                        last.then_inc(turned_in_psum, 1)
                    elif what == "mix":
                        pe.wait_ge(turned_taken[n % 2], it * (TURNS // 2) + n // 2 + 2)
                        if j == 0:
                            pe.wait_ge(mixed_taken, it * UNITS + u + 1)
                        heads = probsT[:, (n + 2 * par) % 4, :].rearrange("p (m a q) -> p a m q", a=2, q=P)
                        for a in range(2):
                            last = pe.matmul(ps[a * HD:(a + 1) * HD, MIX, 0:2 * P].rearrange("p (m q) -> p m q", q=P),
                                             v[:, par, j, :], heads[:, a], start=(j == 0), stop=(j == WIDTH[u] - 1))
                        if j == WIDTH[u] - 1:
                            last.then_inc(mixed_in_psum, 1)
                    elif what == "score":
                        score(*nxt, j)
                    else:
                        project(*following, j)

            def end(b):
                pe.wait_ge(mixed_taken, (b + 1) * (NKV * UNITS) + 1)
                pe.wait_ge(turned_taken[0], (b + 1) * (NKV * TURNS // 2) + 1)
                pe.wait_ge(turned_taken[1], (b + 1) * (NKV * TURNS // 2) + 1)
                for t in range(TS):
                    for k in range(KT):
                        last = pe.matmul(ps[:, TURN + t // 2, t % 2 * D:(t % 2 + 1) * D], outT[:, k, t * P:(t + 1) * P], wo[:, k, :],
                                         start=(k == 0), stop=(k == KT - 1))
                    if t % 2:
                        last.then_inc(rows_in_psum, 1)

            over_sequences(pe, first, unit, end)

        @block.scalar
        def _(act):
            act.sem_inc(proj_taken, 1)
            act.sem_inc(exp_done, GR)
            act.sem_inc(turned_taken[1], 1)
            act.sem_inc(mixed_taken, 1)

            def take(turn, par, part):
                act.wait_ge(proj_in_psum, (turn * 2 + par) * 4 + part + 9)
                if part == 0:
                    act.copy(kT[0:HD, par, :], ps[0:HD, PROJ, :])
                    act.copy(kT[HD:2 * HD, par, :], ps[0:HD, PROJ, :])
                    last = act.copy(vT[HD:2 * HD, :], ps[HD:2 * HD, PROJ, :])
                elif part == 1:
                    last = act.copy(v[:, par, :, :], ps[:, PROJ, 0:TS * HD].rearrange("p (t d) -> p t d", d=HD))
                else:
                    last = act.copy(qT[:, par, part - 2, :], ps[:, PROJ, :])
                last.then_inc(proj_taken, 1)

            def exponential(turn, par, u, h):
                n = WIDTH[u] * P
                act.wait_ge(shift_ready, ((turn * 2 + par) * UNITS + u) * GR + h + 1)
                act.activation(probs[:, u % 2, h, 0:n], ps[:, SCORES + h, 0:n], ACT.Exp, bias=shift[:, u % 2, h:h + 1],
                               scale=-1.0, accum_out=total[:, u % 2, h:h + 1]).then_inc(exp_done, 1)

            def first(group, second):
                for part in range(4):
                    take(*group, part)
                take(*second, 0)
                for h in range(GR):
                    exponential(*group, 0, h)

            def unit(it, g, par, u, nxt, following):
                for what, j in steps(u, nxt, following, behind=1):
                    n = FIRST[u] + j
                    if what == "turn" and n % 2:
                        act.wait_ge(turned_in_psum, it * TURNS + n + 1)
                        act.copy(probsT[:, (n + 2 * par) % 4, :], ps[:, TURN + 1, :]).then_inc(turned_taken[1], 1)
                    elif what == "score":
                        exponential(*nxt, j)
                    elif what == "project":
                        take(*following, j)
                i = WIDTH[u] - 1
                act.wait_ge(mixed_in_psum, it * UNITS + u + 1)
                act.copy(outT[:, bass.ds(g * 2, 2), i * P:(i + 1) * P],
                         ps[:, MIX, 0:2 * P].rearrange("p (m q) -> p m q", q=P)).then_inc(mixed_taken, 1)

            over_sequences(act, first, unit, lambda b: None)

        @block.vector
        def _(dve):
            dve.sem_inc(turned_taken[0], 1)
            dve.sem_inc(rows_added, 1)
            dve.wait_ge(consts_loaded, 32)

            def largest(turn, par, u, h):
                n = WIDTH[u] * P
                dve.wait_ge(scores_in_psum, ((turn * 2 + par) * UNITS + u) * GR + h + 1)
                dve.sem_inc(dve_passed, 1)
                bank = ps[:, SCORES + h, 0:n]
                dve.tensor_tensor_reduce(bank, bank, causal[:, S - n:S], -float(HD) ** -0.5, -NEG, ALU.add, ALU.min,
                                         shift[:, u % 2, h:h + 1]).then_inc(shift_ready, 1)

            def first(group, second):
                for h in range(GR):
                    largest(*group, 0, h)

            def unit(it, g, par, u, nxt, following):
                n = WIDTH[u] * P
                for h in range(0, GR, 2):
                    dve.wait_ge(exp_done, (it * UNITS + u) * GR + GR + h + 2)
                    dve.reciprocal(inverse[:, u % 2, h:h + 2], total[:, u % 2, h:h + 2]).then_inc(dve_step, 1)
                    dve.wait_ge(dve_step, (it * UNITS + u) * 2 + h // 2 + 1)
                    for k in range(h, h + 2):
                        dve.tensor_scalar(probs[:, u % 2, k, 0:n], probs[:, u % 2, k, 0:n], inverse[:, u % 2, k:k + 1],
                                          None, ALU.mult).then_inc(probs_ready, 1)
                for what, j in steps(u, nxt, following):
                    n = FIRST[u] + j
                    if what == "score":
                        largest(*nxt, j)
                    elif what == "turn" and n % 2 == 0:
                        dve.wait_ge(turned_in_psum, it * TURNS + n + 1)
                        dve.tensor_copy(probsT[:, (n + 2 * par) % 4, :], ps[:, TURN, :]).then_inc(turned_taken[0], 1)

            def end(b):
                for k in range(2):
                    dve.wait_ge(rows_in_psum, b * 2 + k + 1)
                    rows = keep["z"][:, bass.ds(b * TS + 2 * k, 2), :]
                    last = dve.tensor_tensor(rows, rows, ps[:, TURN + k, :].rearrange("p (t d) -> p t d", d=D), ALU.add)
                last.then_inc(rows_added, 1)

            over_sequences(dve, first, unit, end)


def route(nc, dram, keep):
    ROUND = 4
    with ExitStack() as ctx:
        def sb(name, shape, dt=F32):
            return ctx.enter_context(nc.sbuf_tensor(name, shape, dt))

        def sem(name):
            return ctx.enter_context(nc.semaphore(name))

        ln2 = sb("ln2", [P, D])
        gate = sb("gate", [P, DC, E])
        before = sb("before", [P, P])
        ones = sb("ones", [P, P])
        expert_ids = sb("expert_ids", [P, E])
        block_ids = sb("block_ids", [P, NBLK])
        square = sb("square3", [P, TT, D])
        meansq = sb("meansq", [P, TT])
        root = sb("root3", [P, TT])
        scale = sb("scale3", [P, TT])
        t_rows = sb("t_rows", [P, TT, D])
        tT = sb("tT", [P, 2, DC, ROUND * P])
        logits = sb("logits", [P, TT, E])
        largest = sb("largest", [P, TT])
        odds = sb("odds", [P, TT, E])
        odds_sum = sb("odds_sum", [P, TT])
        prob = sb("prob", [P, TT, E])
        best = sb("best", [P, TT, 8])
        best_at = sb("best_at", [P, TT, 8], U32)
        best_id = sb("best_id", [P, TT, TOPK])
        pair_sum = sb("pair_sum", [P, TT])
        chosen = [sb(f"chosen{k}", [P, TT, E]) for k in range(TOPK)]
        member = sb("member", [P, TT, E])
        count = sb("count", [P, TT + 1, E])
        nblocks_i = sb("nblocks_i", [P, E], I32)
        nblocks = sb("nblocks", [P, E])
        blocks_end = sb("blocks_end", [P, E])
        first_slot = sb("first_slot", [P, E])
        slot = sb("slot", [P, TT, E])
        picked = [sb(f"picked{k}", [P, TT, E]) for k in range(TOPK)]
        slot_k = sb("slot_k", [P, TOPK, TT])
        past = sb("past", [P, NBLK, E])
        owner = sb("owner", [P, NBLK])
        ps = ctx.enter_context(nc.psum_tensor("ps3", [P, 8, 512], F32))
        LOGITS, BEFORE, TOTAL = 4, 5, 6

        loaded = sem("loaded3")
        ones_set = sem("ones_set")
        square_sum = sem("square_sum")
        root_ready = sem("root_ready3")
        t_ready = sem("t_ready")
        turned = sem("turned3")
        turned_taken = sem("turned_taken3")
        logits_in_psum = sem("logits_in_psum")
        shifted = sem("shifted")
        odds_ready = sem("odds_ready")
        member_ready = sem("member_ready")
        counted = sem("counted")
        slots_ready = sem("slots_ready")
        scattered = sem("scattered")
        dve_step = sem("dve_step3")

        block = ctx.enter_context(nc.Block())
        loads = [(ln2[:], dram["ln2"].to_broadcast([P, D])), (gate[:], dram["gate_w"].rearrange("(c p) e -> p c e", p=P)),
                 (before[:], dram["before"]), (expert_ids[:], dram["expert_ids"]), (block_ids[:], dram["block_ids"])]

        @block.sync
        def _(sp):
            for dst, src in loads:
                sp.dma_start(dst, src).then_inc(loaded, 16)

        @block.scalar
        def _(act):
            for t in range(TT):
                last = act.activation(square[:, t, :], keep["z"][:, t, :], ACT.Square, accum_out=meansq[:, t:t + 1])
            last.then_inc(square_sum, 1)
            act.wait_ge(square_sum, 1)
            act.activation(root[:], meansq[:], ACT.Sqrt, bias=keep["eps"][:, 0:1], scale=1.0 / D).then_inc(root_ready, 1)
            for r in range(TT // ROUND):
                act.wait_ge(turned, r + 1)
                for c in range(DC):
                    last = act.copy(tT[:, r % 2, c, :], ps[:, r % 2 * DC + c, :])
                last.then_inc(turned_taken, 1)
            act.wait_ge(shifted, 1)
            act.activation(odds[:], odds[:], ACT.Exp).then_inc(odds_ready, 1)

        @block.tensor
        def _(pe):
            pe.wait_ge(loaded, 16 * len(loads))
            for r in range(TT // ROUND):
                pe.wait_ge(t_ready, (r + 1) * ROUND)
                if r >= 2:
                    pe.wait_ge(turned_taken, r - 1)
                for c in range(DC):
                    for t in range(ROUND):
                        last = pe.transpose(ps[:, r % 2 * DC + c, t * P:(t + 1) * P], t_rows[:, r * ROUND + t, c * P:(c + 1) * P],
                                            keep["ident"][:])
                last.then_inc(turned, 1)
                pe.wait_ge(turned_taken, r + 1)
                for t in range(ROUND):
                    at = (r * ROUND + t) * E
                    for c in range(DC):
                        last = pe.matmul(ps[:, LOGITS, at:at + E], tT[:, r % 2, c, t * P:(t + 1) * P], gate[:, c, :],
                                         start=(c == 0), stop=(c == DC - 1))
            last.then_inc(logits_in_psum, 1)
            pe.wait_ge(ones_set, 1)
            pe.wait_ge(member_ready, 1)
            flat = member[:].rearrange("p t e -> p (t e)")
            pe.matmul(ps[:, BEFORE, 0:TT * E], before[:], flat, start=True, stop=True)
            pe.matmul(ps[:, TOTAL, 0:TT * E], ones[:], flat, start=True, stop=True).then_inc(counted, 1)

        @block.gpsimd
        def _(pool):
            pool.memset(ones[:], 1.0).then_inc(ones_set, 1)
            pool.wait_ge(slots_ready, 1)
            pool.wait_ge(t_ready, TT)
            for t in range(TT):
                for k in range(TOPK):
                    pool.indirect_dma_start(dram["slot_rows"], bass.IndirectOffsetOnAxis(keep["slots"][:, k, t:t + 1], 0),
                                            t_rows[:, t, :], None).then_inc(scattered, 16)
            pool.wait_ge(scattered, 16 * TT * TOPK)

        @block.vector
        def _(dve):
            done = [0]

            def link(ins):
                done[0] += 1
                ins.then_inc(dve_step, 1)
                dve.wait_ge(dve_step, done[0])

            dve.wait_ge(loaded, 16 * len(loads))
            dve.wait_ge(root_ready, 1)
            link(dve.reciprocal(scale[:], root[:]))
            for t in range(TT):
                dve.scalar_tensor_tensor(t_rows[:, t, :], keep["z"][:, t, :], scale[:, t:t + 1], ln2[:], ALU.mult, ALU.mult)\
                   .then_inc(t_ready, 1)
            dve.wait_ge(logits_in_psum, 1)
            link(dve.tensor_copy(logits[:].rearrange("p t e -> p (t e)"), ps[:, LOGITS, 0:TT * E]))
            link(dve.tensor_reduce(largest[:], logits[:], AX.X, ALU.max))
            dve.tensor_tensor(odds[:], logits[:], largest[:].unsqueeze(2).to_broadcast([P, TT, E]), ALU.subtract)\
               .then_inc(shifted, 1)
            dve.wait_ge(odds_ready, 1)
            link(dve.tensor_reduce(odds_sum[:], odds[:], AX.X, ALU.add))
            link(dve.reciprocal(odds_sum[:], odds_sum[:]))
            link(dve.tensor_tensor(prob[:], odds[:], odds_sum[:].unsqueeze(2).to_broadcast([P, TT, E]), ALU.mult))
            for t in range(TT):
                last = dve.max(best[:, t, :], prob[:, t, :])
            link(last)
            for t in range(TT):
                last = dve.max_index(best_at[:, t, :], best[:, t, :], prob[:, t, :])
            link(last)
            dve.tensor_copy(best_id[:], best_at[:, :, 0:TOPK])
            link(dve.tensor_tensor(pair_sum[:], best[:, :, 0], best[:, :, 1], ALU.add))
            link(dve.reciprocal(pair_sum[:], pair_sum[:]))
            dve.tensor_tensor(keep["shares"][:], best[:, :, 0:TOPK], pair_sum[:].unsqueeze(2).to_broadcast([P, TT, TOPK]), ALU.mult)
            ids = expert_ids[:].unsqueeze(1).to_broadcast([P, TT, E])
            for k in range(TOPK):
                last = dve.tensor_tensor(chosen[k][:], ids, best_id[:, :, k:k + 1].to_broadcast([P, TT, E]), ALU.is_equal)
            link(last)
            dve.tensor_tensor(member[:], chosen[0][:], chosen[1][:], ALU.add).then_inc(member_ready, 1)
            link(dve.memset(count[:, 0, :], 0.0))
            dve.wait_ge(counted, 1)
            for t in range(TT):
                link(dve.tensor_tensor(count[:, t + 1, :], count[:, t, :], ps[:, TOTAL, t * E:(t + 1) * E], ALU.add))
            link(dve.tensor_scalar(nblocks_i[:], count[:, TT, :], float(BLK - 1), None, ALU.add))
            link(dve.tensor_scalar(nblocks_i[:], nblocks_i[:], BLK.bit_length() - 1, None, ALU.arith_shift_right))
            link(dve.tensor_copy(nblocks[:], nblocks_i[:]))
            link(dve.tensor_copy(blocks_end[:, 0:1], nblocks[:, 0:1]))
            for e in range(1, E):
                link(dve.tensor_tensor(blocks_end[:, e:e + 1], blocks_end[:, e - 1:e], nblocks[:, e:e + 1], ALU.add))
            link(dve.tensor_tensor(first_slot[:], blocks_end[:], nblocks[:], ALU.subtract))
            link(dve.tensor_scalar(first_slot[:], first_slot[:], float(BLK), None, ALU.mult))
            link(dve.tensor_tensor(slot[:], count[:, 0:TT, :], first_slot[:].unsqueeze(1).to_broadcast([P, TT, E]), ALU.add))
            link(dve.tensor_tensor(slot[:], slot[:], ps[:, BEFORE, 0:TT * E].rearrange("p (t e) -> p t e", e=E), ALU.add))
            for k in range(TOPK):
                last = dve.tensor_tensor(picked[k][:], chosen[k][:], slot[:], ALU.mult)
            link(last)
            for k in range(TOPK):
                last = dve.tensor_reduce(slot_k[:, k, :], picked[k][:], AX.X, ALU.add)
            link(last)
            dve.tensor_copy(keep["slots"][:], slot_k[:]).then_inc(slots_ready, 1)
            link(dve.tensor_tensor(past[:], blocks_end[:].unsqueeze(1).to_broadcast([P, NBLK, E]),
                                   block_ids[:].unsqueeze(2).to_broadcast([P, NBLK, E]), ALU.is_le))
            link(dve.tensor_reduce(owner[:], past[:], AX.X, ALU.add))
            link(dve.tensor_scalar(keep["block_expert"][:], owner[:], float(E - 1), None, ALU.min))


def experts(nc, dram, keep):
    Q = FC // 2
    PASSES = ((0, 0), (1, 0), (0, 1))
    with ExitStack() as ctx:
        def sb(name, shape, dt=F32):
            return ctx.enter_context(nc.sbuf_tensor(name, shape, dt))

        def sem(name):
            return ctx.enter_context(nc.semaphore(name))

        W = {"w1": (DC, F), "w3": (DC, F), "w2": (FC, D)}
        raw = {x: sb(f"{x}_raw", [P, *W[x]]) for x in W}
        parts = {x: [sb(f"{x}_{n}", [P, 2, *W[x]], F32R) for n in ("high", "low")] for x in W}
        rows = sb("rows", [P, 2, BH, D])
        rowsT = [sb(f"rowsT_{n}", [P, 2, DC * BLK], F32R) for n in ("high", "low")]
        relu = sb("relu", [P, 2, 2, BLK])
        product = sb("product", [P, 2, 2, BLK])
        gatedT = [sb(f"gatedT_{n}", [P, FC, BLK], F32R) for n in ("high", "low")]
        result = sb("result", [P, 2, BH, D])
        ps = ctx.enter_context(nc.psum_tensor("ps4", [P, 8, 512], F32))
        TURN, DOWN, UP = 0, 2, 4

        raw_loaded = {x: sem(f"{x}_raw_loaded") for x in W}
        high_ready = {x: sem(f"{x}_high_ready") for x in W}
        split = {x: sem(f"{x}_split") for x in W}
        rows_loaded = [sem("rows_loaded0"), sem("rows_loaded1")]
        turned = sem("turned4")
        rowsT_high = sem("rowsT_high_ready")
        rowsT_split = sem("rowsT_split")
        up_in_psum = sem("up_in_psum")
        relu_ready = sem("relu_ready")
        product_ready = sem("product_ready")
        gated_high = sem("gated_high_ready")
        gated_split = sem("gated_split")
        down_in_psum = sem("down_in_psum")
        result_ready = sem("result_ready")
        stored = [sem("stored0"), sem("stored1")]

        passed = sem("passed4")

        block = ctx.enter_context(nc.Block())
        slot_rows = dram["slot_rows"].rearrange("(n h p) d -> n p h d", h=BH, p=P)
        expert_rows = dram["expert_rows"].rearrange("(n h p) d -> n p h d", h=BH, p=P)

        def one(ap):
            return ap.rearrange("o p c n -> (o p) c n")

        def over_blocks(eng, step):
            assert NBLK % 2 and NBLK >= 5
            step(0, 0, 0)
            with eng.Fori(0, (NBLK - 3) // 2) as pair:
                step(pair * 2 + 1, pair, 1)
                step(pair * 2 + 2, pair + 1, 0)
            step(NBLK - 2, NBLK // 2 - 1, 1)
            step(NBLK - 1, NBLK // 2, 0)

        def is_first(j):
            return isinstance(j, int) and j == 0

        def is_last(j):
            return isinstance(j, int) and j == NBLK - 1

        @block.sync
        def _(sp):
            def step(j, n, par):
                if isinstance(j, int):
                    e = sp.value_load(keep["block_expert"][0:1, j:j + 1], min_val=0, max_val=E - 1)
                else:
                    e = sp.value_load(keep["block_expert"][0:1, bass.ds(j, 1)], min_val=0, max_val=E - 1)
                sp.wait_ge(turned, j + 1)
                sp.dma_start(rows[:, par], one(slot_rows[bass.ds(j, 1)])).then_inc(rows_loaded[par], 16)
                for x in W:
                    sp.wait_ge(split[x], j + 1)
                    weights = dram[x].rearrange("e (c p) n -> e p c n", p=P)
                    sp.dma_start(raw[x][:], one(weights[bass.ds(e, 1)])).then_inc(raw_loaded[x], 16)

            over_blocks(sp, step)

        @block.tensor
        def _(pe):
            pe.sem_inc(down_in_psum, 2)
            pe.sem_inc(turned, 2)
            pe.sem_inc(up_in_psum, 2 * Q)

            def turn(j, n, par):
                pe.wait_ge(rows_loaded[par], n * 16 + 16)
                for c in range(DC):
                    for h in range(BH):
                        last = pe.transpose(ps[:, TURN + par, c * BLK + h * P:c * BLK + (h + 1) * P], rows[:, par, h, c * P:(c + 1) * P],
                                            keep["ident"][:])
                last.then_inc(turned, 1)

            def step(j, n, par):
                pe.wait_ge(rowsT_split, j + 1)
                for q in range(Q):
                    pe.wait_ge(product_ready, j * Q + q + 1)
                    for m in (2 * q, 2 * q + 1):
                        for x, at in (("w1", 0), ("w3", BLK)):
                            if m == 0:
                                pe.wait_ge(split[x], j + 2)
                            for c in range(DC):
                                for a, b in PASSES:
                                    last = pe.matmul(ps[:, UP + m % 4, at:at + BLK], parts[x][a][:, par, c, m * P:(m + 1) * P],
                                                     rowsT[b][:, par, c * BLK:(c + 1) * BLK],
                                                     start=((c, a, b) == (0, 0, 0)), stop=((c, a, b) == (DC - 1, *PASSES[-1])))
                    last.then_inc(up_in_psum, 1)
                if not is_last(j):
                    turn(j + 1, n + par, 1 - par)
                pe.wait_ge(split["w2"], j + 2)
                pe.wait_ge(result_ready, j + 1)
                for h in range(BH):
                    for m in range(FC):
                        if h == 0 and m % 2 == 0:
                            pe.wait_ge(gated_split, j * Q + m // 2 + 3)
                        for a, b in PASSES:
                            last = pe.matmul(ps[:, DOWN + par, h * D:(h + 1) * D], gatedT[a][:, m, h * P:(h + 1) * P],
                                             parts["w2"][b][:, par, m, :],
                                             start=((m, a, b) == (0, 0, 0)), stop=((m, a, b) == (FC - 1, *PASSES[-1])))
                last.then_inc(down_in_psum, 1)

            turn(0, 0, 0)
            over_blocks(pe, step)

        @block.scalar
        def _(act):
            act.sem_inc(result_ready, 2)
            act.sem_inc(stored[0], 16)
            act.sem_inc(stored[1], 16)

            def high_weights(x, j, par):
                act.wait_ge(raw_loaded[x], j * 16 + 16)
                act.wait_ge(up_in_psum, (j + 1) * Q)
                act.copy(parts[x][0][:, par], raw[x][:]).then_inc(high_ready[x], 1)

            def high_rows(j, par):
                act.wait_ge(turned, j + 3)
                act.copy(rowsT[0][:, par], ps[:, TURN + par, :]).then_inc(rowsT_high, 1)

            def high_gated(j, q):
                act.wait_ge(product_ready, j * Q + q + 3)
                act.copy(gatedT[0][:, 2 * q:2 * q + 2, :], product[:, q % 2]).then_inc(gated_high, 1)

            def take_result(j, n, par):
                act.wait_ge(down_in_psum, j + 3)
                act.wait_ge(stored[par], n * 16 + 16)
                act.copy(result[:, par].rearrange("p h d -> p (h d)"), ps[:, DOWN + par, :]).then_inc(result_ready, 1)
                act.wait_ge(result_ready, j + 3)
                act.dma_start(one(expert_rows[bass.ds(j, 1)]), result[:, par]).then_inc(stored[par], 16)

            def step(j, n, par):
                if not is_first(j):
                    take_result(j - 1, n + par - 1, 1 - par)
                for q in range(Q):
                    act.wait_ge(up_in_psum, j * Q + q + 1 + 2 * Q)
                    act.activation(relu[:, q % 2], ps[:, UP + q % 2 * 2:UP + q % 2 * 2 + 2, 0:BLK], ACT.Relu).then_inc(relu_ready, 1)
                    if q:
                        high_gated(j, q - 1)
                    if q == 0 and not is_last(j):
                        high_weights("w1", j + 1, 1 - par)
                high_gated(j, Q - 1)
                if not is_last(j):
                    high_rows(j + 1, 1 - par)
                    high_weights("w3", j + 1, 1 - par)

            high_rows(0, 0)
            high_weights("w1", 0, 0)
            high_weights("w3", 0, 0)
            over_blocks(act, step)
            take_result(NBLK - 1, NBLK // 2, 0)
            act.wait_ge(stored[0], 16 * (NBLK // 2 + 1) + 16)
            act.wait_ge(stored[1], 16 * (NBLK // 2) + 16)

        @block.vector
        def _(dve):
            dve.sem_inc(product_ready, 2)
            dve.sem_inc(gated_split, 2)
            dve.sem_inc(split["w1"], 1)
            dve.sem_inc(split["w3"], 1)

            def low_weights(x, j, par):
                dve.wait_ge(high_ready[x], j + 1)
                dve.tensor_tensor(parts[x][1][:, par], raw[x][:], parts[x][0][:, par].bitcast(F32), ALU.subtract)\
                   .then_inc(split[x], 1)

            def low_rows(j, par):
                dve.wait_ge(rowsT_high, j + 1)
                dve.tensor_tensor(rowsT[1][:, par], ps[:, TURN + par, :], rowsT[0][:, par].bitcast(F32), ALU.subtract)\
                   .then_inc(rowsT_split, 1)

            def low_gated(j, q):
                dve.wait_ge(gated_high, j * Q + q + 1)
                at = slice(2 * q, 2 * q + 2)
                dve.tensor_tensor(gatedT[1][:, at, :], product[:, q % 2], gatedT[0][:, at, :].bitcast(F32), ALU.subtract)\
                   .then_inc(gated_split, 1)

            def step(j, n, par):
                for q in range(Q):
                    dve.wait_ge(gated_split, j * Q + q + 1)
                    dve.wait_ge(relu_ready, j * Q + q + 1)
                    dve.tensor_tensor(product[:, q % 2], relu[:, q % 2], ps[:, UP + q % 2 * 2:UP + q % 2 * 2 + 2, BLK:2 * BLK], ALU.mult)\
                       .then_inc(product_ready, 1)
                    if q:
                        low_gated(j, q - 1)
                    if q == 1 and not is_last(j):
                        low_weights("w1", j + 1, 1 - par)
                low_gated(j, Q - 1)
                if not is_last(j):
                    low_rows(j + 1, 1 - par)
                    low_weights("w3", j + 1, 1 - par)

            low_rows(0, 0)
            low_weights("w1", 0, 0)
            low_weights("w3", 0, 0)
            over_blocks(dve, step)

        @block.gpsimd
        def _(pool):
            pool.sem_inc(split["w2"], 1)

            def step(j, n, par):
                pool.wait_ge(raw_loaded["w2"], j * 16 + 16)
                pool.wait_ge(down_in_psum, j + 1)
                pool.sem_inc(passed, 1)
                pool.tensor_copy(parts["w2"][0][:, par], raw["w2"][:]).then_inc(high_ready["w2"], 1)
                pool.wait_ge(high_ready["w2"], j + 1)
                pool.tensor_tensor(parts["w2"][1][:, par], raw["w2"][:], parts["w2"][0][:, par].bitcast(F32), ALU.subtract)\
                    .then_inc(split["w2"], 1)

            over_blocks(pool, step)


def combine(nc, dram, keep):
    with ExitStack() as ctx:
        def sb(name, shape, dt=F32):
            return ctx.enter_context(nc.sbuf_tensor(name, shape, dt))

        def sem(name):
            return ctx.enter_context(nc.semaphore(name))

        y = sb("y5", [P, TT, TOPK, D])
        stats = sb("stats5", [P, TT, 6])
        mean = sb("mean5", [P, TT])
        apart = sb("apart5", [P, TT])
        spread = sb("spread5", [P, TT])
        root = sb("root5", [P, TT])
        rstd = sb("rstd5", [P, TT])
        final = sb("final5", [P, TT, D])

        gathered = [sem(f"gathered{b}") for b in range(B)]
        mixed = sem("mixed5")
        var_ready = sem("var_ready5")
        root_ready = sem("root_ready5")
        out_ready = sem("out_ready5")
        stored = sem("stored5")
        dve_step = sem("dve_step5")

        block = ctx.enter_context(nc.Block())

        @block.gpsimd
        def _(pool):
            for t in range(TT):
                for k in range(TOPK):
                    pool.indirect_dma_start(y[:, t, k, :], None, dram["expert_rows"],
                                            bass.IndirectOffsetOnAxis(keep["slots"][:, k, t:t + 1], 0)).then_inc(gathered[t // TS], 16)

        @block.scalar
        def _(act):
            for b in range(B):
                at = slice(b * TS, (b + 1) * TS)
                act.wait_ge(var_ready, b + 1)
                act.activation(root[:, at], spread[:, at], ACT.Sqrt, bias=keep["eps"][:, 0:1], scale=1.0 / D).then_inc(root_ready, 1)

        @block.sync
        def _(sp):
            for b in range(B):
                sp.wait_ge(out_ready, b + 1)
                sp.dma_start(dram["out"][b].rearrange("(t p) d -> p t d", p=P), final[:, b * TS:(b + 1) * TS, :]).then_inc(stored, 16)
            sp.wait_ge(stored, 16 * B)

        @block.vector
        def _(dve):
            done = [0]

            def link(ins):
                done[0] += 1
                ins.then_inc(dve_step, 1)
                dve.wait_ge(dve_step, done[0])

            for b in range(B):
                tiles = range(b * TS, (b + 1) * TS)
                at = slice(b * TS, (b + 1) * TS)
                dve.wait_ge(gathered[b], 16 * TOPK * TS)
                for k in range(TOPK):
                    for t in tiles:
                        last = dve.scalar_tensor_tensor(keep["z"][:, t, :], y[:, t, k, :], keep["shares"][:, t, k:k + 1], keep["z"][:, t, :],
                                                        ALU.mult, ALU.add)
                    link(last)
                for t in tiles:
                    last = dve.bn_stats(stats[:, t, :], keep["z"][:, t, :])
                link(last)
                dve.tensor_tensor(mean[:, at], stats[:, at, 1], stats[:, at, 4], ALU.add)
                dve.tensor_tensor(apart[:, at], stats[:, at, 1], stats[:, at, 4], ALU.subtract)
                link(dve.tensor_tensor(spread[:, at], stats[:, at, 2], stats[:, at, 5], ALU.add))
                dve.tensor_scalar(mean[:, at], mean[:, at], 0.5, None, ALU.mult)
                link(dve.tensor_tensor(apart[:, at], apart[:, at], apart[:, at], ALU.mult))
                dve.scalar_tensor_tensor(spread[:, at], apart[:, at], D / 4.0, spread[:, at], ALU.mult, ALU.add).then_inc(var_ready, 1)
                dve.wait_ge(root_ready, b + 1)
                link(dve.reciprocal(rstd[:, at], root[:, at]))
                for t in tiles:
                    last = dve.tensor_scalar(final[:, t, :], keep["z"][:, t, :], mean[:, t:t + 1], rstd[:, t:t + 1], ALU.subtract, ALU.mult)
                link(last)
                dve.tensor_tensor(final[:, at, :], final[:, at, :], keep["x1"][:, at, :], ALU.add).then_inc(out_ready, 1)


def program(nc, dram):
    with ExitStack() as ctx:
        def sb(name, shape, dt=F32):
            return ctx.enter_context(nc.sbuf_tensor(name, shape, dt))

        keep = dict(
            ident=sb("ident", [P, P]),
            eps=sb("eps", [P, 1]),
            x1=sb("x1", [P, TT, D]),
            z=sb("z", [P, TT, D]),
            slots=sb("slots", [P, TOPK, TT], U32),
            shares=sb("shares", [P, TT, TOPK]),
            block_expert=sb("block_expert", [P, NBLK], I32),
        )
        with nc.sbuf_tensor("hT", [P, DC, T], F32) as hT:
            keep["hT"] = hT
            layer_one(nc, dram, keep)
            attention(nc, dram, keep)
        route(nc, dram, keep)
        experts(nc, dram, keep)
        combine(nc, dram, keep)


def kernel(**inputs):
    import concourse.bacc as bacc
    from concourse.bass_utils import run_bass_kernel_spmd

    X, W_in, W_out = (np.asarray(inputs[f"L0_attn_{n}"]) for n in ("X", "W_in", "W_out"))
    b_in, b_out = np.asarray(inputs["L0_attn_b_in"]), np.asarray(inputs["L0_attn_b_out"])
    ffn = {n: np.asarray(inputs[f"L0_ffn_{n}"]) for n in ("ln1_w", "wq", "wk", "wv", "wo", "ln2_w", "gate_w", "w1", "w2", "w3")}

    inv_freq = (1.0 / np.float32(10000.0) ** (np.arange(0, ROT, 2, dtype=np.float32) / np.float32(ROT))).astype(np.float32)
    angle = np.repeat(np.arange(S, dtype=np.float32)[:, None] * inv_freq[None, :], 2, axis=-1)
    cos = np.cos(angle).astype(np.float32)
    sin = (np.sin(angle) * np.where(np.arange(ROT) % 2 == 0, -1.0, 1.0)).astype(np.float32)
    swap = np.arange(ROT).reshape(-1, 2)[:, ::-1].ravel()
    causal = np.zeros((P, S), np.float32)
    causal[:, S - P:] = np.where(np.arange(P)[:, None] >= np.arange(P)[None, :], 0.0, NEG)

    arrays = {
        "x": X,
        "winT": W_in.T,
        "wswT": W_in[swap].T,
        "woutT": W_out.T,
        "b_in": b_in[None, :],
        "b_out": b_out[None, :],
        "qbias": np.stack([b_in[:P], b_in[P:2 * P], b_in[swap]], axis=1),
        "ln1": ffn["ln1_w"].reshape(DC, P).T,
        "ln2": ffn["ln2_w"][None, :],
        "wq": ffn["wq"].reshape(D, NKV, QG).transpose(1, 0, 2),
        "wkv": np.concatenate([ffn["wk"].reshape(D, NKV, HD), ffn["wv"].reshape(D, NKV, HD)], axis=2).transpose(1, 0, 2),
        "wo": ffn["wo"],
        "gate_w": ffn["gate_w"],
        "w1": ffn["w1"],
        "w2": ffn["w2"],
        "w3": ffn["w3"],
        "cos_tok": cos,
        "sin_tok": sin,
        "cos_ch": cos.T,
        "sin_ch": sin.T,
        "ident": np.eye(P, dtype=np.float32),
        "causal": causal,
        "before": np.triu(np.ones((P, P), np.float32), 1),
        "expert_ids": np.tile(np.arange(E, dtype=np.float32), (P, 1)),
        "block_ids": np.tile(np.arange(NBLK, dtype=np.float32), (P, 1)),
    }
    nc = bacc.Bacc("TRN2", target_bir_lowering=False, num_devices=1)
    given, dram = {}, {}
    for name, array in arrays.items():
        array = np.ascontiguousarray(array)
        given[f"in_{name}"] = array
        dram[name] = nc.dram_tensor(f"in_{name}", array.shape, mybir.dt.from_np(array.dtype), kind="ExternalInput").ap()
    dram["slot_rows"] = nc.dram_tensor("slot_rows", (SLOTS, D), F32, kind="Internal").ap()
    dram["expert_rows"] = nc.dram_tensor("expert_rows", (SLOTS, D), F32, kind="Internal").ap()
    dram["out"] = nc.dram_tensor("out_rows", (B, S, D), F32, kind="ExternalOutput").ap()
    program(nc, dram)
    result = run_bass_kernel_spmd(nc, [given], core_ids=[0])
    return result.results[0]["out_rows"]
```

```python
from contextlib import ExitStack

import numpy as np

import concourse.bass as bass
from concourse import mybir

ALU = mybir.AluOpType
ACT = mybir.ActivationFunctionType
AX = mybir.AxisListType
F32 = mybir.dt.float32
F32R = mybir.dt.float32r
I32 = mybir.dt.int32
U32 = mybir.dt.uint32

P = 128
B, S, D = 4, 512, 256
T = B * S
TT = T // P
TS = S // P
DC = D // P
ROT = D // 2
NH, NKV, HD = 32, 8, 64
GR = NH // NKV
QG = GR * HD
E, F, TOPK = 8, 1024, 2
FC = F // P
EXPERT_WEIGHTS = {"w1": (DC, F), "w3": (DC, F), "w2": (FC, D)}
EPS = 1e-5
BLK = 256
BH = BLK // P
NBLK = (TOPK * T + E * (BLK - 1)) // BLK
SLOTS = NBLK * BLK
NEG = -1e30
PASSES = ((0, 0), (1, 0), (0, 1))
NORMS = 3


def layer_one(nc, dram, keep):
    with ExitStack() as ctx:
        def sb(name, shape, dt=F32):
            return ctx.enter_context(nc.sbuf_tensor(name, shape, dt))

        def sem(name):
            return ctx.enter_context(nc.semaphore(name))

        winT = sb("winT", [P, DC, 3 * D])
        wswT = sb("wswT", [P, DC, ROT])
        woutT = sb("woutT", [P, DC, D])
        kvbias = sb("kvbias", [P, 2 * D])
        outbias = sb("outbias", [P, D])
        qbias = sb("qbias", [P, 3])
        ln1 = sb("ln1", [P, DC])
        cos_tok = sb("cos_tok", [P, TS, ROT])
        sin_tok = sb("sin_tok", [P, TS, ROT])
        cos_ch = sb("cos_ch", [ROT, S])
        sin_ch = sb("sin_ch", [ROT, S])
        ident = keep["ident"]
        x = sb("x", [P, TS, D])
        xres = sb("xres", [P, TS, D])
        zc = sb("zc", [P, TS, D])
        stats = sb("stats", [P, TS, 6])
        mean = sb("mean", [P, TS])
        apart = sb("apart", [P, TS])
        spread = sb("spread", [P, TS])
        rstd = sb("rstd", [P, TS])
        xn = sb("xn", [P, TS, D])
        xnb = sb("xnb", [P, TS, D])
        xnT = sb("xnT", [P, DC, S])
        kv = sb("kv", [P, TS, 2 * D])
        kswap = sb("kswap", [P, TS, ROT])
        square = sb("square", [P, TS, D])
        ksum = sb("ksum", [P, TS])
        rnorm = sb("rnorm", [P, TS])
        kvprod = sb("kvprod", [P, TS, D])
        q0 = sb("q0", [P, S])
        qsw = sb("qsw", [P, S])
        qT = sb("qT", [P, DC, S])
        state = sb("state", [P, DC])
        wstate = sb("wstate", [P, DC, D])
        y = sb("y", [P, TS, D])
        root = sb("root", [P, TS])
        knorm = sb("knorm", [P, TS])
        zroot = sb("zroot", [P, TS])
        zscale = sb("zscale", [P, TS])
        zsum = sb("zsum", [P, TS])
        zn = sb("zn", [P, TS, D])
        zeros = sb("zeros", [P, 8 * D])
        ps = ctx.enter_context(nc.psum_tensor("ps1", [P, 8, 512], F32))

        x_loaded = sem("x_loaded")
        xres_loaded = sem("xres_loaded")
        x_taken = sem("x_taken")
        kept = sem("kept")
        y_added = sem("y_added")
        y_normalised = sem("y_normalised")
        ident_loaded = sem("ident_loaded")
        win_loaded = sem("win_loaded")
        weights_loaded = sem("weights_loaded")
        zeroed = sem("zeroed")
        eps_set = sem("eps_set")
        slots_zero = sem("slots_zero")
        project_step = sem("project_step")
        finish_step = sem("finish_step")
        gp_step = sem("gp_step")
        xn_ready = sem("xn_ready")
        xnT_in_psum = sem("xnT_in_psum")
        xnT_ready = sem("xnT_ready")
        kv_in_psum = sem("kv_in_psum")
        kv_taken = sem("kv_taken")
        q_in_psum = sem("q_in_psum")
        q_biased = sem("q_biased")
        qT_ready = sem("qT_ready")
        k_rotated = sem("k_rotated")
        var_ready = sem("var_ready")
        root_ready = sem("root_ready")
        ksquares = sem("ksquares")
        zsquares = sem("zsquares")
        ksum_ready = sem("ksum_ready")
        kvprod_ready = sem("kvprod_ready")
        rnorm_ready = sem("rnorm_ready")
        state_in_psum = sem("state_in_psum")
        wstate_ready = sem("wstate_ready")
        y_in_psum = sem("y_in_psum")
        xnb_ready = sem("xnb_ready")
        z_ready = sem("z_ready")
        zsum_ready = sem("zsum_ready")
        zn_ready = sem("zn_ready")
        znT_in_psum = sem("znT_in_psum")
        hT_high = sem("hT_high")
        hT_done = sem("hT_done")
        dve_passed = sem("dve_passed1")

        block = ctx.enter_context(nc.Block())

        T_BANK, Q_BANK, KV_BANK, Y_BANK, STATE_BANK = 0, (2, 7, 6), 3, 6, 6

        def over_sequences(eng, step):
            step(None, 0)
            with eng.Fori(0, B - 1) as b:
                step(b, b + 1)
            step(B - 1, None)

        @block.sync
        def _(sp):
            xd = dram["x"].rearrange("b (t p) d -> b p t d", p=P)
            sp.dma_start(x[:], xd[0]).then_inc(x_loaded, 16)
            sp.dma_start(ident[:], dram["ident"]).then_inc(ident_loaded, 16)
            sp.dma_start(winT[:], dram["winT"].rearrange("(c p) n -> p c n", p=P)).then_inc(win_loaded, 16)
            loads = [
                (wswT[:], dram["wswT"].rearrange("(c p) n -> p c n", p=P)),
                (woutT[:], dram["woutT"].rearrange("(c p) n -> p c n", p=P)),
                (kvbias[:], dram["b_in"][:, D:3 * D].to_broadcast([P, 2 * D])),
                (outbias[:], dram["b_out"].to_broadcast([P, D])),
                (qbias[:], dram["qbias"]),
                (ln1[:], dram["ln1"]),
                (cos_tok[:], dram["cos_tok"].rearrange("(t p) n -> p t n", p=P)),
                (sin_tok[:], dram["sin_tok"].rearrange("(t p) n -> p t n", p=P)),
                (cos_ch[:], dram["cos_ch"]),
                (sin_ch[:], dram["sin_ch"]),
            ]
            for dst, src in loads:
                sp.dma_start(dst, src).then_inc(weights_loaded, 16)
            sp.dma_start(xres[:], xd[0]).then_inc(xres_loaded, 16)
            sp.wait_ge(zeroed, 1)
            fill = dram["slot_rows"].rearrange("(n p) d -> p n d", p=P)
            rows = SLOTS // P
            fills = 0
            for n in range(0, rows, 8):
                k = min(8, rows - n)
                sp.dma_start(fill[:, n:n + k, :], zeros[:, 0:k * D].rearrange("p (n d) -> p n d", d=D)).then_inc(slots_zero, 16)
                fills += 1
            with sp.Fori(1, B) as b:
                rows = xd[bass.ds(b, 1)].rearrange("o p t d -> (o p) t d")
                sp.wait_ge(xn_ready, b)
                sp.dma_start(x[:], rows).then_inc(x_loaded, 16)
                sp.wait_ge(x_taken, b)
                sp.dma_start(xres[:], rows).then_inc(xres_loaded, 16)
            sp.wait_ge(slots_zero, 16 * fills)
        n_loads = 10

        @block.tensor
        def _(pe):
            pe.wait_ge(ident_loaded, 16)

            def step(b, a):
                if b is not None:
                    pe.wait_ge(kvprod_ready, b + 1)
                    pe.wait_ge(rnorm_ready, b + 1)
                    pe.wait_ge(q_biased, b + 1)
                    for m in range(DC):
                        for t in range(TS):
                            last = pe.matmul(ps[:, STATE_BANK, m:m + 1], kvprod[:, t, m * P:(m + 1) * P], rnorm[:, t:t + 1],
                                             start=(t == 0), stop=(t == TS - 1))
                    last.then_inc(state_in_psum, 1)
                if a is not None:
                    pe.wait_ge(xn_ready, a + 1)
                    for c in range(DC):
                        for t in range(TS):
                            last = pe.transpose(ps[:, T_BANK + c, t * P:(t + 1) * P], xn[:, t, c * P:(c + 1) * P], ident[:])
                    last.then_inc(xnT_in_psum, 1)
                if b is not None:
                    pe.wait_ge(wstate_ready, b + 1)
                    pe.wait_ge(qT_ready, b * 2 + 2)
                    for t in range(TS):
                        for m in range(DC):
                            last = pe.matmul(ps[:, Y_BANK + t // 2, (t % 2) * D:(t % 2 + 1) * D], qT[:, m, t * P:(t + 1) * P],
                                             wstate[:, m, :], start=(m == 0), stop=(m == DC - 1))
                    last.then_inc(y_in_psum, 1)
                if a is not None:
                    if b is None:
                        pe.wait_ge(win_loaded, 16)
                    pe.wait_ge(xnT_ready, a + 1)
                    for t in range(TS):
                        if t >= 3:
                            pe.wait_ge(kv_taken, a * TS + t - 2)
                        for c in range(DC):
                            last = pe.matmul(ps[:, KV_BANK + t % 3, :], xnT[:, c, t * P:(t + 1) * P], winT[:, c, D:3 * D],
                                             start=(c == 0), stop=(c == DC - 1))
                        last.then_inc(kv_in_psum, 1)
                if a is not None:
                    if b is None:
                        pe.wait_ge(weights_loaded, 16 * n_loads)
                    else:
                        pe.wait_ge(y_added, b + 1)
                    for m in range(DC + 1):
                        for c in range(DC):
                            w = winT[:, c, m * P:(m + 1) * P] if m < DC else wswT[:, c, :]
                            last = pe.matmul(ps[:, Q_BANK[m], :], w, xnT[:, c, :], start=(c == 0), stop=(c == DC - 1))
                    last.then_inc(q_in_psum, 1)
                if b is not None:
                    pe.wait_ge(zn_ready, b + 1)
                    for c in range(DC):
                        for t in range(TS):
                            last = pe.transpose(ps[:, T_BANK + c, t * P:(t + 1) * P], zn[:, t, c * P:(c + 1) * P], ident[:])
                    last.then_inc(znT_in_psum, 1)

            over_sequences(pe, step)

        @block.scalar
        def _(act):
            act.wait_ge(eps_set, 1)

            def step(b, a):
                def deviation(n):
                    act.wait_ge(var_ready, n)
                    act.activation(root[:], spread[:], ACT.Sqrt, bias=keep["eps"][:, 0:1], scale=1.0 / D).then_inc(root_ready, 1)

                if a is not None:
                    deviation(1 if b is None else b * NORMS + 2)
                    act.wait_ge(xnT_in_psum, a + 1)
                    for c in range(DC):
                        last = act.copy(xnT[:, c, :], ps[:, T_BANK + c, :])
                    last.then_inc(xnT_ready, 1)
                if b is not None:
                    first = b * NORMS + (2 if a is None else 3)
                    deviation(first)
                    deviation(first + 1)
                    act.wait_ge(z_ready, b + 1)
                    for t in range(TS):
                        last = act.activation(square[:, t, :], zc[:, t, :], ACT.Square, accum_out=zsum[:, t:t + 1])
                    last.then_inc(zsquares, 1)
                    act.wait_ge(zsquares, b + 1)
                    act.activation(zroot[:], zsum[:], ACT.Sqrt, bias=keep["eps"][:, 0:1], scale=1.0 / D).then_inc(zsum_ready, 1)
                if a is not None:
                    act.wait_ge(k_rotated, a + 1)
                    for t in range(TS):
                        last = act.activation(square[:, t, :], kv[:, t, 0:D], ACT.Square, accum_out=ksum[:, t:t + 1])
                    last.then_inc(ksquares, 1)
                    act.wait_ge(ksquares, a + 1)
                    act.activation(knorm[:], ksum[:], ACT.Sqrt).then_inc(ksum_ready, 1)
                if a is not None:
                    if b is None:
                        act.wait_ge(weights_loaded, 16 * n_loads)
                    else:
                        act.wait_ge(y_in_psum, b + 1)
                    act.wait_ge(q_in_psum, a + 1)
                    act.activation(q0[:], ps[:, Q_BANK[0], :], ACT.Identity, bias=qbias[:, 0:1])
                    act.activation(qsw[:], ps[:, Q_BANK[2], :], ACT.Identity, bias=qbias[:, 2:3]).then_inc(q_biased, 1)
                    act.activation(qT[:, 1, :], ps[:, Q_BANK[1], :], ACT.Identity, bias=qbias[:, 1:2]).then_inc(qT_ready, 1)
                if b is not None:
                    act.wait_ge(znT_in_psum, b + 1)
                    for c in range(DC):
                        last = act.activation(keep["hT"][0][:, c, bass.ds(b * S, S)], ps[:, T_BANK + c, :], ACT.Copy,
                                              scale=ln1[:, c:c + 1])
                    last.then_inc(hT_high, 1)

            over_sequences(act, step)

        @block.gpsimd
        def _(pool):
            pool.memset(zeros[:], 0.0).then_inc(zeroed, 1)
            pool.memset(keep["eps"][:], EPS).then_inc(eps_set, 1)
            pool.sem_inc(kept, 1)
            pool.wait_ge(weights_loaded, 16 * n_loads)

            def step(b, a):
                if a is not None:
                    pool.wait_ge(xn_ready, a + 1)
                    if b is not None:
                        pool.wait_ge(y_added, b + 1)
                    for t in range(TS):
                        last = pool.tensor_tensor(xnb[:, t, :], xn[:, t, :], outbias[:], ALU.add)
                    last.then_inc(xnb_ready, 1)
                if b is not None:
                    tiles = bass.ds(b * TS, TS)
                    pool.wait_ge(x_taken, b + 1)
                    pool.tensor_copy(keep["x1"][:, tiles, :], y[:])
                    pool.wait_ge(z_ready, b + 1)
                    pool.tensor_copy(keep["z"][:, tiles, :], zc[:]).then_inc(kept, 1)
                if a is not None:
                    pool.wait_ge(q_biased, a + 1)
                    pool.tensor_tensor(q0[:], q0[:], cos_ch[:], ALU.mult)
                    pool.tensor_tensor(qsw[:], qsw[:], sin_ch[:], ALU.mult).then_inc(gp_step, 1)
                    pool.wait_ge(gp_step, a + 1)
                    pool.tensor_tensor(qT[:, 0, :], q0[:], qsw[:], ALU.add).then_inc(qT_ready, 1)

            over_sequences(pool, step)

        @block.vector
        def _(dve):
            PROJECT, FINISH = 7, 10

            def step(b, a):
                links = {project_step: 0, finish_step: 0}
                which, norm = [None], [0]
                norms_before = 0 if b is None else b * NORMS + 1

                def link(ins):
                    sequence, count = (a, PROJECT) if which[0] is project_step else (b, FINISH)
                    links[which[0]] += 1
                    ins.then_inc(which[0], 1)
                    dve.wait_ge(which[0], sequence * count + links[which[0]])

                def moments(rows):
                    for t in range(TS):
                        last = dve.bn_stats(stats[:, t, :], rows[:, t, :])
                    link(last)
                    dve.tensor_tensor(mean[:], stats[:, :, 1], stats[:, :, 4], ALU.add)
                    dve.tensor_tensor(apart[:], stats[:, :, 1], stats[:, :, 4], ALU.subtract)
                    link(dve.tensor_tensor(spread[:], stats[:, :, 2], stats[:, :, 5], ALU.add))
                    dve.tensor_scalar(mean[:], mean[:], 0.5, None, ALU.mult)
                    link(dve.tensor_tensor(apart[:], apart[:], apart[:], ALU.mult))
                    dve.scalar_tensor_tensor(spread[:], apart[:], D / 4.0, spread[:], ALU.mult, ALU.add).then_inc(var_ready, 1)
                    norm[0] += 1
                    dve.wait_ge(root_ready, norms_before + norm[0])
                    link(dve.reciprocal(rstd[:], root[:]))

                def normalised(out, rows, done):
                    for t in range(TS):
                        last = dve.tensor_scalar(out[:, t, :], rows[:, t, :], mean[:, t:t + 1], rstd[:, t:t + 1], ALU.subtract, ALU.mult)
                    last.then_inc(done, 1)

                def take_kv(t):
                    if a is not None:
                        dve.wait_ge(kv_in_psum, a * TS + t + 1)
                        dve.tensor_tensor(kv[:, t, :], ps[:, KV_BANK + t % 3, :], kvbias[:], ALU.add).then_inc(kv_taken, 1)

                if a is not None:
                    which[0] = project_step
                    dve.wait_ge(x_loaded, a * 16 + 16)
                    moments(x)
                    if b is not None:
                        dve.wait_ge(xnb_ready, b + 1)
                    normalised(xn, x, xn_ready)
                if b is not None:
                    which[0] = finish_step
                    dve.wait_ge(state_in_psum, b + 1)
                    link(dve.tensor_copy(state[:], ps[:, STATE_BANK, 0:DC]))
                    for m in range(DC):
                        last = dve.tensor_scalar(wstate[:, m, :], woutT[:, m, :], state[:, m:m + 1], None, ALU.mult)
                    last.then_inc(wstate_ready, 1)
                    dve.wait_ge(kept, b + 1)
                    dve.wait_ge(xnb_ready, b + 1)
                    dve.wait_ge(y_in_psum, b + 1)
                    for c in range(TS // 2):
                        last = dve.tensor_tensor(y[:, 2 * c:2 * c + 2, :], ps[:, Y_BANK + c, :].rearrange("p (t d) -> p t d", d=D),
                                                 xnb[:, 2 * c:2 * c + 2, :], ALU.add)
                    last.then_inc(y_added, 1)
                    dve.wait_ge(y_added, b + 1)
                    moments(y)
                    normalised(y, y, y_normalised)
                if b is None:
                    dve.wait_ge(weights_loaded, 16 * n_loads)
                take_kv(0)
                if b is not None:
                    dve.wait_ge(y_normalised, b + 1)
                    dve.wait_ge(xres_loaded, b * 16 + 16)
                    dve.tensor_tensor(y[:], y[:], xres[:], ALU.add).then_inc(x_taken, 1)
                    dve.wait_ge(x_taken, b + 1)
                    moments(y)
                    normalised(zc, y, z_ready)
                take_kv(1)
                take_kv(2)
                take_kv(3)
                if a is not None:
                    which[0] = project_step
                    dve.wait_ge(kv_taken, a * TS + TS)
                    k = kv[:, :, 0:ROT]
                    for s in range(2):
                        last = dve.tensor_tensor(kswap[:, :, s:ROT:2], k[:, :, 1 - s:ROT:2], sin_tok[:, :, s:ROT:2], ALU.mult)
                    link(last)
                    link(dve.tensor_tensor(k, k, cos_tok[:], ALU.mult))
                    dve.tensor_tensor(k, k, kswap[:], ALU.add).then_inc(k_rotated, 1)
                    dve.wait_ge(k_rotated, a + 1)
                    dve.tensor_tensor(kvprod[:], kv[:, :, 0:D], kv[:, :, D:2 * D], ALU.mult).then_inc(kvprod_ready, 1)
                if b is not None:
                    which[0] = finish_step
                    dve.wait_ge(zsum_ready, b + 1)
                    link(dve.reciprocal(zscale[:], zroot[:]))
                    dve.wait_ge(z_ready, b + 1)
                    for t in range(TS):
                        last = dve.tensor_scalar(zn[:, t, :], zc[:, t, :], zscale[:, t:t + 1], None, ALU.mult)
                    last.then_inc(zn_ready, 1)
                    assert links[finish_step] == FINISH
                if a is not None:
                    which[0] = project_step
                    dve.wait_ge(ksum_ready, a + 1)
                    link(dve.tensor_scalar(rnorm[:], knorm[:], 1e-12, None, ALU.max))
                    dve.reciprocal(rnorm[:], rnorm[:]).then_inc(rnorm_ready, 1)
                    assert links[project_step] == PROJECT
                if b is not None:
                    at = bass.ds(b * S, S)
                    dve.wait_ge(hT_high, b + 1)
                    dve.sem_inc(dve_passed, 1)
                    for c in range(DC):
                        last = dve.scalar_tensor_tensor(keep["hT"][1][:, c, at], ps[:, T_BANK + c, :], ln1[:, c:c + 1],
                                                        keep["hT"][0][:, c, at].bitcast(F32), ALU.mult, ALU.subtract)
                    last.then_inc(hT_done, 1)

            over_sequences(dve, step)
            dve.wait_ge(hT_done, B)
            dve.wait_ge(kept, B + 1)


def attention(nc, dram, keep):
    UNITS = TS
    TURNS = UNITS * (UNITS + 1) // 2
    KT = NH * HD // P
    PAIRS = NKV // 2
    with ExitStack() as ctx:
        def sb(name, shape, dt=F32):
            return ctx.enter_context(nc.sbuf_tensor(name, shape, dt))

        def sem(name):
            return ctx.enter_context(nc.semaphore(name))

        w_raw = sb("w_raw", [P, 2, DC, QG + 2 * HD])
        w_parts = [sb(f"w_{n}", [P, 2, DC, QG + 2 * HD], F32R) for n in ("high", "low")]
        wo = sb("wo", [P, KT, D])
        causal = sb("causal", [P, S])
        q_raw = sb("q_raw", [P, 2, S])
        k_raw = sb("k_raw", [P, S])
        q_parts = sb("q_parts", [P, 2, GR, S], F32R)
        k_high = sb("k_high", [P, 2, S], F32R)
        k_low = sb("k_low", [P, 2, S], F32R)
        vT = sb("vTg", [P, S])
        v = sb("vg", [P, 2, TS, HD])
        probs = sb("probs", [P, 2, GR, S])
        shift = sb("shift", [P, 2, GR])
        total = sb("total", [P, 2, GR])
        inverse = sb("inverse", [P, 2, GR])
        probsT = sb("probsT", [P, 4, GR * P])
        outT = sb("outT", [P, QG // P, S])
        ident = keep["ident"]
        ps = ctx.enter_context(nc.psum_tensor("ps2", [P, 8, 512], F32))
        SCORES, TURN, MIX, PROJ = 0, 4, 6, 7

        consts_loaded = sem("consts_loaded")
        w_loaded = [sem("w_loaded0"), sem("w_loaded1")]
        w_high = sem("w_high")
        w_split = sem("w_split")
        proj_in_psum = sem("proj_in_psum")
        proj_taken = sem("proj_taken")
        pool_step = sem("pool_step2")
        split_ready = sem("split_ready")
        pool_passed = sem("pool_passed")
        scores_in_psum = sem("scores_in_psum")
        shift_ready = sem("shift_ready")
        exp_done = sem("exp_done")
        probs_ready = sem("probs_ready")
        turned_in_psum = sem("turned_in_psum")
        turned_taken = [sem("turned_by_dve"), sem("turned_by_act")]
        mixed_in_psum = sem("mixed_in_psum")
        mixed_taken = sem("mixed_taken")
        rows_in_psum = sem("rows_in_psum")
        rows_added = sem("rows_added")
        dve_step = sem("dve_step2")
        dve_passed = sem("dve_passed")
        pe_passed = sem("pe_passed")

        block = ctx.enter_context(nc.Block())

        WIDTH = [4, 3, 2, 1]
        FIRST = [0, 4, 7, 9]
        AGENDA = [
            ["score 0", "turn 0", "turn 1", "score 1", "mix 0", "project 1", "turn 2", "score 2", "mix 1", "turn 3", "project 2",
             "score 3", "mix 2", "mix 3", "project 3"],
            ["score 0", "score 1", "turn 0", "turn 1", "score 2", "rows 0", "turn 2", "mix 0", "score 3", "mix 1", "mix 2"],
            ["score 0", "score 1", "turn 0", "turn 1", "score 2", "rows 1", "score 3", "mix 0", "mix 1"],
            ["score 0", "score 1", "turn 0", "score 2", "rows 2", "mix 0", "score 3", "rows 3", "project 0"],
        ]

        def steps(u, nxt, following):
            for what, n in ((step.split()[0], int(step.split()[1])) for step in AGENDA[u]):
                if not (what == "score" and not nxt or what == "project" and not following):
                    yield what, n

        def over_sequences(eng, first, unit):
            def group(turn, pair, par, more, ahead=True):
                it, g = turn * 2 + par, pair * 2 + par
                following = (turn, 1) if par == 0 else (turn + 1, 0)
                after = (turn + 1, par) if ahead else None
                for u in range(UNITS):
                    if u + 1 < UNITS:
                        unit(it, g, par, u, (turn, par, u + 1), following if more else None, after)
                    else:
                        unit(it, g, par, u, (*following, 0) if more else None, after, after)

            first((0, 0), (0, 1))
            with eng.Fori(0, B - 1) as b:
                with eng.Fori(0, PAIRS) as pair:
                    turn = eng.snap(b * PAIRS + pair)
                    group(turn, pair, 0, True)
                    group(turn, pair, 1, True)
            b = B - 1
            with eng.Fori(0, PAIRS - 1) as pair:
                turn = eng.snap(pair + b * PAIRS)
                group(turn, pair, 0, True)
                group(turn, pair, 1, True)
            pair = PAIRS - 1
            group(b * PAIRS + pair, pair, 0, True, False)
            group(b * PAIRS + pair, pair, 1, False, False)

        @block.sync
        def _(sp):
            wqd = dram["wq"].rearrange("g (c p) n -> g p c n", p=P)
            wkvd = dram["wkv"].rearrange("g (c p) n -> g p c n", p=P)
            with sp.Fori(0, B) as b:
                with sp.Fori(0, NKV // 2) as pair:
                    for par in range(2):
                        sp.wait_ge(w_split, b * NKV + pair * 2 + par + 1)
                        g = bass.ds(pair * 2 + par, 1)
                        sp.dma_start(w_raw[:, par, :, 0:QG], wqd[g].rearrange("o p c n -> (o p) c n")).then_inc(w_loaded[par], 16)
                        sp.dma_start(w_raw[:, par, :, QG:QG + 2 * HD], wkvd[g].rearrange("o p c n -> (o p) c n")).then_inc(w_loaded[par], 16)

        @block.tensor
        def _(pe):
            pe.sem_inc(proj_in_psum, 8)

            def project(turn, par, part):
                it, b = turn * 2 + par, turn // PAIRS
                if part == 0:
                    pe.wait_ge(w_split, it + 3)
                pe.wait_ge(proj_taken, it * 4 + part + 1)
                if part == 1:
                    pe.sem_inc(pe_passed, 1)
                    for t in range(TS):
                        last = pe.transpose(ps[:, PROJ, t * HD:(t + 1) * HD], vT[HD:2 * HD, t * P:(t + 1) * P],
                                            ident[HD:2 * HD, HD:2 * HD])
                else:
                    cols = slice(QG, QG + P) if part == 0 else slice((part - 2) * P, (part - 1) * P)
                    for c in range(DC):
                        for x, y in PASSES:
                            last = pe.matmul(ps[:, PROJ, :], w_parts[x][:, par, c, cols], keep["hT"][y][:, c, bass.ds(b * S, S)],
                                             start=((c, x, y) == (0, 0, 0)), stop=((c, x, y) == (DC - 1, *PASSES[-1])))
                last.then_inc(proj_in_psum, 1)

            def score(turn, par, u, h):
                it, n, i = turn * 2 + par, WIDTH[u] * P, WIDTH[u] - 1
                if u == 0 and h % 2 == 0:
                    pe.wait_ge(split_ready, it * 3 + 5 + h // 2)
                half = slice(h % 2 * HD, h % 2 * HD + HD)
                pe.wait_ge(exp_done, (it * UNITS + u) * GR + h + 1)
                at = slice(i * P, (i + 1) * P)
                pe.matmul(ps[:, SCORES + h, 0:n], q_parts[:, par, h, at], k_high[:, par, 0:n], start=True, stop=False)
                pe.matmul(ps[:, SCORES + h, 0:n], q_parts[half, par, h, at], k_low[half, par, 0:n],
                          start=False, stop=True).then_inc(scores_in_psum, 1)

            def first(group, second):
                for part in range(4):
                    project(*group, part)
                for h in range(GR):
                    score(*group, 0, h)
                project(*second, 0)
                pe.wait_ge(consts_loaded, 32)

            def unit(it, g, par, u, nxt, following, after):
                for what, j in steps(u, nxt, following):
                    n = FIRST[u] + j
                    if what == "turn":
                        pe.wait_ge(turned_taken[n % 2], it * (TURNS // 2) + n // 2 + 1)
                        for h in range(GR):
                            if j == 0:
                                pe.wait_ge(probs_ready, (it * UNITS + u) * GR + h + 1)
                            last = pe.transpose(ps[:, TURN + n % 2, h * P:(h + 1) * P], probs[:, u % 2, h, j * P:(j + 1) * P], ident[:])
                        last.then_inc(turned_in_psum, 1)
                    elif what == "mix":
                        pe.wait_ge(turned_taken[n % 2], it * (TURNS // 2) + n // 2 + 2)
                        if j == 0:
                            if u == 0:
                                pe.wait_ge(proj_taken, it * 4 + 3)
                            pe.wait_ge(mixed_taken, it * UNITS + u + 1)
                        heads = probsT[:, (n + 2 * par) % 4, :].rearrange("p (m a q) -> p a m q", a=2, q=P)
                        for a in range(2):
                            last = pe.matmul(ps[a * HD:(a + 1) * HD, MIX, 0:2 * P].rearrange("p (m q) -> p m q", q=P),
                                             v[:, par, j, :], heads[:, a], start=(j == 0), stop=(j == WIDTH[u] - 1))
                        if j == WIDTH[u] - 1:
                            last.then_inc(mixed_in_psum, 1)
                    elif what == "score":
                        score(*nxt, j)
                    elif what == "project":
                        if j == 0:
                            pe.wait_ge(rows_added, (it + 1) * UNITS + 1)
                        project(*following, j)
                    else:
                        tile = slice((WIDTH[j] - 1) * P, WIDTH[j] * P)
                        if j == 0 and following:
                            pe.wait_ge(proj_taken, it * 4 + 9)
                        pe.wait_ge(mixed_taken, it * UNITS + j + 2)
                        pe.wait_ge(rows_added, it * UNITS + j + 1)
                        for k in range(QG // P):
                            last = pe.matmul(ps[:, PROJ, 0:D], outT[:, k, tile],
                                             wo[:, bass.ds(g * 2 + k, 1), :].rearrange("p k n -> p (k n)"),
                                             start=(k == 0), stop=(k == QG // P - 1))
                        last.then_inc(rows_in_psum, 1)

            over_sequences(pe, first, unit)

        @block.scalar
        def _(act):
            act.sem_inc(proj_taken, 1)
            act.sem_inc(exp_done, GR)
            act.sem_inc(turned_taken[1], 1)
            act.sem_inc(mixed_taken, 1)

            def high_weights(turn, par):
                it = turn * 2 + par
                act.wait_ge(proj_in_psum, it * 4 + 4)
                act.wait_ge(w_loaded[par], turn * 32 + 32)
                act.copy(w_parts[0][:, par], w_raw[:, par]).then_inc(w_high, 1)

            def take(turn, par, part):
                it = turn * 2 + par
                if part != 1:
                    act.wait_ge(split_ready, it * 3 + max(part - 1, 0) + 1)
                act.wait_ge(proj_in_psum, it * 4 + part + 9)
                if part == 0:
                    act.copy(k_raw[0:HD, :], ps[0:HD, PROJ, :])
                    act.copy(k_raw[HD:2 * HD, :], ps[0:HD, PROJ, :])
                    last = act.copy(vT[HD:2 * HD, :], ps[HD:2 * HD, PROJ, :])
                elif part == 1:
                    last = act.copy(v[:, par, :, :], ps[:, PROJ, 0:TS * HD].rearrange("p (t d) -> p t d", d=HD))
                else:
                    act.copy(q_parts[0:HD, par, (part - 2) * 2, :], ps[0:HD, PROJ, :])
                    last = act.copy(q_raw[:, part - 2, :], ps[:, PROJ, :])
                last.then_inc(proj_taken, 1)

            def exponential(turn, par, u, h):
                n = WIDTH[u] * P
                act.wait_ge(shift_ready, ((turn * 2 + par) * UNITS + u) * GR + h + 1)
                act.activation(probs[:, u % 2, h, 0:n], ps[:, SCORES + h, 0:n], ACT.Exp, bias=shift[:, u % 2, h:h + 1],
                               scale=-1.0, accum_out=total[:, u % 2, h:h + 1]).then_inc(exp_done, 1)

            def first(group, second):
                high_weights(*group)
                act.dma_start(causal[:], dram["causal"]).then_inc(consts_loaded, 16)
                act.dma_start(wo[:], dram["wo"].rearrange("(k p) n -> p k n", p=P)).then_inc(consts_loaded, 16)
                for part in range(4):
                    take(*group, part)
                high_weights(*second)
                for h in range(GR):
                    exponential(*group, 0, h)
                take(*second, 0)

            def unit(it, g, par, u, nxt, following, after):
                if u == 1 and after:
                    high_weights(*after)
                for what, j in steps(u, nxt, following):
                    n = FIRST[u] + j
                    if what == "turn" and n % 2:
                        act.wait_ge(turned_in_psum, it * TURNS + n + 1)
                        act.copy(probsT[:, (n + 2 * par) % 4, :], ps[:, TURN + 1, :]).then_inc(turned_taken[1], 1)
                    elif what == "score":
                        exponential(*nxt, j)
                    elif what == "project":
                        take(*following, j)
                    elif what == "mix" and j == WIDTH[u] - 1:
                        act.wait_ge(mixed_in_psum, it * UNITS + u + 1)
                        act.copy(outT[:, :, j * P:(j + 1) * P],
                                 ps[:, MIX, 0:2 * P].rearrange("p (m q) -> p m q", q=P)).then_inc(mixed_taken, 1)

            over_sequences(act, first, unit)

        @block.gpsimd
        def _(pool):
            pool.sem_inc(split_ready, 3)
            pool.sem_inc(w_split, 2)

            def split_weights(turn, par):
                it = turn * 2 + par
                pool.wait_ge(split_ready, it * 3 + 3)
                pool.wait_ge(w_high, it + 1)
                pool.tensor_tensor(w_parts[1][:, par], w_raw[:, par], w_parts[0][:, par].bitcast(F32), ALU.subtract)\
                    .then_inc(w_split, 1)

            def split(turn, par, part):
                if part == 1:
                    return
                it, n = turn * 2 + par, max(part - 1, 0)
                done = [it * 5 + (0, 1, 3)[n]]

                def link(ins):
                    done[0] = done[0] + 1
                    ins.then_inc(pool_step, 1)
                    pool.wait_ge(pool_step, done[0])
                    pool.sem_inc(pool_passed, 1)

                if part == 0:
                    pool.wait_ge(w_split, it + 3)
                else:
                    pool.wait_ge(split_ready, it * 3 + n + 3)
                pool.wait_ge(proj_taken, it * 4 + part + 2)
                pool.sem_inc(pool_passed, 1)
                if part == 0:
                    splits = [(k_high[:, par, :], k_low[:, par, :], k_raw[:])]
                else:
                    a, b, h = slice(0, HD), slice(HD, 2 * HD), n * 2 - 2
                    splits = [(q_parts[a, par, h, :], q_parts[b, par, h, :], q_raw[a, n - 1, :]),
                              (q_parts[b, par, h + 1, :], q_parts[a, par, h + 1, :], q_raw[b, n - 1, :])]
                high, low, raw = splits[-1]
                link(pool.tensor_copy(high, raw))
                for high, low, raw in splits:
                    last = pool.tensor_tensor(low, raw, high.bitcast(F32), ALU.subtract)
                    if high is not splits[-1][0]:
                        link(last)
                last.then_inc(split_ready, 1)

            def first(group, second):
                split_weights(*group)
                for part in range(4):
                    split(*group, part)
                split_weights(*second)
                split(*second, 0)

            def unit(it, g, par, u, nxt, following, after):
                if u == 1 and after:
                    split_weights(*after)
                for what, j in steps(u, nxt, following):
                    if what == "project":
                        split(*following, j)

            over_sequences(pool, first, unit)

        @block.vector
        def _(dve):
            dve.sem_inc(turned_taken[0], 1)
            dve.sem_inc(rows_added, 1)
            dve.wait_ge(consts_loaded, 32)

            def largest(turn, par, u, h):
                n = WIDTH[u] * P
                dve.wait_ge(scores_in_psum, ((turn * 2 + par) * UNITS + u) * GR + h + 1)
                dve.sem_inc(dve_passed, 1)
                bank = ps[:, SCORES + h, 0:n]
                dve.tensor_tensor_reduce(bank, bank, causal[:, S - n:S], -float(HD) ** -0.5, -NEG, ALU.add, ALU.min,
                                         shift[:, u % 2, h:h + 1]).then_inc(shift_ready, 1)

            def first(group, second):
                for h in range(GR):
                    largest(*group, 0, h)

            def unit(it, g, par, u, nxt, following, after):
                n = WIDTH[u] * P
                for h in range(0, GR, 2):
                    dve.wait_ge(exp_done, (it * UNITS + u) * GR + GR + h + 2)
                    dve.reciprocal(inverse[:, u % 2, h:h + 2], total[:, u % 2, h:h + 2]).then_inc(dve_step, 1)
                    dve.wait_ge(dve_step, (it * UNITS + u) * 2 + h // 2 + 1)
                    for k in range(h, h + 2):
                        dve.tensor_scalar(probs[:, u % 2, k, 0:n], probs[:, u % 2, k, 0:n], inverse[:, u % 2, k:k + 1],
                                          None, ALU.mult).then_inc(probs_ready, 1)
                for what, j in steps(u, nxt, following):
                    n = FIRST[u] + j
                    if what == "score":
                        largest(*nxt, j)
                    elif what == "turn" and n % 2 == 0:
                        dve.wait_ge(turned_in_psum, it * TURNS + n + 1)
                        dve.tensor_copy(probsT[:, (n + 2 * par) % 4, :], ps[:, TURN, :]).then_inc(turned_taken[0], 1)
                    elif what == "rows":
                        dve.wait_ge(rows_in_psum, it * UNITS + j + 1)
                        rows = keep["z"][:, bass.ds((it // NKV) * TS + WIDTH[j] - 1, 1), :].rearrange("p t d -> p (t d)")
                        dve.tensor_tensor(rows, rows, ps[:, PROJ, 0:D], ALU.add).then_inc(rows_added, 1)

            over_sequences(dve, first, unit)


def route(nc, dram, keep):
    ROUND = 4
    with ExitStack() as ctx:
        def sb(name, shape, dt=F32):
            return ctx.enter_context(nc.sbuf_tensor(name, shape, dt))

        def sem(name):
            return ctx.enter_context(nc.semaphore(name))

        ln2 = sb("ln2", [P, D])
        gate = sb("gate", [P, DC, E])
        before = sb("before", [P, P])
        ones = sb("ones", [P, P])
        expert_ids = sb("expert_ids", [P, E])
        block_ids = sb("block_ids", [P, NBLK])
        square = sb("square3", [P, TT, D])
        meansq = sb("meansq", [P, TT])
        root = sb("root3", [P, TT])
        scale = sb("scale3", [P, TT])
        t_rows = sb("t_rows", [P, TT, D])
        tT = sb("tT", [P, 2, DC, ROUND * P])
        logits = sb("logits", [P, TT, E])
        largest = sb("largest", [P, TT])
        odds = sb("odds", [P, TT, E])
        odds_sum = sb("odds_sum", [P, TT])
        prob = sb("prob", [P, TT, E])
        best = sb("best", [P, TT, 8])
        best_at = sb("best_at", [P, TT, 8], U32)
        best_id = sb("best_id", [P, TT, TOPK])
        pair_sum = sb("pair_sum", [P, TT])
        chosen = [sb(f"chosen{k}", [P, TT, E]) for k in range(TOPK)]
        member = sb("member", [P, TT, E])
        counts = sb("count", [P, 2, TT + 1, E])
        nblocks_i = sb("nblocks_i", [P, E], I32)
        nblocks = sb("nblocks", [P, E])
        blocks_end = sb("blocks_end", [P, E])
        first_slot = sb("first_slot", [P, E])
        slot = sb("slot", [P, TT, E])
        picked = [sb(f"picked{k}", [P, TT, E]) for k in range(TOPK)]
        slot_k = sb("slot_k", [P, TOPK, TT])
        past = sb("past", [P, NBLK, E])
        owner = sb("owner", [P, NBLK])
        ps = ctx.enter_context(nc.psum_tensor("ps3", [P, 8, 512], F32))
        LOGITS, BEFORE, TOTAL = 4, 5, 6

        loaded = sem("loaded3")
        ones_set = sem("ones_set")
        square_sum = sem("square_sum")
        root_ready = sem("root_ready3")
        t_ready = sem("t_ready")
        turned = sem("turned3")
        turned_taken = sem("turned_taken3")
        logits_in_psum = sem("logits_in_psum")
        shifted = sem("shifted")
        odds_ready = sem("odds_ready")
        member_ready = sem("member_ready")
        counted = sem("counted")
        slots_ready = sem("slots_ready")
        scattered = sem("scattered")
        owners_ready = sem("owners_ready")
        dve_step = sem("dve_step3")

        block = ctx.enter_context(nc.Block())
        loads = [(ln2[:], dram["ln2"].to_broadcast([P, D])), (gate[:], dram["gate_w"].rearrange("(c p) e -> p c e", p=P)),
                 (before[:], dram["before"]), (expert_ids[:], dram["expert_ids"]), (block_ids[:], dram["block_ids"])]

        @block.sync
        def _(sp):
            for dst, src in loads:
                sp.dma_start(dst, src).then_inc(loaded, 16)
            sp.wait_ge(owners_ready, 1)
            e = sp.value_load(keep["block_expert"][0:1, 0:1], min_val=0, max_val=E - 1)
            for x in keep["raw"]:
                weights = dram[x].rearrange("e (c p) n -> e p c n", p=P)
                sp.dma_start(keep["raw"][x][:], weights[bass.ds(e, 1)].rearrange("o p c n -> (o p) c n")).then_inc(keep["raw_loaded"][x], 16)

        @block.scalar
        def _(act):
            def root_mean_square(r):
                for t in range(r * ROUND, (r + 1) * ROUND):
                    last = act.activation(square[:, t, :], keep["z"][:, t, :], ACT.Square, accum_out=meansq[:, t:t + 1])
                last.then_inc(square_sum, 1)
                act.wait_ge(square_sum, r + 1)
                at = slice(r * ROUND, (r + 1) * ROUND)
                act.activation(root[:, at], meansq[:, at], ACT.Sqrt, bias=keep["eps"][:, 0:1], scale=1.0 / D).then_inc(root_ready, 1)

            root_mean_square(0)
            root_mean_square(1)
            for r in range(TT // ROUND):
                act.wait_ge(turned, r + 1)
                if r >= 2:
                    act.wait_ge(logits_in_psum, r - 1)
                for c in range(DC):
                    last = act.copy(tT[:, r % 2, c, :], ps[:, r % 2 * DC + c, :])
                last.then_inc(turned_taken, 1)
                if r + 2 < TT // ROUND:
                    root_mean_square(r + 2)
            act.wait_ge(shifted, 1)
            act.activation(odds[:], odds[:], ACT.Exp).then_inc(odds_ready, 1)

        @block.tensor
        def _(pe):
            pe.wait_ge(loaded, 16 * len(loads))

            def turn(r):
                pe.wait_ge(t_ready, (r + 1) * ROUND)
                if r >= 2:
                    pe.wait_ge(turned_taken, r - 1)
                for c in range(DC):
                    for t in range(ROUND):
                        last = pe.transpose(ps[:, r % 2 * DC + c, t * P:(t + 1) * P], t_rows[:, r * ROUND + t, c * P:(c + 1) * P],
                                            keep["ident"][:])
                last.then_inc(turned, 1)

            turn(0)
            for r in range(TT // ROUND):
                if r + 1 < TT // ROUND:
                    turn(r + 1)
                pe.wait_ge(turned_taken, r + 1)
                for t in range(ROUND):
                    at = (r * ROUND + t) * E
                    for c in range(DC):
                        last = pe.matmul(ps[:, LOGITS, at:at + E], tT[:, r % 2, c, t * P:(t + 1) * P], gate[:, c, :],
                                         start=(c == 0), stop=(c == DC - 1))
                last.then_inc(logits_in_psum, 1)
            pe.wait_ge(ones_set, 1)
            pe.wait_ge(member_ready, 1)
            flat = member[:].rearrange("p t e -> p (t e)")
            pe.matmul(ps[:, BEFORE, 0:TT * E], before[:], flat, start=True, stop=True)
            pe.matmul(ps[:, TOTAL, 0:TT * E], ones[:], flat, start=True, stop=True).then_inc(counted, 1)

        @block.gpsimd
        def _(pool):
            pool.memset(ones[:], 1.0).then_inc(ones_set, 1)
            pool.wait_ge(slots_ready, 1)
            pool.wait_ge(t_ready, TT)
            for t in range(TT):
                for k in range(TOPK):
                    pool.indirect_dma_start(dram["slot_rows"], bass.IndirectOffsetOnAxis(keep["slots"][:, k, t:t + 1], 0),
                                            t_rows[:, t, :], None).then_inc(scattered, 16)
            pool.wait_ge(scattered, 16 * TT * TOPK)

        @block.vector
        def _(dve):
            done = [0]

            def link(ins):
                done[0] += 1
                ins.then_inc(dve_step, 1)
                dve.wait_ge(dve_step, done[0])

            dve.wait_ge(loaded, 16 * len(loads))
            for r in range(TT // ROUND):
                at = slice(r * ROUND, (r + 1) * ROUND)
                dve.wait_ge(root_ready, r + 1)
                link(dve.reciprocal(scale[:, at], root[:, at]))
                for t in range(r * ROUND, (r + 1) * ROUND):
                    dve.scalar_tensor_tensor(t_rows[:, t, :], keep["z"][:, t, :], scale[:, t:t + 1], ln2[:], ALU.mult, ALU.mult)\
                       .then_inc(t_ready, 1)
            dve.wait_ge(logits_in_psum, TT // ROUND)
            link(dve.tensor_copy(logits[:].rearrange("p t e -> p (t e)"), ps[:, LOGITS, 0:TT * E]))
            link(dve.tensor_reduce(largest[:], logits[:], AX.X, ALU.max))
            dve.tensor_tensor(odds[:], logits[:], largest[:].unsqueeze(2).to_broadcast([P, TT, E]), ALU.subtract)\
               .then_inc(shifted, 1)
            dve.wait_ge(odds_ready, 1)
            link(dve.tensor_reduce(odds_sum[:], odds[:], AX.X, ALU.add))
            link(dve.reciprocal(odds_sum[:], odds_sum[:]))
            link(dve.tensor_tensor(prob[:], odds[:], odds_sum[:].unsqueeze(2).to_broadcast([P, TT, E]), ALU.mult))
            for t in range(TT):
                last = dve.max(best[:, t, :], prob[:, t, :])
            link(last)
            for t in range(TT):
                last = dve.max_index(best_at[:, t, :], best[:, t, :], prob[:, t, :])
            link(last)
            dve.tensor_copy(best_id[:], best_at[:, :, 0:TOPK])
            link(dve.tensor_tensor(pair_sum[:], best[:, :, 0], best[:, :, 1], ALU.add))
            link(dve.reciprocal(pair_sum[:], pair_sum[:]))
            dve.tensor_tensor(keep["shares"][:], best[:, :, 0:TOPK], pair_sum[:].unsqueeze(2).to_broadcast([P, TT, TOPK]), ALU.mult)
            ids = expert_ids[:].unsqueeze(1).to_broadcast([P, TT, E])
            for k in range(TOPK):
                last = dve.tensor_tensor(chosen[k][:], ids, best_id[:, :, k:k + 1].to_broadcast([P, TT, E]), ALU.is_equal)
            link(last)
            dve.tensor_tensor(member[:], chosen[0][:], chosen[1][:], ALU.add).then_inc(member_ready, 1)
            link(dve.memset(counts[:, :, 0, :], 0.0))
            dve.wait_ge(counted, 1)
            link(dve.tensor_copy(counts[:, 0, 1:, :], ps[:, TOTAL, 0:TT * E].rearrange("p (t e) -> p t e", e=E)))
            step, now = 1, 0
            while step < TT:
                dve.tensor_copy(counts[:, 1 - now, 1:1 + step, :], counts[:, now, 1:1 + step, :])
                link(dve.tensor_tensor(counts[:, 1 - now, 1 + step:, :], counts[:, now, 1 + step:, :], counts[:, now, 1:TT + 1 - step, :],
                                       ALU.add))
                step, now = step * 2, 1 - now
            count = counts[:, now]
            link(dve.tensor_scalar(nblocks_i[:], count[:, TT, :], float(BLK - 1), None, ALU.add))
            link(dve.tensor_scalar(nblocks_i[:], nblocks_i[:], BLK.bit_length() - 1, None, ALU.arith_shift_right))
            link(dve.tensor_copy(nblocks[:], nblocks_i[:]))
            link(dve.tensor_copy(blocks_end[:, 0:1], nblocks[:, 0:1]))
            for e in range(1, E):
                link(dve.tensor_tensor(blocks_end[:, e:e + 1], blocks_end[:, e - 1:e], nblocks[:, e:e + 1], ALU.add))
            link(dve.tensor_tensor(first_slot[:], blocks_end[:], nblocks[:], ALU.subtract))
            link(dve.tensor_scalar(first_slot[:], first_slot[:], float(BLK), None, ALU.mult))
            link(dve.tensor_tensor(slot[:], count[:, 0:TT, :], first_slot[:].unsqueeze(1).to_broadcast([P, TT, E]), ALU.add))
            link(dve.tensor_tensor(slot[:], slot[:], ps[:, BEFORE, 0:TT * E].rearrange("p (t e) -> p t e", e=E), ALU.add))
            for k in range(TOPK):
                last = dve.tensor_tensor(picked[k][:], chosen[k][:], slot[:], ALU.mult)
            link(last)
            for k in range(TOPK):
                last = dve.tensor_reduce(slot_k[:, k, :], picked[k][:], AX.X, ALU.add)
            link(last)
            dve.tensor_copy(keep["slots"][:], slot_k[:]).then_inc(slots_ready, 1)
            link(dve.tensor_tensor(past[:], blocks_end[:].unsqueeze(1).to_broadcast([P, NBLK, E]),
                                   block_ids[:].unsqueeze(2).to_broadcast([P, NBLK, E]), ALU.is_le))
            link(dve.tensor_reduce(owner[:], past[:], AX.X, ALU.add))
            dve.tensor_scalar(keep["block_expert"][:], owner[:], float(E - 1), None, ALU.min).then_inc(owners_ready, 1)


def experts(nc, dram, keep):
    Q = FC // 2
    with ExitStack() as ctx:
        def sb(name, shape, dt=F32):
            return ctx.enter_context(nc.sbuf_tensor(name, shape, dt))

        def sem(name):
            return ctx.enter_context(nc.semaphore(name))

        W = EXPERT_WEIGHTS
        raw = keep["raw"]
        parts = {x: [sb(f"{x}_{n}", [P, 2, *W[x]], F32R) for n in ("high", "low")] for x in W}
        rows = sb("rows", [P, 2, BH, D])
        rowsT = [sb(f"rowsT_{n}", [P, 2, DC * BLK], F32R) for n in ("high", "low")]
        relu = sb("relu", [P, 2, 2, BLK])
        product = sb("product", [P, 2, 2, BLK])
        gatedT = [sb(f"gatedT_{n}", [P, FC, BLK], F32R) for n in ("high", "low")]
        result = sb("result", [P, 2, BH, D])
        ps = ctx.enter_context(nc.psum_tensor("ps4", [P, 8, 512], F32))
        TURN, DOWN, UP = 0, 2, 4

        raw_loaded = keep["raw_loaded"]
        high_ready = {x: sem(f"{x}_high_ready") for x in W}
        split = {x: sem(f"{x}_split") for x in W}
        rows_loaded = [sem("rows_loaded0"), sem("rows_loaded1")]
        turned = sem("turned4")
        rowsT_high = sem("rowsT_high_ready")
        rowsT_split = sem("rowsT_split")
        up_in_psum = sem("up_in_psum")
        relu_ready = sem("relu_ready")
        product_ready = sem("product_ready")
        gated_high = sem("gated_high_ready")
        gated_split = sem("gated_split")
        down_in_psum = sem("down_in_psum")
        result_ready = sem("result_ready")
        stored = [sem("stored0"), sem("stored1")]

        passed = sem("passed4")

        block = ctx.enter_context(nc.Block())
        slot_rows = dram["slot_rows"].rearrange("(n h p) d -> n p h d", h=BH, p=P)
        expert_rows = dram["expert_rows"].rearrange("(n h p) d -> n p h d", h=BH, p=P)

        def one(ap):
            return ap.rearrange("o p c n -> (o p) c n")

        def over_blocks(eng, step):
            assert NBLK % 2 and NBLK >= 5
            step(0, 0, 0)
            with eng.Fori(0, (NBLK - 3) // 2) as pair:
                step(pair * 2 + 1, pair, 1)
                step(pair * 2 + 2, pair + 1, 0)
            step(NBLK - 2, NBLK // 2 - 1, 1)
            step(NBLK - 1, NBLK // 2, 0)

        def is_first(j):
            return isinstance(j, int) and j == 0

        def is_last(j):
            return isinstance(j, int) and j == NBLK - 1

        @block.sync
        def _(sp):
            def step(j, n, par):
                sp.wait_ge(turned, j + 1)
                sp.dma_start(rows[:, par], one(slot_rows[bass.ds(j, 1)])).then_inc(rows_loaded[par], 16)
                if is_first(j):
                    return
                block_expert = keep["block_expert"][0:1, j:j + 1] if isinstance(j, int) else keep["block_expert"][0:1, bass.ds(j, 1)]
                e = sp.value_load(block_expert, min_val=0, max_val=E - 1)
                for x in W:
                    sp.wait_ge(split[x], j + 1)
                    weights = dram[x].rearrange("e (c p) n -> e p c n", p=P)
                    sp.dma_start(raw[x][:], one(weights[bass.ds(e, 1)])).then_inc(raw_loaded[x], 16)

            over_blocks(sp, step)

        @block.tensor
        def _(pe):
            pe.sem_inc(down_in_psum, 2)
            pe.sem_inc(turned, 2)
            pe.sem_inc(up_in_psum, 2 * Q)

            def turn(j, n, par):
                pe.wait_ge(rows_loaded[par], n * 16 + 16)
                for c in range(DC):
                    for h in range(BH):
                        last = pe.transpose(ps[:, TURN + par, c * BLK + h * P:c * BLK + (h + 1) * P], rows[:, par, h, c * P:(c + 1) * P],
                                            keep["ident"][:])
                last.then_inc(turned, 1)

            def step(j, n, par):
                pe.wait_ge(rowsT_split, j + 1)
                for q in range(Q):
                    pe.wait_ge(product_ready, j * Q + q + 1)
                    for m in (2 * q, 2 * q + 1):
                        for x, at in (("w1", 0), ("w3", BLK)):
                            if m == 0:
                                pe.wait_ge(split[x], j + 2)
                            for c in range(DC):
                                for a, b in PASSES:
                                    last = pe.matmul(ps[:, UP + m % 4, at:at + BLK], parts[x][a][:, par, c, m * P:(m + 1) * P],
                                                     rowsT[b][:, par, c * BLK:(c + 1) * BLK],
                                                     start=((c, a, b) == (0, 0, 0)), stop=((c, a, b) == (DC - 1, *PASSES[-1])))
                    last.then_inc(up_in_psum, 1)
                if not is_last(j):
                    turn(j + 1, n + par, 1 - par)
                pe.wait_ge(split["w2"], j + 2)
                pe.wait_ge(result_ready, j + 1)
                for h in range(BH):
                    for m in range(FC):
                        if h == 0 and m % 2 == 0:
                            pe.wait_ge(gated_split, j * Q + m // 2 + 3)
                        for a, b in PASSES:
                            last = pe.matmul(ps[:, DOWN + par, h * D:(h + 1) * D], gatedT[a][:, m, h * P:(h + 1) * P],
                                             parts["w2"][b][:, par, m, :],
                                             start=((m, a, b) == (0, 0, 0)), stop=((m, a, b) == (FC - 1, *PASSES[-1])))
                last.then_inc(down_in_psum, 1)

            turn(0, 0, 0)
            over_blocks(pe, step)

        @block.scalar
        def _(act):
            act.sem_inc(result_ready, 2)
            act.sem_inc(stored[0], 16)
            act.sem_inc(stored[1], 16)

            def high_weights(x, j, par):
                act.wait_ge(raw_loaded[x], j * 16 + 16)
                act.wait_ge(up_in_psum, (j + 1) * Q)
                act.copy(parts[x][0][:, par], raw[x][:]).then_inc(high_ready[x], 1)

            def high_rows(j, par):
                act.wait_ge(turned, j + 3)
                act.copy(rowsT[0][:, par], ps[:, TURN + par, :]).then_inc(rowsT_high, 1)

            def high_gated(j, q):
                act.wait_ge(product_ready, j * Q + q + 3)
                act.copy(gatedT[0][:, 2 * q:2 * q + 2, :], product[:, q % 2]).then_inc(gated_high, 1)

            def take_result(j, n, par):
                act.wait_ge(down_in_psum, j + 3)
                act.wait_ge(stored[par], n * 16 + 16)
                act.copy(result[:, par].rearrange("p h d -> p (h d)"), ps[:, DOWN + par, :]).then_inc(result_ready, 1)
                act.wait_ge(result_ready, j + 3)
                act.dma_start(one(expert_rows[bass.ds(j, 1)]), result[:, par]).then_inc(stored[par], 16)

            def step(j, n, par):
                if not is_first(j):
                    take_result(j - 1, n + par - 1, 1 - par)
                for q in range(Q):
                    act.wait_ge(up_in_psum, j * Q + q + 1 + 2 * Q)
                    act.activation(relu[:, q % 2], ps[:, UP + q % 2 * 2:UP + q % 2 * 2 + 2, 0:BLK], ACT.Relu).then_inc(relu_ready, 1)
                    if q:
                        high_gated(j, q - 1)
                    if q == 0 and not is_last(j):
                        high_weights("w1", j + 1, 1 - par)
                high_gated(j, Q - 1)
                if not is_last(j):
                    high_rows(j + 1, 1 - par)
                    high_weights("w3", j + 1, 1 - par)

            high_rows(0, 0)
            high_weights("w1", 0, 0)
            high_weights("w3", 0, 0)
            over_blocks(act, step)
            take_result(NBLK - 1, NBLK // 2, 0)
            act.wait_ge(stored[0], 16 * (NBLK // 2 + 1) + 16)
            act.wait_ge(stored[1], 16 * (NBLK // 2) + 16)

        @block.vector
        def _(dve):
            dve.sem_inc(product_ready, 2)
            dve.sem_inc(gated_split, 2)
            dve.sem_inc(split["w1"], 1)
            dve.sem_inc(split["w3"], 1)

            def low_weights(x, j, par):
                dve.wait_ge(high_ready[x], j + 1)
                dve.tensor_tensor(parts[x][1][:, par], raw[x][:], parts[x][0][:, par].bitcast(F32), ALU.subtract)\
                   .then_inc(split[x], 1)

            def low_rows(j, par):
                dve.wait_ge(rowsT_high, j + 1)
                dve.tensor_tensor(rowsT[1][:, par], ps[:, TURN + par, :], rowsT[0][:, par].bitcast(F32), ALU.subtract)\
                   .then_inc(rowsT_split, 1)

            def low_gated(j, q):
                dve.wait_ge(gated_high, j * Q + q + 1)
                at = slice(2 * q, 2 * q + 2)
                dve.tensor_tensor(gatedT[1][:, at, :], product[:, q % 2], gatedT[0][:, at, :].bitcast(F32), ALU.subtract)\
                   .then_inc(gated_split, 1)

            def step(j, n, par):
                for q in range(Q):
                    dve.wait_ge(gated_split, j * Q + q + 1)
                    dve.wait_ge(relu_ready, j * Q + q + 1)
                    dve.tensor_tensor(product[:, q % 2], relu[:, q % 2], ps[:, UP + q % 2 * 2:UP + q % 2 * 2 + 2, BLK:2 * BLK], ALU.mult)\
                       .then_inc(product_ready, 1)
                    if q:
                        low_gated(j, q - 1)
                    if q == 1 and not is_last(j):
                        low_weights("w1", j + 1, 1 - par)
                low_gated(j, Q - 1)
                if not is_last(j):
                    low_rows(j + 1, 1 - par)
                    low_weights("w3", j + 1, 1 - par)

            low_rows(0, 0)
            low_weights("w1", 0, 0)
            low_weights("w3", 0, 0)
            over_blocks(dve, step)

        @block.gpsimd
        def _(pool):
            pool.sem_inc(split["w2"], 1)

            def step(j, n, par):
                pool.wait_ge(raw_loaded["w2"], j * 16 + 16)
                pool.wait_ge(down_in_psum, j + 1)
                pool.sem_inc(passed, 1)
                pool.tensor_copy(parts["w2"][0][:, par], raw["w2"][:]).then_inc(high_ready["w2"], 1)
                pool.wait_ge(high_ready["w2"], j + 1)
                pool.tensor_tensor(parts["w2"][1][:, par], raw["w2"][:], parts["w2"][0][:, par].bitcast(F32), ALU.subtract)\
                    .then_inc(split["w2"], 1)

            over_blocks(pool, step)


def combine(nc, dram, keep):
    with ExitStack() as ctx:
        def sb(name, shape, dt=F32):
            return ctx.enter_context(nc.sbuf_tensor(name, shape, dt))

        def sem(name):
            return ctx.enter_context(nc.semaphore(name))

        y = sb("y5", [P, TT, TOPK, D])
        stats = sb("stats5", [P, TT, 6])
        mean = sb("mean5", [P, TT])
        apart = sb("apart5", [P, TT])
        spread = sb("spread5", [P, TT])
        root = sb("root5", [P, TT])
        rstd = sb("rstd5", [P, TT])
        final = sb("final5", [P, TT, D])

        gathered = [sem(f"gathered{b}") for b in range(B)]
        var_ready = sem("var_ready5")
        root_ready = sem("root_ready5")
        out_ready = sem("out_ready5")
        stored = sem("stored5")
        dve_step = sem("dve_step5")

        block = ctx.enter_context(nc.Block())

        @block.gpsimd
        def _(pool):
            for t in range(TT):
                for k in range(TOPK):
                    pool.indirect_dma_start(y[:, t, k, :], None, dram["expert_rows"],
                                            bass.IndirectOffsetOnAxis(keep["slots"][:, k, t:t + 1], 0)).then_inc(gathered[t // TS], 16)

        @block.scalar
        def _(act):
            for b in range(B):
                at = slice(b * TS, (b + 1) * TS)
                act.wait_ge(var_ready, b + 1)
                act.activation(root[:, at], spread[:, at], ACT.Sqrt, bias=keep["eps"][:, 0:1], scale=1.0 / D).then_inc(root_ready, 1)

        @block.sync
        def _(sp):
            for b in range(B):
                sp.wait_ge(out_ready, b + 1)
                sp.dma_start(dram["out"][b].rearrange("(t p) d -> p t d", p=P), final[:, b * TS:(b + 1) * TS, :]).then_inc(stored, 16)
            sp.wait_ge(stored, 16 * B)

        @block.vector
        def _(dve):
            done = [0]

            def link(ins):
                done[0] += 1
                ins.then_inc(dve_step, 1)
                dve.wait_ge(dve_step, done[0])

            for b in range(B):
                tiles = range(b * TS, (b + 1) * TS)
                at = slice(b * TS, (b + 1) * TS)
                dve.wait_ge(gathered[b], 16 * TOPK * TS)
                for k in range(TOPK):
                    for t in tiles:
                        last = dve.scalar_tensor_tensor(keep["z"][:, t, :], y[:, t, k, :], keep["shares"][:, t, k:k + 1], keep["z"][:, t, :],
                                                        ALU.mult, ALU.add)
                    link(last)
                for t in tiles:
                    last = dve.bn_stats(stats[:, t, :], keep["z"][:, t, :])
                link(last)
                dve.tensor_tensor(mean[:, at], stats[:, at, 1], stats[:, at, 4], ALU.add)
                dve.tensor_tensor(apart[:, at], stats[:, at, 1], stats[:, at, 4], ALU.subtract)
                link(dve.tensor_tensor(spread[:, at], stats[:, at, 2], stats[:, at, 5], ALU.add))
                dve.tensor_scalar(mean[:, at], mean[:, at], 0.5, None, ALU.mult)
                link(dve.tensor_tensor(apart[:, at], apart[:, at], apart[:, at], ALU.mult))
                dve.scalar_tensor_tensor(spread[:, at], apart[:, at], D / 4.0, spread[:, at], ALU.mult, ALU.add).then_inc(var_ready, 1)
                dve.wait_ge(root_ready, b + 1)
                link(dve.reciprocal(rstd[:, at], root[:, at]))
                for t in tiles:
                    last = dve.tensor_scalar(final[:, t, :], keep["z"][:, t, :], mean[:, t:t + 1], rstd[:, t:t + 1], ALU.subtract, ALU.mult)
                link(last)
                dve.tensor_tensor(final[:, at, :], final[:, at, :], keep["x1"][:, at, :], ALU.add).then_inc(out_ready, 1)


def program(nc, dram):
    with ExitStack() as ctx:
        def sb(name, shape, dt=F32):
            return ctx.enter_context(nc.sbuf_tensor(name, shape, dt))

        keep = dict(
            ident=sb("ident", [P, P]),
            eps=sb("eps", [P, 1]),
            x1=sb("x1", [P, TT, D]),
            z=sb("z", [P, TT, D]),
            slots=sb("slots", [P, TOPK, TT], U32),
            shares=sb("shares", [P, TT, TOPK]),
            block_expert=sb("block_expert", [P, NBLK], I32),
        )
        with nc.sbuf_tensor("hT_high", [P, DC, T], F32R) as high, nc.sbuf_tensor("hT_low", [P, DC, T], F32R) as low:
            keep["hT"] = high, low
            layer_one(nc, dram, keep)
            attention(nc, dram, keep)
        with ExitStack() as late:
            keep["raw"] = {x: late.enter_context(nc.sbuf_tensor(f"{x}_raw", [P, *EXPERT_WEIGHTS[x]], F32)) for x in EXPERT_WEIGHTS}
            keep["raw_loaded"] = {x: late.enter_context(nc.semaphore(f"{x}_raw_loaded")) for x in EXPERT_WEIGHTS}
            route(nc, dram, keep)
            experts(nc, dram, keep)
        combine(nc, dram, keep)


def kernel(**inputs):
    import concourse.bacc as bacc
    from concourse.bass_utils import run_bass_kernel_spmd

    X, W_in, W_out = (np.asarray(inputs[f"L0_attn_{n}"]) for n in ("X", "W_in", "W_out"))
    b_in, b_out = np.asarray(inputs["L0_attn_b_in"]), np.asarray(inputs["L0_attn_b_out"])
    ffn = {n: np.asarray(inputs[f"L0_ffn_{n}"]) for n in ("ln1_w", "wq", "wk", "wv", "wo", "ln2_w", "gate_w", "w1", "w2", "w3")}

    inv_freq = (1.0 / np.float32(10000.0) ** (np.arange(0, ROT, 2, dtype=np.float32) / np.float32(ROT))).astype(np.float32)
    angle = np.repeat(np.arange(S, dtype=np.float32)[:, None] * inv_freq[None, :], 2, axis=-1)
    cos = np.cos(angle).astype(np.float32)
    sin = (np.sin(angle) * np.where(np.arange(ROT) % 2 == 0, -1.0, 1.0)).astype(np.float32)
    swap = np.arange(ROT).reshape(-1, 2)[:, ::-1].ravel()
    causal = np.zeros((P, S), np.float32)
    causal[:, S - P:] = np.where(np.arange(P)[:, None] >= np.arange(P)[None, :], 0.0, NEG)

    arrays = {
        "x": X,
        "winT": W_in.T,
        "wswT": W_in[swap].T,
        "woutT": W_out.T,
        "b_in": b_in[None, :],
        "b_out": b_out[None, :],
        "qbias": np.stack([b_in[:P], b_in[P:2 * P], b_in[swap]], axis=1),
        "ln1": ffn["ln1_w"].reshape(DC, P).T,
        "ln2": ffn["ln2_w"][None, :],
        "wq": ffn["wq"].reshape(D, NKV, QG).transpose(1, 0, 2),
        "wkv": np.concatenate([ffn["wk"].reshape(D, NKV, HD), ffn["wv"].reshape(D, NKV, HD)], axis=2).transpose(1, 0, 2),
        "wo": ffn["wo"],
        "gate_w": ffn["gate_w"],
        "w1": ffn["w1"],
        "w2": ffn["w2"],
        "w3": ffn["w3"],
        "cos_tok": cos,
        "sin_tok": sin,
        "cos_ch": cos.T,
        "sin_ch": sin.T,
        "ident": np.eye(P, dtype=np.float32),
        "causal": causal,
        "before": np.triu(np.ones((P, P), np.float32), 1),
        "expert_ids": np.tile(np.arange(E, dtype=np.float32), (P, 1)),
        "block_ids": np.tile(np.arange(NBLK, dtype=np.float32), (P, 1)),
    }
    nc = bacc.Bacc("TRN2", target_bir_lowering=False, num_devices=1)
    given, dram = {}, {}
    for name, array in arrays.items():
        array = np.ascontiguousarray(array)
        given[f"in_{name}"] = array
        dram[name] = nc.dram_tensor(f"in_{name}", array.shape, mybir.dt.from_np(array.dtype), kind="ExternalInput").ap()
    dram["slot_rows"] = nc.dram_tensor("slot_rows", (SLOTS, D), F32, kind="Internal").ap()
    dram["expert_rows"] = nc.dram_tensor("expert_rows", (SLOTS, D), F32, kind="Internal").ap()
    dram["out"] = nc.dram_tensor("out_rows", (B, S, D), F32, kind="ExternalOutput").ap()
    program(nc, dram)
    result = run_bass_kernel_spmd(nc, [given], core_ids=[0])
    return result.results[0]["out_rows"]
```
